# Optimizing a Trainium2 kernel written in Bass

```python
import numpy as np
import jax
import jax.numpy as jnp

def _softmax(x, axis=-1):
    return jax.nn.softmax(x, axis=axis)

def _gelu(x):
    return jax.nn.gelu(x, approximate=True)

def _silu(x):
    return jax.nn.silu(x)

def _sigmoid(x):
    return jax.nn.sigmoid(x)

def _layernorm(x, axis=-1, eps=1e-05):
    m = jnp.mean(x, axis=axis, keepdims=True)
    v = jnp.var(x, axis=axis, keepdims=True)
    return (x - m) / jnp.sqrt(v + eps)

def _scatter_add(tgt, idx, src, axis=0):
    return tgt.at[idx].add(src)

def _segment_sum(src, seg, n):
    return jax.ops.segment_sum(src, seg, n)
kernel_name = 'mk_flamingo_gated_d2_seqx_r4_b06db5'

def setup_inputs(seed: int=0):
    np.random.seed(seed)
    _w = jnp.asarray

    def _rec_inputs():
        import jax
        import jax.numpy as jnp
        _rk = jax.random.key(seed)
        x = 7.22e-05 + 1 * jax.random.normal(jax.random.fold_in(_rk, 1), (16, 128, 256), jnp.float32)
        _lenS = 128 - jax.random.randint(jax.random.fold_in(_rk, 7), (16,), 0, max(1, 128 // 4) + 1, jnp.int32)
        _lenS2 = 128 - jax.random.randint(jax.random.fold_in(_rk, 8), (16,), 0, max(1, 128 // 4) + 1, jnp.int32)
        _ctx_1024P = jax.random.normal(jax.random.fold_in(_rk, 11), (16, 16, 256), jnp.float32)
        _ctx_1024c = jax.random.dirichlet(jax.random.fold_in(_rk, 511), 0.3 * jnp.ones((16,), jnp.float32), (16, 128))
        _ctx_1024t = jnp.einsum('bsk,bkd->bsd', _ctx_1024c, _ctx_1024P)
        _ctx_1024t = _ctx_1024t * jax.lax.rsqrt(jnp.mean(jnp.square(_ctx_1024t)) + 1e-12) * 0.953939
        ctx_1024 = 4.13588e-05 + 0.999923 * (_ctx_1024t + 0.3 * jax.random.normal(jax.random.fold_in(_rk, 611), (16, 128, 256), jnp.float32))
        _g = jax.random.normal(jax.random.fold_in(_rk, 9001), (2, 2), jnp.float32)
        _g = jnp.sign(_g) * jnp.maximum(jnp.abs(_g), 1.0) + (_g == 0) * 1.0
        g_xattn = _g[0]
        g_ffn = _g[1]
        return (x, ctx_1024, g_xattn, g_ffn)
    x, ctx_1024, g_xattn, g_ffn = _rec_inputs()

    def _L0_xattn_setup():
        import jax, jax.numpy as jnp
        import numpy as np
        H = 16
        D_K = 64
        D_V = 64
        D_MODEL = 256
        B, N = (4, 512)
        key = jax.random.key(seed)
        ks = jax.random.split(key, 7)
        return {'Q': jax.random.normal(ks[0], (B, N, D_MODEL), dtype=jnp.float32), 'K': jax.random.normal(ks[1], (B, N, D_MODEL), dtype=jnp.float32), 'V': jax.random.normal(ks[2], (B, N, D_MODEL), dtype=jnp.float32), 'W_Q': jax.random.normal(ks[3], (D_MODEL, D_K * H), dtype=jnp.float32) * 0.02, 'W_K': jax.random.normal(ks[4], (D_MODEL, D_K * H), dtype=jnp.float32) * 0.02, 'W_V': jax.random.normal(ks[5], (D_MODEL, D_V * H), dtype=jnp.float32) * 0.02, 'W_O': jax.random.normal(ks[6], (D_V * H, D_MODEL), dtype=jnp.float32) * 0.02}
    _L0_xattn_all = _L0_xattn_setup()
    _L0_xattn_in = {k: v for k, v in _L0_xattn_all.items() if k in ('W_Q', 'W_K', 'W_V', 'W_O')}
    del _L0_xattn_all

    def _L0_ffn_setup():
        import jax, jax.numpy as jnp
        import numpy as np
        TOP_K = 8
        NUM_EXPERTS = 32
        HIDDEN = 256
        EXPERT_DIM = 128
        key = jax.random.key(seed)
        k1, k2, k3, k4 = jax.random.split(key, 4)
        hidden_states = jax.random.normal(k1, (1, 512, HIDDEN), dtype=jnp.float32)
        gate_w = jax.random.normal(k2, (NUM_EXPERTS, HIDDEN), dtype=jnp.float32) * 0.02
        gate_up_w = jax.random.normal(k3, (NUM_EXPERTS, 2 * EXPERT_DIM, HIDDEN), dtype=jnp.float32) * 0.02
        down_w = jax.random.normal(k4, (NUM_EXPERTS, HIDDEN, EXPERT_DIM), dtype=jnp.float32) * 0.02
        return {'hidden_states': hidden_states, 'gate_w': gate_w, 'gate_up_w': gate_up_w, 'down_w': down_w}
    _L0_ffn_all = _L0_ffn_setup()
    _L0_ffn_in = {k: v for k, v in _L0_ffn_all.items() if k in ('gate_w', 'gate_up_w', 'down_w')}
    del _L0_ffn_all

    def _L1_xattn_setup():
        import jax, jax.numpy as jnp
        import numpy as np
        B, S, D_Q, D_K, D_V, D_H, D_O = (8, 512, 256, 256, 256, 256, 256)
        key = jax.random.key(seed)
        ks = jax.random.split(key, 9)
        lim_q = 1.0 / np.sqrt(D_Q)
        lim_k = 1.0 / np.sqrt(D_K)
        lim_v = 1.0 / np.sqrt(D_V)
        return {'input_query': jax.random.normal(ks[0], (B, S, D_Q), jnp.float32), 'input_key': jax.random.normal(ks[1], (B, S, D_K), jnp.float32), 'input_value': jax.random.normal(ks[2], (B, S, D_V), jnp.float32), 'Wq': jax.random.uniform(ks[3], (D_H, D_Q), jnp.float32, -lim_q, lim_q), 'bq': jax.random.uniform(ks[4], (D_H,), jnp.float32, -lim_q, lim_q), 'Wk': jax.random.uniform(ks[5], (D_H, D_K), jnp.float32, -lim_k, lim_k), 'bk': jax.random.uniform(ks[6], (D_H,), jnp.float32, -lim_k, lim_k), 'Wv': jax.random.uniform(ks[7], (D_O, D_V), jnp.float32, -lim_v, lim_v), 'bv': jax.random.uniform(ks[8], (D_O,), jnp.float32, -lim_v, lim_v)}
    _L1_xattn_all = _L1_xattn_setup()
    _L1_xattn_in = {k: v for k, v in _L1_xattn_all.items() if k in ('Wq', 'bq', 'Wk', 'bk', 'Wv', 'bv')}
    del _L1_xattn_all

    def _L1_ffn_setup():
        import jax, jax.numpy as jnp
        import numpy as np
        EPS_LN = 1e-05
        EPS_GATE = 1e-08

        def layer_norm(x, gamma, beta):
            mu = jnp.mean(x, axis=-1, keepdims=True)
            var = jnp.mean(jnp.square(x - mu), axis=-1, keepdims=True)
            return (x - mu) * jax.lax.rsqrt(var + EPS_LN) * gamma + beta
        key = jax.random.key(seed)
        ks = jax.random.split(key, 8)
        B, S, D, E, H = (4, 1024, 256, 4, 512)
        s_in = 1.0 / np.sqrt(D)
        s_h = 1.0 / np.sqrt(H)
        return {'h': jax.random.normal(ks[0], (B, S, D), dtype=jnp.float32), 'router_w': jax.random.uniform(ks[1], (E, D), jnp.float32, -s_in, s_in), 'rn_g': jnp.ones((D,), jnp.float32), 'rn_b': jnp.zeros((D,), jnp.float32), 'w1': jax.random.uniform(ks[2], (E, D, H), jnp.float32, -s_in, s_in), 'ln_g': jnp.ones((E, H), jnp.float32), 'ln_b': jnp.zeros((E, H), jnp.float32), 'w2': jax.random.uniform(ks[3], (E, H, D), jnp.float32, -s_h, s_h), 'on_g': jnp.ones((D,), jnp.float32), 'on_b': jnp.zeros((D,), jnp.float32)}
    _L1_ffn_all = _L1_ffn_setup()
    _L1_ffn_in = {k: v for k, v in _L1_ffn_all.items() if k in ('router_w', 'rn_g', 'rn_b', 'w1', 'ln_g', 'ln_b', 'w2', 'on_g', 'on_b')}
    del _L1_ffn_all
    return {'x': x, 'ctx_1024': ctx_1024, 'g_xattn': g_xattn, 'g_ffn': g_ffn, 'L0_xattn_W_Q': _L0_xattn_in['W_Q'], 'L0_xattn_W_K': _L0_xattn_in['W_K'], 'L0_xattn_W_V': _L0_xattn_in['W_V'], 'L0_xattn_W_O': _L0_xattn_in['W_O'], 'L0_ffn_gate_w': _L0_ffn_in['gate_w'], 'L0_ffn_gate_up_w': _L0_ffn_in['gate_up_w'], 'L0_ffn_down_w': _L0_ffn_in['down_w'], 'L1_xattn_Wq': _L1_xattn_in['Wq'], 'L1_xattn_bq': _L1_xattn_in['bq'], 'L1_xattn_Wk': _L1_xattn_in['Wk'], 'L1_xattn_bk': _L1_xattn_in['bk'], 'L1_xattn_Wv': _L1_xattn_in['Wv'], 'L1_xattn_bv': _L1_xattn_in['bv'], 'L1_ffn_router_w': _L1_ffn_in['router_w'], 'L1_ffn_rn_g': _L1_ffn_in['rn_g'], 'L1_ffn_rn_b': _L1_ffn_in['rn_b'], 'L1_ffn_w1': _L1_ffn_in['w1'], 'L1_ffn_ln_g': _L1_ffn_in['ln_g'], 'L1_ffn_ln_b': _L1_ffn_in['ln_b'], 'L1_ffn_w2': _L1_ffn_in['w2'], 'L1_ffn_on_g': _L1_ffn_in['on_g'], 'L1_ffn_on_b': _L1_ffn_in['on_b']}

def reference(x, ctx_1024, g_xattn, g_ffn, L0_xattn_W_Q, L0_xattn_W_K, L0_xattn_W_V, L0_xattn_W_O, L0_ffn_gate_w, L0_ffn_gate_up_w, L0_ffn_down_w, L1_xattn_Wq, L1_xattn_bq, L1_xattn_Wk, L1_xattn_bk, L1_xattn_Wv, L1_xattn_bv, L1_ffn_router_w, L1_ffn_rn_g, L1_ffn_rn_b, L1_ffn_w1, L1_ffn_ln_g, L1_ffn_ln_b, L1_ffn_w2, L1_ffn_on_g, L1_ffn_on_b):
    import jax
    import jax.numpy as jnp

    def _L0_xattn_ref(Q, K, V, W_Q, W_K, W_V, W_O):
        import jax, jax.numpy as jnp
        import numpy as np
        H = 16
        D_K = 64
        D_V = 64
        D_MODEL = 256
        B, N = (4, 512)
        b, n, _ = Q.shape
        q = (Q @ W_Q).reshape(b, n, H, D_K)
        k = (K @ W_K).reshape(b, n, H, D_K)
        v = (V @ W_V).reshape(b, n, H, D_V)
        scores = jnp.einsum('bqhd,bkhd->bhqk', q, k) / jnp.sqrt(jnp.asarray(D_K, q.dtype))
        attn = jax.nn.softmax(scores, axis=2)
        out = jnp.einsum('bhqk,bkhd->bqhd', attn, v).reshape(b, n, H * D_V)
        return out @ W_O

    def _L0_ffn_ref(hidden_states, gate_w, gate_up_w, down_w):
        import jax, jax.numpy as jnp
        import numpy as np
        TOP_K = 8
        NUM_EXPERTS = 32
        HIDDEN = 256
        EXPERT_DIM = 128
        B, S, H = hidden_states.shape
        x = hidden_states.reshape(-1, H)
        logits = x @ gate_w.T
        probs = jax.nn.softmax(logits.astype(jnp.float32), axis=-1)
        top_w, top_idx = jax.lax.top_k(probs, TOP_K)
        top_w = top_w / jnp.sum(top_w, axis=-1, keepdims=True)
        top_w = top_w.astype(x.dtype)
        comb = jnp.sum(jax.nn.one_hot(top_idx, NUM_EXPERTS, dtype=x.dtype) * top_w[..., None], axis=1)

        def body(acc, ws):
            guw, dw, w_e = ws
            gu = x @ guw.T
            g, u = jnp.split(gu, 2, axis=-1)
            y = u * jax.nn.silu(g) @ dw.T
            return (acc + y * w_e[:, None], None)
        init = jnp.zeros_like(x)
        out, _ = jax.lax.scan(body, init, (gate_up_w, down_w, comb.T))
        return out.reshape(B, S, H)

    def _L1_xattn_ref(input_query, input_key, input_value, Wq, bq, Wk, bk, Wv, bv):
        import jax, jax.numpy as jnp
        import numpy as np
        B, S, D_Q, D_K, D_V, D_H, D_O = (8, 512, 256, 256, 256, 256, 256)
        q = jnp.einsum('bsd,hd->bsh', input_query, Wq) + bq
        k = jnp.einsum('bsd,hd->bsh', input_key, Wk) + bk
        v = jnp.einsum('bsd,od->bso', input_value, Wv) + bv
        scale = 1.0 / jnp.sqrt(jnp.float32(q.shape[-1]))
        scores = jax.nn.softmax(jnp.einsum('bqh,bkh->bqk', q, k) * scale, axis=-1)
        out = jnp.einsum('bqk,bko->bqo', scores, v)
        return out

    def _L1_ffn_ref(h, router_w, rn_g, rn_b, w1, ln_g, ln_b, w2, on_g, on_b):
        import jax, jax.numpy as jnp
        import numpy as np
        EPS_LN = 1e-05
        EPS_GATE = 1e-08

        def layer_norm(x, gamma, beta):
            mu = jnp.mean(x, axis=-1, keepdims=True)
            var = jnp.mean(jnp.square(x - mu), axis=-1, keepdims=True)
            return (x - mu) * jax.lax.rsqrt(var + EPS_LN) * gamma + beta
        D = h.shape[-1]
        h_norm = layer_norm(h, rn_g, rn_b)
        g = jax.nn.softmax(jnp.einsum('bsd,ed->bse', h_norm, router_w), axis=-1)
        top2_w, top2_idx = jax.lax.top_k(g, 2)
        top2_w = top2_w / (jnp.sum(top2_w, axis=-1, keepdims=True) + EPS_GATE)
        hid = jnp.einsum('bsd,edh->bseh', h, w1)
        hid = jax.nn.relu(layer_norm(hid, ln_g, ln_b))
        expert_out = jnp.einsum('bseh,ehd->bsed', hid, w2)
        idx = jnp.broadcast_to(top2_idx[..., None], top2_idx.shape + (D,))
        top2_out = jnp.take_along_axis(expert_out, idx, axis=-2)
        out = jnp.sum(top2_out * top2_w[..., None], axis=-2)
        return layer_norm(out, on_g, on_b)
    x = x + jnp.tanh(g_xattn[0]) * _L0_xattn_ref(_layernorm(x, axis=-1), ctx_1024, ctx_1024, L0_xattn_W_Q, L0_xattn_W_K, L0_xattn_W_V, L0_xattn_W_O)
    x = x + jnp.tanh(g_ffn[0]) * _L0_ffn_ref(_layernorm(x, axis=-1), L0_ffn_gate_w, L0_ffn_gate_up_w, L0_ffn_down_w)
    x = x + jnp.tanh(g_xattn[1]) * _L1_xattn_ref(_layernorm(x, axis=-1), ctx_1024, ctx_1024, L1_xattn_Wq, L1_xattn_bq, L1_xattn_Wk, L1_xattn_bk, L1_xattn_Wv, L1_xattn_bv)
    x = x + jnp.tanh(g_ffn[1]) * _L1_ffn_ref(_layernorm(x, axis=-1), L1_ffn_router_w, L1_ffn_rn_g, L1_ffn_rn_b, L1_ffn_w1, L1_ffn_ln_g, L1_ffn_ln_b, L1_ffn_w2, L1_ffn_on_g, L1_ffn_on_b)
    return x

_drawn_inputs = setup_inputs


def setup_inputs(seed=0):
    import zlib

    import numpy as np

    out = dict(_drawn_inputs(seed))
    spreads = {'g_ffn': (-1.0, 0.2),
     'L1_ffn_rn_g': (1.0, 0.2),
     'L1_ffn_rn_b': (0.0, 0.1),
     'L1_ffn_ln_g': (1.0, 0.2),
     'L1_ffn_ln_b': (0.0, 0.1),
     'L1_ffn_on_g': (1.0, 0.2),
     'L1_ffn_on_b': (0.0, 0.1)}
    factors = {'L0_ffn_gate_w': 2.835,
     'L0_ffn_gate_up_w': 4.129,
     'L0_ffn_down_w': 2.864,
     'L1_xattn_bq': 3.847,
     'L1_xattn_bk': 8.0}
    for name, (base, spread) in spreads.items():
        noise = np.random.default_rng([zlib.crc32(name.encode()), seed]).standard_normal(out[name].shape)
        drawn = base * np.exp(spread * noise) if base else spread * noise
        out[name] = jnp.asarray(drawn.astype(out[name].dtype))
    for name, factor in factors.items():
        out[name] = (out[name] * factor).astype(out[name].dtype)
    return out
```

```python
from contextlib import ExitStack

import concourse.bass as bass
from concourse import mybir

F32 = mybir.dt.float32
F32R = mybir.dt.float32r
ALU = mybir.AluOpType
ACT = mybir.ActivationFunctionType
AX_X = mybir.AxisListType.X

P = 128
D = 256
KC = D // P
TOK = 2048
TILES = TOK // P
GT = 4
GW = GT * P
GROUPS = TILES // GT
HEADS, DH = 16, 64
HD = HEADS * DH
CH = HD // P
EXPERTS, TOPK, XD = 32, 8, 128
EG = 4
EGS = EXPERTS // EG
E1, H1 = 4, 512
HC1 = H1 // P
EPS_LN = 1e-5
EPS_GATE = 1e-8

PASSES = ((0, 0), (0, 1), (1, 0))


def product(pe, out, stationary, moving, chunks, start=True, stop=True, skip=False):
    last = None
    for k in range(chunks):
        for n, (a, b) in enumerate(PASSES):
            last = pe.matmul(out, stationary(a, k), moving(b, k), start=start and k == 0 and n == 0,
                             stop=stop and k == chunks - 1 and n == 2, skip_group_check=skip)
    return last


class Space:

    def __init__(self, nc, stack, prefix):
        self.nc, self.stack, self.prefix = nc, stack, prefix

    def sb(self, name, shape, dt=F32):
        return self.stack.enter_context(self.nc.sbuf_tensor(f"{self.prefix}_{name}", shape, dt))

    def pair(self, name, shape):
        return [self.sb(f"{name}_hi", shape, F32R), self.sb(f"{name}_lo", shape, F32R)]

    def ps(self, name, shape):
        return self.stack.enter_context(self.nc.psum_tensor(f"{self.prefix}_{name}", shape, F32))

    def sems(self, *names):
        return [self.stack.enter_context(self.nc.semaphore(f"{self.prefix}_{n}")) for n in names]


def stage_a(nc, dram, keep):
    x, xnT, ctxT, ident, tg = keep
    with ExitStack() as stack:
        sp_ = Space(nc, stack, "a")
        w = {n: sp_.pair(n, [P, KC, HD]) for n in ("wq", "wk", "wv")}
        w["wo"] = sp_.pair("wo", [P, CH, D])
        with ExitStack() as early:
            er = Space(nc, early, "a_raw")
            ctx_raw = er.sb("ctx", [P, KC, TOK])
            raw = {n: er.sb(n, [P, KC, HD]) for n in ("wq", "wk", "wv")}
            raw["wo"] = er.sb("wo", [P, CH, D])
        v32 = sp_.sb("v32", [P, GT, HD])
        qT = [sp_.pair(f"qT{b}", [P, GW]) for b in range(2)]
        kT = [sp_.pair(f"kT{b}", [P, GW]) for b in range(2)]
        p32 = sp_.sb("p32", [P, GT, 2, P])
        probs = sp_.pair("probs", [P, GT, 2, P])
        vs32 = sp_.sb("vs32", [P, GT, 2, DH])
        vs = sp_.pair("vs", [P, GT, 2, DH])
        oT = sp_.pair("oT", [P, GT, P])
        stage = sp_.sb("stage", [P, GT, 2, KC, P], F32R)
        xn32 = sp_.sb("xn32", [P, GT, D])
        graw = sp_.sb("graw", [P, 4])
        stats = sp_.sb("stats", [P, GT, 6])
        mv = sp_.sb("mv", [P, GT, 2])
        ve = sp_.sb("ve", [P, GT])
        rstd = sp_.sb("rstd", [P, GT])
        neghalf = sp_.sb("neghalf", [P, GT])
        pad = sp_.sb("pad", [P, 4])
        neg = sp_.sb("neg", [P, 2, GT])
        sums = sp_.sb("sums", [P, GT, 2])
        rinv = sp_.sb("rinv", [P, GT, 2])

        ring = [sp_.ps(f"ring{b}", [P, GW]) for b in range(2)]
        psS = sp_.ps("scores", [P, 2, GT, P])
        psV = sp_.ps("values", [P, GT, 2 * P])
        psO = sp_.ps("outs", [P, GT, D])

        g_in, ctx_in, wq_in, wk_in, wv_in, wo_in = sp_.sems("g_in", "ctx_in", "wq_in", "wk_in", "wv_in", "wo_in")
        x_in = sp_.sems(*[f"x_in{g}" for g in range(GROUPS)])
        split_hi, split_lo, split_v, ident_done = sp_.sems("split_hi", "split_lo", "split_v", "ident_done")
        job_done, act_hi, ring_done = sp_.sems("job_done", "act_hi", "ring_done")
        s_done, neg_done, exp_done, rinv_done, vs32_done = sp_.sems("s_done", "neg_done", "exp_done", "rinv_done", "vs32_done")
        vhi_done, vlo_done, phi_done, plo_done, pv_done = sp_.sems("vhi_done", "vlo_done", "phi_done", "plo_done", "pv_done")
        ohi_done, ot_done, o_done, x_upd, staged = sp_.sems("ohi_done", "ot_done", "o_done", "x_upd", "staged")
        st_done, mv_done, ve_done, rstd_done, xn_ready, held = sp_.sems("st_done", "mv_done", "ve_done", "rstd_done", "xn_ready", "held")

        JOBS0, HIS0 = 10, 6
        jobs, his = {}, {}
        nj = nh = 0
        for s in range(CH):
            if s in (2, 4):
                jobs[s, "ln"], his[s, "ln"] = nj, nh
                nj, nh = nj + KC, nh + KC
            jobs[s, "v"] = nj
            jobs[s, "q"], his[s, "q"] = nj + 1, nh
            jobs[s, "k"], his[s, "k"] = nj + 2, nh + 1
            nj, nh = nj + 3, nh + 2
        JOBS, HIS = nj, nh
        assert JOBS % 2 == 0 and JOBS0 % 2 == 0
        SPLITS = ("wq", "ctx", "wk")

        block = stack.enter_context(nc.Block())

        @block.sync
        def _(sp):
            sp.dma_start(x[:, 0:GT, :], dram["x"][:, 0:GT, :]).then_inc(x_in[0], 16)
            sp.dma_start(ctx_raw[:, :, :], dram["ctxT"]).then_inc(ctx_in, 16)
            sp.dma_start(raw["wv"][:, :, :], dram["wv"]).then_inc(wv_in, 16)
            for g in range(1, GROUPS):
                sp.dma_start(x[:, GT * g:GT * g + GT, :], dram["x"][:, GT * g:GT * g + GT, :]).then_inc(x_in[g], 16)

        @block.gpsimd
        def _(pool):
            pool.memset(ident[:, :], 0.0).then_inc(ident_done, 1)
            pool.memset(neghalf[:, :], -0.5).then_inc(ident_done, 1)
            pool.wait_ge(ident_done, 2)
            pool.affine_select(out=ident[:, :], in_=ident[:, :], compare_op=ALU.not_equal, fill=1.0, base=0,
                               pattern=[[-1, P]], channel_multiplier=1).then_inc(ident_done, 1)

            def rsqrt(n):
                pool.wait_ge(ve_done, n + 1)
                pool.tensor_tensor(rstd[:, :], ve[:, :], neghalf[:, :], ALU.pow).then_inc(rstd_done, 1)

            def split_here(name, value):
                pool.tensor_copy(w[name][0][:, :, :], raw[name][:, :, :]).then_inc(split_v, 1)
                pool.wait_ge(split_v, value)
                pool.tensor_tensor(w[name][1][:, :, :], raw[name][:, :, :], w[name][0][:, :, :].bitcast(F32),
                                   ALU.subtract).then_inc(split_v, 1)

            def stage_tile(t, g):
                for part in range(2):
                    pool.tensor_copy(stage[:, t, part, :, :], ctxT[part][:, :, bass.ds(g * GW + t * P, P)].bitcast(F32)
                                     ).then_inc(staged, 1)

            def probs_lo(n):
                pool.wait_ge(phi_done, n + 1)
                pool.tensor_tensor(probs[1][:, :, :, :], p32[:, :, :, :], probs[0][:, :, :, :].bitcast(F32),
                                   ALU.subtract).then_inc(plo_done, 1)

            rsqrt(0)
            pool.wait_ge(wv_in, 16)
            split_here("wv", 1)
            pool.wait_ge(split_lo, 2)
            for t in range(GT):
                stage_tile(t, 0)
            pool.wait_ge(wo_in, 16)
            split_here("wo", 3)
            probs_lo(0)
            with pool.Fori(0, GROUPS) as i:
                for s in range(CH):
                    if s == 1:
                        rsqrt(2 * i + 1)
                    if s == 3:
                        rsqrt(2 * i + 2)
                    if s < GT:
                        pool.wait_ge(job_done, JOBS0 + JOBS * i + jobs[s, "v"] + 1)
                        stage_tile(s, (i + 1) % GROUPS)
                    probs_lo(CH * i + s + 1)
            rsqrt(2 * GROUPS + 1)

        @block.scalar
        def _(act):
            act.dma_start(raw["wq"][:, :, :], dram["wq"]).then_inc(wq_in, 16)
            act.dma_start(raw["wk"][:, :, :], dram["wk"]).then_inc(wk_in, 16)
            act.dma_start(raw["wo"][:, :, :], dram["wo"]).then_inc(wo_in, 16)
            act.dma_start(graw[:, :], dram["g"].partition_broadcast(P)).then_inc(g_in, 16)
            for name, sem in zip(SPLITS, (wq_in, ctx_in, wk_in)):
                act.wait_ge(sem, 16)
                hi, src = (ctxT[0], ctx_raw) if name == "ctx" else (w[name][0], raw[name])
                act.activation(hi[:, :, :], src[:, :, :], ACT.Copy).then_inc(split_hi, 1)
            act.wait_ge(g_in, 16)
            act.activation(tg[:, :], graw[:, :], ACT.Tanh).then_inc(g_in, 1)

            def ln_hi(job, kc, g):
                act.wait_ge(job_done, job + 1)
                act.activation(xnT[0][:, kc, bass.ds(g * GW, GW)], ring[kc][:, :], ACT.Copy).then_inc(act_hi, 1)

            def qk_hi(which, job, bank, buf, n):
                act.wait_ge(job_done, job + 1)
                if n is not None:
                    act.wait_ge(s_done, n)
                dst, scale = (qT, DH ** -0.5) if which == "q" else (kT, 1.0)
                act.activation(dst[buf][0][:, :], ring[bank][:, :], ACT.Copy, scale=scale).then_inc(act_hi, 1)

            def exps(n, part, first):
                if part == 0:
                    act.wait_ge(neg_done, n + 1)
                    if not first:
                        act.wait_ge(plo_done, n)
                        act.wait_ge(phi_done, n)
                for b in range(2 * part, 2 * part + 2):
                    for j in range(2):
                        ins = act.activation(p32[:, b, j, :], psS[:, j, b, :], ACT.Exp, bias=neg[:, j, b:b + 1],
                                             accum_out=sums[:, b, j:j + 1])
                if part == 1:
                    ins.then_inc(exp_done, 1)

            def out_hi(n):
                act.wait_ge(pv_done, n + 1)
                act.wait_ge(o_done, n + 1)
                for j in range(2):
                    lanes = slice(DH * j, DH * j + DH)
                    act.activation(oT[0][lanes, :, :], psV[lanes, :, P * j:P * j + P], ACT.Copy).then_inc(ohi_done, 1)

            for kc in range(KC):
                ln_hi(kc, kc, 0)
            for step in range(2):
                qk_hi("q", 6 + 2 * step, 0, step, None)
                qk_hi("k", 7 + 2 * step, 1, step, None)
            exps(0, 0, True)
            exps(0, 1, True)
            with act.Fori(0, GROUPS) as i:
                for s in range(CH):
                    n = CH * i + s + 1
                    J = JOBS0 + JOBS * i
                    if s in (2, 4):
                        for kc in range(KC):
                            ln_hi(J + jobs[s, "ln"] + kc, kc, (i + (3 if s == 2 else 1)) % GROUPS)
                    out_hi(n - 1)
                    exps(n, 0, False)
                    qk_hi("q", J + jobs[s, "q"], jobs[s, "q"] % 2, s % 2, n)
                    exps(n, 1, False)
                    qk_hi("k", J + jobs[s, "k"], jobs[s, "k"] % 2, s % 2, n)
            for kc in range(KC):
                ln_hi(JOBS0 + JOBS * GROUPS + kc, kc, GROUPS - 1)

        @block.vector
        def _(dve):
            dve.memset(pad[:, 1:2], 0.0).then_inc(x_upd, 1)
            dve.memset(pad[:, 2:3], 0.0).then_inc(ot_done, 1)
            dve.memset(pad[:, 3:4], 0.0).then_inc(o_done, 1)
            dve.memset(pad[:, 0:1], 0.0).then_inc(held, 1)

            def ln_stats(n, g, landed):
                if landed is not None:
                    dve.wait_ge(landed, 16)
                else:
                    dve.wait_ge(x_upd, g[1])
                gx = g[0]
                for t in range(GT):
                    dve.bn_stats(stats[:, t, :], x[:, gx * GT + t, :]).then_inc(st_done, 1)
                dve.wait_ge(held, n + 1)
                dve.wait_ge(st_done, GT * n + GT)
                dve.memset(pad[:, 0:1], 0.0).then_inc(held, 1)
                for t in range(GT):
                    dve.bn_aggr(mv[:, t, :], stats[:, t, :]).then_inc(mv_done, 1)
                dve.wait_ge(mv_done, GT * n + GT)
                dve.tensor_scalar(ve[:, :], mv[:, :, 1], EPS_LN, None, ALU.add).then_inc(ve_done, 1)

            def ln_apply(n, gx):
                dve.wait_ge(rstd_done, n + 1)
                for t in range(GT):
                    dve.tensor_scalar(xn32[:, t, :], x[:, gx * GT + t, :], mv[:, t, 0:1], rstd[:, t:t + 1],
                                      ALU.subtract, ALU.mult).then_inc(xn_ready, 1)

            def ln_lo(hi, kc, g):
                dve.wait_ge(act_hi, hi + 1)
                at = bass.ds(g * GW, GW)
                dve.tensor_tensor(xnT[1][:, kc, at], ring[kc][:, :], xnT[0][:, kc, at].bitcast(F32),
                                  ALU.subtract).then_inc(ring_done, 1)

            def v_out(job, bank, t, half):
                dve.wait_ge(job_done, job + 1)
                dve.tensor_copy(v32[:, t, half * 512:half * 512 + 512], ring[bank][:, :]).then_inc(ring_done, 1)

            def qk_lo(which, hi, bank, buf):
                dve.wait_ge(act_hi, hi + 1)
                if which == "q":
                    dve.scalar_tensor_tensor(qT[buf][1][:, :], ring[bank][:, :], DH ** -0.5,
                                             qT[buf][0][:, :].bitcast(F32), ALU.mult, ALU.subtract).then_inc(ring_done, 1)
                else:
                    dve.tensor_tensor(kT[buf][1][:, :], ring[bank][:, :], kT[buf][0][:, :].bitcast(F32),
                                      ALU.subtract).then_inc(ring_done, 1)

            def minus_max(n):
                dve.wait_ge(s_done, n + 1)
                dve.tensor_reduce(neg[:, :, :], psS[:, :, :, :], AX_X, ALU.max, negate=True).then_inc(neg_done, 1)

            def scale_values(n, c, rows, first):
                dve.wait_ge(exp_done, n + 1)
                dve.reciprocal(rinv[:, :, :], sums[:, :, :]).then_inc(rinv_done, 1)
                dve.wait_ge(rinv_done, n + 1)
                dve.wait_ge(ring_done, rows)
                dve.tensor_tensor(vs32[:, :, :, :], v32[:, :, c * P:c * P + P].rearrange("p t (j d) -> p t j d", j=2),
                                  rinv[:, :, :].unsqueeze(3).broadcast_to([P, GT, 2, DH]), ALU.mult).then_inc(vs32_done, 1)
                dve.wait_ge(vs32_done, n + 1)
                if not first:
                    dve.wait_ge(pv_done, n)
                dve.tensor_copy(vs[0][:, :, :, :], vs32[:, :, :, :]).then_inc(vhi_done, 1)
                dve.tensor_copy(probs[0][:, :, :, :], p32[:, :, :, :]).then_inc(phi_done, 1)
                dve.wait_ge(vhi_done, n + 1)
                dve.tensor_tensor(vs[1][:, :, :, :], vs32[:, :, :, :], vs[0][:, :, :, :].bitcast(F32),
                                  ALU.subtract).then_inc(vlo_done, 1)

            def out_lo(n):
                dve.wait_ge(ohi_done, 2 * n + 2)
                for j in range(2):
                    lanes = slice(DH * j, DH * j + DH)
                    ins = dve.tensor_tensor(oT[1][lanes, :, :], psV[lanes, :, P * j:P * j + P],
                                            oT[0][lanes, :, :].bitcast(F32), ALU.subtract)
                ins.then_inc(ot_done, 1)

            ln_stats(0, (0, None), x_in[0])
            dve.wait_ge(split_hi, 1)
            dve.tensor_tensor(w["wq"][1][:, :, :], raw["wq"][:, :, :], w["wq"][0][:, :, :].bitcast(F32),
                              ALU.subtract).then_inc(split_lo, 1)
            ln_apply(0, 0)
            dve.wait_ge(split_hi, 2)
            dve.tensor_tensor(ctxT[1][:, :, :], ctx_raw[:, :, :], ctxT[0][:, :, :].bitcast(F32),
                              ALU.subtract).then_inc(split_lo, 1)
            dve.wait_ge(split_hi, 3)
            dve.tensor_tensor(w["wk"][1][:, :, :], raw["wk"][:, :, :], w["wk"][0][:, :, :].bitcast(F32),
                              ALU.subtract).then_inc(split_lo, 1)
            dve.wait_ge(split_lo, 3)
            for kc in range(KC):
                ln_lo(kc, kc, 0)
            for t in range(GT):
                v_out(2 + t, t % 2, t, 0)
            for step in range(2):
                qk_lo("q", 2 + 2 * step, 0, step)
                qk_lo("k", 3 + 2 * step, 1, step)
            minus_max(0)
            dve.wait_ge(split_v, 4)
            scale_values(0, 0, 6, True)
            for g in range(1, GROUPS):
                dve.wait_ge(x_in[g], 16)
            dve.wait_ge(g_in, 17)
            with dve.Fori(0, GROUPS) as i:
                for s in range(CH):
                    n = CH * i + s + 1
                    J, H = JOBS0 + JOBS * i, HIS0 + HIS * i
                    minus_max(n)
                    if s in (2, 4):
                        for kc in range(KC):
                            ln_lo(H + his[s, "ln"] + kc, kc, (i + (3 if s == 2 else 1)) % GROUPS)
                    out_lo(n - 1)
                    v_out(J + jobs[s, "v"], jobs[s, "v"] % 2, s % GT, 1 - s // GT)
                    qk_lo("q", H + his[s, "q"], jobs[s, "q"] % 2, s % 2)
                    qk_lo("k", H + his[s, "k"], jobs[s, "k"] % 2, s % 2)
                    if s in (1, 3):
                        gx = (i + (3 if s == 1 else 1)) % GROUPS
                        ln_stats(2 * i + (1 if s == 1 else 2), (gx, i + 1), None)
                    scale_values(n, (s + 1) % CH, J + jobs[s, "v"] + 1, False)
                    if s in (1, 3):
                        ln_apply(2 * i + (1 if s == 1 else 2), gx)
                dve.wait_ge(o_done, CH * i + CH + 1)
                at = bass.ds(i * GT, GT)
                dve.scalar_tensor_tensor(x[:, at, :], psO[:, :, :], tg[:, 0:1], x[:, at, :],
                                         ALU.mult, ALU.add).then_inc(x_upd, 1)
            n = 2 * GROUPS + 1
            ln_stats(n, (GROUPS - 1, GROUPS + 1), None)
            ln_apply(n, GROUPS - 1)
            for kc in range(KC):
                ln_lo(HIS0 + HIS * GROUPS + kc, kc, GROUPS - 1)

        @block.tensor
        def _(pe):
            def ring_free(job, first=False):
                if not first:
                    pe.wait_ge(ring_done, job - 1)

            def ln_jobs(n, job, first=False):
                pe.wait_ge(xn_ready, GT * n + GT)
                for kc in range(KC):
                    ring_free(job + kc, first)
                    for t in range(GT):
                        mm = pe.transpose(ring[kc][:, t * P:t * P + P], xn32[:, t, kc * P:kc * P + P], ident[:, :])
                    mm.then_inc(job_done, 1)

            def v_job(job, bank, t, half):
                ring_free(job)
                product(pe, ring[bank][:, :], lambda a, k: stage[:, t, a, k, :],
                        lambda b, k: w["wv"][b][:, k, half * 512:half * 512 + 512], KC).then_inc(job_done, 1)

            def qk_job(which, job, bank, c, g):
                ring_free(job)
                src = xnT if which == "q" else ctxT
                wt = w["w" + which]
                product(pe, ring[bank][:, :], lambda a, k: wt[a][:, k, c * P:c * P + P],
                        lambda b, k: src[b][:, k, bass.ds(g * GW, GW)], KC).then_inc(job_done, 1)

            def scores(n, rows, buf, first):
                pe.wait_ge(ring_done, rows)
                if not first:
                    pe.wait_ge(exp_done, n)
                for b in range(GT):
                    for m, (ka, qb) in enumerate(PASSES):
                        for j in range(2):
                            lanes = slice(DH * j, DH * j + DH)
                            mm = pe.matmul(psS[:, j, b, :], kT[buf][ka][lanes, b * P:b * P + P],
                                           qT[buf][qb][lanes, b * P:b * P + P], start=m == 0, stop=m == 2)
                mm.then_inc(s_done, 1)

            def values(n):
                pe.wait_ge(vlo_done, n + 1)
                pe.wait_ge(plo_done, n + 1)
                pe.wait_ge(ot_done, n + 1)
                for b in range(GT):
                    for m, (a, q) in enumerate(PASSES):
                        mm = pe.matmul(psV[:, b, :], vs[a][:, b, :, :], probs[q][:, b, :, :], start=m == 0, stop=m == 2)
                mm.then_inc(pv_done, 1)

            def outs(n, c, free):
                pe.wait_ge(ot_done, n + 2)
                if c == 0:
                    pe.wait_ge(x_upd, free)
                for b in range(GT):
                    for m, (a, q) in enumerate(PASSES):
                        mm = pe.matmul(psO[:, b, :], oT[a][:, b, :], w["wo"][q][:, c, :],
                                       start=c == 0 and m == 0 and b % 2 == 0, stop=c == CH - 1 and m == 2,
                                       skip_group_check=True)
                mm.then_inc(o_done, 1)

            pe.wait_ge(ident_done, 3)
            ln_jobs(0, 0, True)
            pe.wait_ge(split_v, 2)
            pe.wait_ge(split_lo, 3)
            pe.wait_ge(staged, 2 * GT)
            for t in range(GT):
                v_job(2 + t, t % 2, t, 0)
            for step in range(2):
                qk_job("q", 6 + 2 * step, 0, step, 0)
                qk_job("k", 7 + 2 * step, 1, step, 0)
            scores(0, 8, 0, True)
            pe.wait_ge(split_v, 4)
            with pe.Fori(0, GROUPS) as i:
                for s in range(CH):
                    n = CH * i + s + 1
                    J = JOBS0 + JOBS * i
                    gq = i if s < CH - 2 else (i + 1) % GROUPS
                    scores(n, J + (jobs[s - 1, "k"] + 1 if s else 0), (s + 1) % 2, False)
                    if s in (2, 4):
                        ln_jobs(2 * i + (1 if s == 2 else 2), J + jobs[s, "ln"])
                    values(n - 1)
                    if s >= GT:
                        pe.wait_ge(staged, 2 * GT * (i + 1) + 2 * (s - GT + 1))
                    v_job(J + jobs[s, "v"], jobs[s, "v"] % 2, s % GT, 1 - s // GT)
                    qk_job("q", J + jobs[s, "q"], jobs[s, "q"] % 2, (s + 2) % CH, gq)
                    qk_job("k", J + jobs[s, "k"], jobs[s, "k"] % 2, (s + 2) % CH, gq)
                    outs(n - 1, s, i + 1)
            ln_jobs(2 * GROUPS + 1, JOBS0 + JOBS * GROUPS)


def stage_b(nc, dram, keep):
    x, xnT, ctxT, ident, tg = keep
    ITEMS = EG * GROUPS
    UP = KC * 2 * XD
    with ExitStack() as stack:
        sp_ = Space(nc, stack, "b")
        wraw = sp_.sb("wraw", [P, EG * (UP + D)])
        wsp = [sp_.pair(f"w{b}", [P, EG * (UP + D)]) for b in range(2)]
        graw = sp_.sb("graw", [P, KC, EXPERTS])
        gate = sp_.pair("gate", [P, KC, EXPERTS])
        neg = sp_.sb("neg", [P, TILES])
        lg = sp_.sb("lg", [P, TILES, EXPERTS])
        ex = sp_.sb("ex", [P, TILES, EXPERTS])
        top = sp_.sb("top", [P, TILES, TOPK])
        rest = sp_.sb("rest", [P, TILES, EXPERTS])
        total = sp_.sb("total", [P, TILES])
        inv = sp_.sb("inv", [P, TILES])
        comb = sp_.sb("comb", [P, TILES, EXPERTS])
        combT = sp_.sb("combT", [P, GROUPS, P])
        share = [sp_.sb(f"share{b}", [P, EG, GW]) for b in range(2)]
        silu = [sp_.sb(f"silu{b}", [P, GW]) for b in range(2)]
        weighted = sp_.sb("weighted", [P, GW])
        h32 = [sp_.sb(f"h32{b}", [P, GW]) for b in range(2)]
        h = [sp_.pair(f"h{b}", [P, GW]) for b in range(2)]
        acc = sp_.sb("acc", [P, KC, TOK])
        pad = sp_.sb("pad", [P, 4])
        psG = [sp_.ps(f"gate{b}", [P, GW]) for b in range(2)]
        psU = [sp_.ps(f"up{b}", [P, GW]) for b in range(2)]
        psY = [sp_.ps(f"down{b}", [P, KC, GW]) for b in range(2)]

        g_in, g_split, lg_done, r_done, ex_done, cT_ps, cT_done, cw_out, padded = sp_.sems(
            "g_in", "g_split", "lg_done", "r_done", "ex_done", "cT_ps", "cT_done", "cw_out", "padded")
        w_in, w_split, share_in0, share_in1 = sp_.sems("w_in", "w_split", "share_in0", "share_in1")
        share_in = [share_in0, share_in1]
        g_done, u_done, d_done, s_done, t_done, h_done, hhi_done, hlo_done, acc_done, yT_done, x_upd = sp_.sems(
            "g_done", "u_done", "d_done", "s_done", "t_done", "h_done", "hhi_done", "hlo_done", "acc_done", "yT_done", "x_upd")

        def up(buf, part, e, k, half):
            at = (e * KC + k) * 2 * XD + half * XD
            return wsp[buf][part][:, at:at + XD]

        def down(buf, part, e, c):
            at = EG * UP + e * D + c * P
            return wsp[buf][part][:, at:at + P]

        block = stack.enter_context(nc.Block())

        @block.sync
        def _(sp):
            def load_weights(eg):
                sp.dma_start(wraw[:, :], dram["moe"][eg, :, :]).then_inc(w_in, 16)

            def load_share(eg, tg_):
                rows = dram["shares"][bass.ds(eg * EG, EG), tg_ * GW:tg_ * GW + GW]
                sp.dma_start(share[tg_ % 2][:, :, :], rows.partition_broadcast(P)).then_inc(share_in[tg_ % 2], 16)

            load_weights(0)
            sp.wait_ge(w_split, 2)
            load_weights(1)
            sp.wait_ge(cT_done, 1)
            for tt in range(GT):
                sp.dma_start(dram["shares"].rearrange("e (g t n) -> t e g n", t=GT, n=P)[tt, :, :, :],
                             combT[tt * EXPERTS:tt * EXPERTS + EXPERTS, :, :]).then_inc(cw_out, 16)
            sp.wait_ge(cw_out, 16 * GT)
            load_share(0, 0)
            load_share(0, 1)
            with sp.Fori(0, EGS) as eg:
                for t in range(GROUPS):
                    sp.wait_ge(t_done, ITEMS * eg + EG * (t + 1))
                    load_share((eg + (t + 2) // GROUPS) % EGS, (t + 2) % GROUPS)
                    if t == 1:
                        sp.wait_ge(w_split, 2 * eg + 4)
                        load_weights((eg + 2) % EGS)
            sp.wait_ge(w_in, 16 * (EGS + 2))
            sp.wait_ge(share_in[0], 16 * (2 * EGS + 1))
            sp.wait_ge(share_in[1], 16 * (2 * EGS + 1))

        @block.gpsimd
        def _(pool):
            pool.memset(pad[:, 1:2], 0.0).then_inc(padded, 1)

            def split(n, buf):
                pool.tensor_copy(wsp[buf][0][:, :], wraw[:, :]).then_inc(w_split, 1)
                pool.wait_ge(w_split, 2 * n + 1)
                pool.tensor_tensor(wsp[buf][1][:, :], wraw[:, :], wsp[buf][0][:, :].bitcast(F32),
                                   ALU.subtract).then_inc(w_split, 1)

            for n in range(2):
                pool.wait_ge(w_in, 16 * (n + 1))
                split(n, n)
            with pool.Fori(0, EGS // 2) as p:
                for q in range(2):
                    n = 2 * p + q + 2
                    pool.wait_ge(d_done, ITEMS * (n - 1) + 1)
                    pool.wait_ge(w_in, 16 * n + 16)
                    pool.wait_ge(padded, n - 1)
                    pool.tensor_tensor(pad[:, 1:2], pad[:, 1:2], pad[:, 1:2], ALU.add).then_inc(padded, 1)
                    split(n, q)

        @block.scalar
        def _(act):
            act.dma_start(graw[:, :, :], dram["gate"]).then_inc(g_in, 16)
            act.wait_ge(ex_done, 1)
            act.activation(ex[:, :, :], lg[:, :, :], ACT.Exp).then_inc(ex_done, 1)

            def silus(n, buf):
                act.wait_ge(g_done, n + 1)
                act.activation(silu[buf][:, :], psG[buf][:, :], ACT.Silu).then_inc(s_done, 1)

            silus(0, 0)
            with act.Fori(0, EGS // 2) as p:
                for k in range(2 * ITEMS):
                    m = 2 * ITEMS * p + k
                    silus(m + 1, (k + 1) % 2)
                    act.wait_ge(h_done, m + 1)
                    act.activation(h[k % 2][0][:, :], h32[k % 2][:, :], ACT.Copy).then_inc(hhi_done, 1)

        @block.vector
        def _(dve):
            dve.memset(pad[:, 0:1], 0.0).then_inc(d_done, 1)
            dve.memset(psY[1][:, :, :], 0.0).then_inc(acc_done, 1)
            dve.memset(acc[:, :, :], 0.0).then_inc(acc_done, 1)
            dve.wait_ge(g_in, 16)
            dve.tensor_copy(gate[0][:, :, :], graw[:, :, :]).then_inc(g_split, 1)
            dve.wait_ge(g_split, 1)
            dve.tensor_tensor(gate[1][:, :, :], graw[:, :, :], gate[0][:, :, :].bitcast(F32),
                              ALU.subtract).then_inc(g_split, 1)
            logits = psG[0][:, :].rearrange("p (t e) -> p t e", e=EXPERTS)
            steps = [0]

            def chain(ins):
                steps[0] += 1
                ins.then_inc(r_done, 1)
                dve.wait_ge(r_done, steps[0])

            def wide(a, n=EXPERTS):
                return a.unsqueeze(2).broadcast_to([P, TILES, n])

            dve.wait_ge(lg_done, 1)
            chain(dve.tensor_reduce(neg[:, :], logits, AX_X, ALU.max, negate=True))
            dve.tensor_tensor(lg[:, :, :], logits, wide(neg[:, :]), ALU.add).then_inc(ex_done, 1)
            dve.wait_ge(ex_done, 2)
            for t in range(TILES):
                last = dve.max(top[:, t, :], ex[:, t, :])
            chain(last)
            for t in range(TILES):
                last = dve.match_replace(rest[:, t, :], top[:, t, :], ex[:, t, :], -1.0)
            chain(last)
            dve.tensor_reduce(total[:, :], top[:, :, :], AX_X, ALU.add)
            chain(dve.scalar_tensor_tensor(comb[:, :, :], rest[:, :, :], 0.0, ex[:, :, :], ALU.is_lt, ALU.mult))
            chain(dve.reciprocal(inv[:, :], total[:, :]))
            chain(dve.tensor_tensor(comb[:, :, :], comb[:, :, :], wide(inv[:, :]), ALU.mult))
            dve.wait_ge(cT_ps, 1)
            dve.tensor_copy(combT[:, :, :], psU[0][:, :].rearrange("p (g n) -> p g n", g=GROUPS)).then_inc(cT_done, 1)

            def add_up(t, buf):
                at = slice(t * GW, t * GW + GW)
                dve.tensor_tensor(acc[:, :, at], acc[:, :, at], psY[buf][:, :, :], ALU.add).then_inc(acc_done, 1)

            with dve.Fori(0, EGS // 2) as p:
                for k in range(2 * ITEMS):
                    m = 2 * ITEMS * p + k
                    e, t, b = k % EG, k // EG % GROUPS, k % 2
                    if e == 0:
                        dve.wait_ge(share_in[t % 2], 16 * (4 * p + k // (2 * EG) + 1))
                    dve.wait_ge(s_done, m + 1)
                    dve.tensor_tensor(weighted[:, :], silu[b][:, :], share[t % 2][:, e, :], ALU.mult).then_inc(t_done, 1)
                    dve.wait_ge(t_done, m + 1)
                    dve.wait_ge(u_done, m + 1)
                    dve.tensor_tensor(h32[b][:, :], weighted[:, :], psU[b][:, :], ALU.mult).then_inc(h_done, 1)
                    dve.wait_ge(hhi_done, m + 1)
                    dve.tensor_tensor(h[b][1][:, :], h32[b][:, :], h[b][0][:, :].bitcast(F32),
                                      ALU.subtract).then_inc(hlo_done, 1)
                    if e == 0:
                        dve.wait_ge(d_done, m + 1)
                        dve.wait_ge(acc_done, EGS * p + k // EG + 2)
                        add_up((t - 1) % GROUPS, (t - 1) % 2)
            n = ITEMS * EGS
            dve.wait_ge(d_done, n + 1)
            add_up(GROUPS - 1, 1)
            for g in range(GROUPS):
                dve.wait_ge(yT_done, g + 1)
                at = slice(g * GT, g * GT + GT)
                dve.scalar_tensor_tensor(x[:, at, :], psY[g % 2][:, :, :].rearrange("p k (t d) -> p (k t) d", d=D),
                                         tg[:, 2:3], x[:, at, :], ALU.mult, ALU.add).then_inc(x_upd, 1)

        @block.tensor
        def _(pe):
            pe.wait_ge(g_split, 2)
            for t in range(TILES):
                mm = product(pe, psG[0][:, t * EXPERTS:t * EXPERTS + EXPERTS],
                             lambda a, k: xnT[a][:, k, t * P:t * P + P], lambda b, k: gate[b][:, k, :], KC)
            mm.then_inc(lg_done, 1)
            pe.wait_ge(r_done, 6)
            for g in range(GROUPS):
                mm = pe.transpose(psU[0][:, g * P:g * P + P], comb[:, g * GT:g * GT + GT, :], ident[:, :])
            mm.then_inc(cT_ps, 1)
            pe.wait_ge(cT_done, 1)

            def gate_up(k, buf):
                e, t = k % EG, k // EG % GROUPS
                for half, out, sem in ((0, psG, g_done), (1, psU, u_done)):
                    product(pe, out[k % 2][:, :], lambda a, c: up(buf, a, e, c, half),
                            lambda b, c: xnT[b][:, c, t * GW:t * GW + GW], KC).then_inc(sem, 1)

            def down_products(k, m, tile):
                e, t, buf = k % EG, k // EG % GROUPS, k // ITEMS
                pe.wait_ge(hlo_done, m + 1)
                if e == 0:
                    pe.wait_ge(acc_done, tile + 2)
                for c in range(KC):
                    for n, (a, b) in enumerate(PASSES):
                        mm = pe.matmul(psY[t % 2][:, c, :], down(buf, a, e, c), h[k % 2][b][:, :],
                                       start=e == 0 and n == 0, stop=e == EG - 1 and n == 2)
                mm.then_inc(d_done, 1)

            pe.wait_ge(w_split, 2)
            gate_up(0, 0)
            with pe.Fori(0, EGS // 2) as p:
                for k in range(2 * ITEMS):
                    nxt = (k + 1) % (2 * ITEMS)
                    if nxt % ITEMS == 0:
                        pe.wait_ge(w_split, 4 * p + 2 * (k + 1) // ITEMS + 2)
                    gate_up(nxt, nxt // ITEMS)
                    down_products(k, 2 * ITEMS * p + k, 2 * EG * p + k // EG)
            for g in range(GROUPS):
                pe.wait_ge(acc_done, GROUPS * EGS + 3)
                if g >= 2:
                    pe.wait_ge(x_upd, g - 1)
                for t in range(GT):
                    for c in range(KC):
                        at = t * D + c * P
                        mm = pe.transpose(psY[g % 2][:, at // GW, at % GW:at % GW + P],
                                          acc[:, c, (g * GT + t) * P:(g * GT + t) * P + P], ident[:, :])
                mm.then_inc(yT_done, 1)


def stage_cd(nc, dram, keep):
    x, _, ctxT, ident, tg = keep
    LNS = 8
    with ExitStack() as stack:
        sp_ = Space(nc, stack, "c")
        names = {"aq": [P, KC, D], "ak": [P, KC, D], "av": [P, KC, D], "router": [P, KC, E1],
                 "w1": [P, E1, KC * H1], "w2": [P, E1, HC1 * D]}
        wt = {n: sp_.pair(n, s) for n, s in names.items()}
        with ExitStack() as early:
            er = Space(nc, early, "c_raw")
            raw = {n: er.sb(n, s) for n, s in names.items()}
        xn32 = sp_.sb("xn32", [P, GT, D])
        hT = sp_.pair("hT", [P, KC, GW])
        rT = sp_.pair("rT", [P, KC, GW])
        qT = sp_.pair("qT", [P, KC, GW])
        kT = sp_.pair("kT", [P, KC, GW])
        f32 = [sp_.sb(f"f32_{b}", [P, GW]) for b in range(2)]
        v = sp_.pair("v", [P, GT, D])
        stage = sp_.sb("stage", [P, GT, 2, KC, P], F32R)
        p32 = sp_.sb("p32", [P, GT, P])
        pT = sp_.pair("pT", [P, GT, P])
        z32 = sp_.sb("z32", [P, GT, H1])
        r32 = z32
        a32 = [sp_.sb(f"a32_{b}", [P, GW]) for b in range(2)]
        a = [sp_.pair(f"a{b}", [P, GW]) for b in range(2)]
        oacc = sp_.sb("oacc", [P, GT, D])
        o32 = xn32
        out32 = sp_.sb("out32", [P, GT, D])
        vec = {n: sp_.sb(n, [P, k]) for n, k in (("bq", KC), ("bk", KC), ("rn_g", KC), ("rn_b", KC),
                                                 ("ln_g", E1 * HC1), ("ln_b", E1 * HC1))}
        wide = {n: sp_.sb(n, [P, D]) for n in ("bv", "on_g", "on_b")}
        stats = sp_.sb("stats", [P, GT, 6])
        mv = sp_.sb("mv", [P, GT, 2])
        ve = sp_.sb("ve", [P, GT])
        rstd = sp_.sb("rstd", [P, GT])
        mr = sp_.sb("mr", [P, GT])
        neghalf = sp_.sb("neghalf", [P, GT])
        pad = sp_.sb("pad", [P, 4])
        neg = sp_.sb("neg", [P, GT])
        sums = sp_.sb("sums", [P, GT])
        coef = sp_.sb("coef", [P, GT])
        g4 = sp_.sb("g4", [P, GT, E1])
        e4 = sp_.sb("e4", [P, GT, E1])
        below = sp_.sb("below", [P, GT, E1, E1])
        above = sp_.sb("above", [P, GT, E1, E1])
        ge = sp_.sb("ge", [P, GT, E1, E1])
        gt = sp_.sb("gt", [P, GT, E1, E1])
        rank = sp_.sb("rank", [P, GT, E1])
        z4 = sp_.sb("z4", [P, GT])
        s4 = sp_.sb("s4", [P, GT])
        w4 = sp_.sb("w4", [P, GT, E1])

        ring = [sp_.ps(f"ring{b}", [P, GW]) for b in range(2)]
        hid = [sp_.ps(f"hid{t}", [P, H1]) for t in range(GT)]
        psY = sp_.ps("y", [P, GT, D])

        small = ("bq", "bk", "rn_g", "rn_b", "ln_g", "ln_b", "bv", "on_g", "on_b")
        in_sems = dict(zip(tuple(names) + small, sp_.sems(*[f"{n}_in" for n in tuple(names) + small])))
        w_hi, w_lo, masks, staged, job_done, act_hi, ring_done = sp_.sems(
            "w_hi", "w_lo", "masks", "staged", "job_done", "act_hi", "ring_done")
        held, st_done, mv_done, ve_done, rstd_done, xn_ready, f_done, r_done = sp_.sems(
            "held", "st_done", "mv_done", "ve_done", "rstd_done", "xn_ready", "f_done", "r_done")
        s_done, neg_done, exp_done, pt_done, pthi_done, ptlo_done, pv_done, coef_done, x_c = sp_.sems(
            "s_done", "neg_done", "exp_done", "pt_done", "pthi_done", "ptlo_done", "pv_done", "coef_done", "x_c")
        lg_done, l4_done, e4_done, w4_done = sp_.sems("lg_done", "l4_done", "e4_done", "w4_done")
        hid_done, mr_done, z_done, t_done, a32_done, ahi_done, alo_done, y_done, y_sum = sp_.sems(
            "hid_done", "mr_done", "z_done", "t_done", "a32_done", "ahi_done", "alo_done", "y_done", "y_sum")
        o_step, out_done = sp_.sems("o_step", "out_done")

        K0, V0, N0, Q0, M0, R0 = 0, 2, 6, 8, 10, 12
        JB = R0 + KC

        block = stack.enter_context(nc.Block())

        @block.sync
        def _(sp):
            for n in names:
                sp.dma_start(raw[n][:, :, :], dram[n]).then_inc(in_sems[n], 16)
            with sp.Fori(0, GROUPS) as i:
                sp.wait_ge(o_step, 3 * i + 3)
                sp.dma_start(dram["out"].rearrange("(g t) p d -> g p t d", t=GT)[i, :, :, :], out32[:, :, :]).then_inc(out_done, 16)
            sp.wait_ge(out_done, 16 * GROUPS + 1)

        @block.gpsimd
        def _(pool):
            pool.memset(pad[:, 0:1], 0.0).then_inc(out_done, 1)
            pool.memset(neghalf[:, :], -0.5).then_inc(masks, 1)
            pool.memset(below[:, :, :, :], 0.0).then_inc(masks, 1)
            pool.memset(above[:, :, :, :], 0.0).then_inc(masks, 1)
            pool.wait_ge(masks, 3)
            for e in range(E1):
                if e:
                    pool.memset(below[:, :, e, 0:e], 1.0).then_inc(masks, 1)
                if e < E1 - 1:
                    pool.memset(above[:, :, e, e + 1:E1], 1.0).then_inc(masks, 1)
            pool.wait_ge(w_hi, 6)
            pool.tensor_tensor(wt["w2"][1][:, :, :], raw["w2"][:, :, :], wt["w2"][0][:, :, :].bitcast(F32),
                               ALU.subtract).then_inc(masks, 1)

            def rsqrt(n):
                pool.wait_ge(ve_done, n + 1)
                pool.tensor_tensor(rstd[:, :], ve[:, :], neghalf[:, :], ALU.pow).then_inc(rstd_done, 1)

            def stage_tiles(g):
                for t in range(GT):
                    for part in range(2):
                        pool.tensor_copy(stage[:, t, part, :, :], ctxT[part][:, :, bass.ds(g * GW + t * P, P)].bitcast(F32)
                                         ).then_inc(staged, 1)

            stage_tiles(0)
            with pool.Fori(0, GROUPS) as i:
                rsqrt(LNS * i)
                pool.wait_ge(job_done, JB * i + V0 + GT)
                stage_tiles((i + 1) % GROUPS)
                for n in range(1, LNS):
                    rsqrt(LNS * i + n)

        @block.scalar
        def _(act):
            for n in small:
                if n in vec:
                    act.dma_start(vec[n][:, :], dram[n]).then_inc(in_sems[n], 16)
                else:
                    act.dma_start(wide[n][:, :], dram[n].partition_broadcast(P)).then_inc(in_sems[n], 16)
            for n in names:
                act.wait_ge(in_sems[n], 16)
                act.activation(wt[n][0][:, :, :], raw[n][:, :, :], ACT.Copy).then_inc(w_hi, 1)
            act.wait_ge(in_sems["ln_g"], 16)
            act.wait_ge(in_sems["ln_b"], 16)
            act.wait_ge(masks, 4 + 2 * (E1 - 1))
            act.wait_ge(w_lo, 5)

            with act.Fori(0, GROUPS) as i:
                F = 2 * KC + GT
                for c in range(KC):
                    act.wait_ge(f_done, F * i + c + 1)
                    act.activation(kT[0][:, c, :], f32[c % 2][:, :], ACT.Copy).then_inc(act_hi, 1)
                for t in range(GT):
                    act.wait_ge(f_done, F * i + KC + t + 1)
                    act.activation(v[0][:, t, :], f32[t % 2][:, 0:D], ACT.Copy).then_inc(act_hi, 1)
                for c in range(KC):
                    act.wait_ge(job_done, JB * i + N0 + c + 1)
                    act.activation(hT[0][:, c, :], ring[c][:, :], ACT.Copy).then_inc(act_hi, 1)
                for c in range(KC):
                    act.wait_ge(f_done, F * i + KC + GT + c + 1)
                    act.activation(qT[0][:, c, :], f32[c % 2][:, :], ACT.Copy).then_inc(act_hi, 1)
                act.wait_ge(neg_done, i + 1)
                for b in range(GT):
                    ins = act.activation(p32[:, b, :], hid[0][:, b * P:b * P + P], ACT.Exp, bias=neg[:, b:b + 1],
                                         accum_out=sums[:, b:b + 1])
                ins.then_inc(exp_done, 1)
                act.wait_ge(pt_done, i + 1)
                act.activation(pT[0][:, :, :], hid[1][:, :].rearrange("p (t n) -> p t n", t=GT), ACT.Copy).then_inc(pthi_done, 1)
                for c in range(KC):
                    act.wait_ge(job_done, JB * i + M0 + c + 1)
                    act.activation(hT[0][:, c, :], ring[c][:, :], ACT.Copy).then_inc(act_hi, 1)
                for c in range(KC):
                    act.wait_ge(r_done, KC * i + c + 1)
                    act.activation(rT[0][:, c, :], r32[:, c, :], ACT.Copy).then_inc(act_hi, 1)
                act.wait_ge(l4_done, i + 1)
                act.activation(e4[:, :, :], g4[:, :, :], ACT.Exp).then_inc(e4_done, 1)
                for e in range(E1):
                    act.wait_ge(mr_done, E1 * i + e + 1)
                    for t in range(GT):
                        ins = act.activation(z32[:, t, :], hid[t][:, :], ACT.Identity, scale=rstd[:, t:t + 1], bias=mr[:, t:t + 1])
                    ins.then_inc(z_done, 1)
                    for c in range(HC1):
                        n = E1 * HC1 * i + e * HC1 + c
                        k = e * HC1 + c
                        act.wait_ge(t_done, n + 1)
                        act.activation(a32[c % 2][:, :], ring[c % 2][:, :], ACT.Relu, scale=vec["ln_g"][:, k:k + 1],
                                       bias=vec["ln_b"][:, k:k + 1]).then_inc(a32_done, 1)
                        act.activation(a[c % 2][0][:, :], ring[c % 2][:, :], ACT.Relu, scale=vec["ln_g"][:, k:k + 1],
                                       bias=vec["ln_b"][:, k:k + 1]).then_inc(ahi_done, 1)

        @block.vector
        def _(dve):
            dve.memset(pad[:, 1:2], 0.0).then_inc(held, 1)
            for k, n in enumerate(("aq", "ak", "av", "router", "w1")):
                dve.wait_ge(w_hi, k + 1)
                dve.tensor_tensor(wt[n][1][:, :, :], raw[n][:, :, :], wt[n][0][:, :, :].bitcast(F32),
                                  ALU.subtract).then_inc(w_lo, 1)
            for n in small:
                dve.wait_ge(in_sems[n], 16)
            dve.wait_ge(masks, 4 + 2 * (E1 - 1))

            def carry(n, sem, value):
                dve.wait_ge(held, n + 1)
                dve.wait_ge(sem, value)
                dve.memset(pad[:, 1:2], 0.0).then_inc(held, 1)

            def ln_stats(n, src):
                for t in range(GT):
                    dve.bn_stats(stats[:, t, :], src(t)).then_inc(st_done, 1)
                carry(n + i + (0 if n is first_ln else 1), st_done, GT * n + GT)
                for t in range(GT):
                    dve.bn_aggr(mv[:, t, :], stats[:, t, :]).then_inc(mv_done, 1)
                dve.wait_ge(mv_done, GT * n + GT)
                dve.tensor_scalar(ve[:, :], mv[:, :, 1], EPS_LN, None, ALU.add).then_inc(ve_done, 1)
                dve.wait_ge(rstd_done, n + 1)

            def ln_apply(dst, src):
                for t in range(GT):
                    dve.tensor_scalar(dst[:, t, :], src(t), mv[:, t, 0:1], rstd[:, t:t + 1],
                                      ALU.subtract, ALU.mult).then_inc(xn_ready, 1)

            def lower(dst, full, hi, n):
                dve.wait_ge(act_hi, n + 1)
                dve.tensor_tensor(dst, full, hi.bitcast(F32), ALU.subtract).then_inc(ring_done, 1)

            with dve.Fori(0, GROUPS) as i:
                F = 2 * KC + GT
                XN = 4 * GT * i
                for c in range(KC):
                    dve.wait_ge(job_done, JB * i + K0 + c + 1)
                    dve.tensor_scalar(f32[c % 2][:, :], ring[c][:, :], vec["bk"][:, c:c + 1], None, ALU.add).then_inc(f_done, 1)
                    lower(kT[1][:, c, :], f32[c % 2][:, :], kT[0][:, c, :], JB * i + K0 + c)
                for t in range(GT):
                    dve.wait_ge(job_done, JB * i + V0 + t + 1)
                    dve.tensor_tensor(f32[t % 2][:, 0:D], ring[t % 2][:, 0:D], wide["bv"][:, :], ALU.add).then_inc(f_done, 1)
                    lower(v[1][:, t, :], f32[t % 2][:, 0:D], v[0][:, t, :], JB * i + V0 + t)
                first_ln = LNS * i
                ln_stats(first_ln, lambda t: x[:, i * GT + t, :])
                ln_apply(xn32, lambda t: x[:, i * GT + t, :])
                for c in range(KC):
                    lower(hT[1][:, c, :], ring[c][:, :], hT[0][:, c, :], JB * i + N0 + c)
                for c in range(KC):
                    dve.wait_ge(job_done, JB * i + Q0 + c + 1)
                    dve.tensor_scalar(f32[c % 2][:, :], ring[c][:, :], vec["bq"][:, c:c + 1], D ** -0.5,
                                      ALU.add, ALU.mult).then_inc(f_done, 1)
                    lower(qT[1][:, c, :], f32[c % 2][:, :], qT[0][:, c, :], JB * i + Q0 + c)
                dve.wait_ge(s_done, i + 1)
                dve.tensor_reduce(neg[:, :], hid[0][:, :].rearrange("p (t n) -> p t n", t=GT), AX_X, ALU.max,
                                  negate=True).then_inc(neg_done, 1)
                dve.wait_ge(pthi_done, i + 1)
                dve.tensor_tensor(pT[1][:, :, :], hid[1][:, :].rearrange("p (t n) -> p t n", t=GT),
                                  pT[0][:, :, :].bitcast(F32), ALU.subtract).then_inc(ptlo_done, 1)
                dve.reciprocal(coef[:, :], sums[:, :]).then_inc(coef_done, 1)
                dve.wait_ge(coef_done, 2 * i + 1)
                dve.tensor_scalar(coef[:, :], coef[:, :], tg[:, 1:2], None, ALU.mult).then_inc(coef_done, 1)
                dve.wait_ge(coef_done, 2 * i + 2)
                dve.wait_ge(pv_done, i + 1)
                for b in range(GT):
                    dve.scalar_tensor_tensor(x[:, i * GT + b, :], hid[2 + b // 2][:, (b % 2) * D:(b % 2) * D + D],
                                             coef[:, b:b + 1], x[:, i * GT + b, :], ALU.mult, ALU.add).then_inc(x_c, 1)
                carry((LNS + 1) * i + 1, x_c, GT * i + GT)
                ln_stats(LNS * i + 1, lambda t: x[:, i * GT + t, :])
                ln_apply(xn32, lambda t: x[:, i * GT + t, :])
                for c in range(KC):
                    lower(hT[1][:, c, :], ring[c][:, :], hT[0][:, c, :], JB * i + M0 + c)
                dve.wait_ge(xn_ready, XN + 2 * GT)
                ln_stats(LNS * i + 2, lambda t: xn32[:, t, :])
                ln_apply(oacc, lambda t: xn32[:, t, :])
                for c in range(KC):
                    dve.wait_ge(job_done, JB * i + R0 + c + 1)
                    dve.tensor_scalar(r32[:, c, :], ring[c][:, :], vec["rn_g"][:, c:c + 1], vec["rn_b"][:, c:c + 1],
                                      ALU.mult, ALU.add).then_inc(r_done, 1)
                    lower(rT[1][:, c, :], r32[:, c, :], rT[0][:, c, :], JB * i + R0 + c)
                steps = [0]
                CHAIN = 15

                def chain(ins):
                    steps[0] += 1
                    ins.then_inc(w4_done, 1)
                    dve.wait_ge(w4_done, CHAIN * i + steps[0])

                def over(ap):
                    return ap[:, :].unsqueeze(2).broadcast_to([P, GT, E1])

                logits = hid[1][:, 0:GT * E1].rearrange("p (t e) -> p t e", e=E1)
                dve.wait_ge(lg_done, i + 1)
                chain(dve.tensor_reduce(s4[:, :], logits, AX_X, ALU.max, negate=True))
                dve.tensor_tensor(g4[:, :, :], logits, over(s4), ALU.add).then_inc(l4_done, 1)
                dve.wait_ge(e4_done, i + 1)
                chain(dve.tensor_reduce(z4[:, :], e4[:, :, :], AX_X, ALU.add))
                chain(dve.reciprocal(s4[:, :], z4[:, :]))
                chain(dve.tensor_tensor(e4[:, :, :], e4[:, :, :], over(s4), ALU.mult))
                mine = e4[:, :, :].unsqueeze(3).broadcast_to([P, GT, E1, E1])
                other = e4[:, :, :].unsqueeze(2).broadcast_to([P, GT, E1, E1])
                chain(dve.tensor_tensor(ge[:, :, :, :], other, mine, ALU.is_ge))
                chain(dve.tensor_tensor(ge[:, :, :, :], ge[:, :, :, :], below[:, :, :, :], ALU.mult))
                chain(dve.tensor_tensor(gt[:, :, :, :], other, mine, ALU.is_gt))
                chain(dve.tensor_tensor(gt[:, :, :, :], gt[:, :, :, :], above[:, :, :, :], ALU.mult))
                chain(dve.tensor_tensor(ge[:, :, :, :], ge[:, :, :, :], gt[:, :, :, :], ALU.add))
                chain(dve.tensor_reduce(rank[:, :, :], ge[:, :, :, :], AX_X, ALU.add))
                chain(dve.scalar_tensor_tensor(w4[:, :, :], rank[:, :, :], 1.5, e4[:, :, :], ALU.is_lt, ALU.mult))
                chain(dve.tensor_reduce(z4[:, :], w4[:, :, :], AX_X, ALU.add))
                chain(dve.tensor_scalar(z4[:, :], z4[:, :], EPS_GATE, None, ALU.add))
                chain(dve.reciprocal(s4[:, :], z4[:, :]))
                chain(dve.tensor_tensor(w4[:, :, :], w4[:, :, :], over(s4), ALU.mult))
                assert steps[0] == CHAIN
                for e in range(E1):
                    dve.wait_ge(hid_done, E1 * i + e + 1)
                    ln_stats(LNS * i + 3 + e, lambda t: hid[t][:, :])
                    dve.scalar_tensor_tensor(mr[:, :], mv[:, :, 0], -1.0, rstd[:, :], ALU.mult, ALU.mult).then_inc(mr_done, 1)
                    for c in range(HC1):
                        n = E1 * HC1 * i + e * HC1 + c
                        dve.wait_ge(ahi_done, n + 1)
                        dve.tensor_tensor(a[c % 2][1][:, :], a32[c % 2][:, :], a[c % 2][0][:, :].bitcast(F32),
                                          ALU.subtract).then_inc(alo_done, 1)
                    dve.wait_ge(y_done, E1 * i + e + 1)
                    if e:
                        dve.wait_ge(y_sum, GT * (E1 * i + e))
                    for t in range(GT):
                        if e == 0:
                            dve.tensor_scalar(oacc[:, t, :], psY[:, t, :], w4[:, t, e:e + 1], None, ALU.mult).then_inc(y_sum, 1)
                        else:
                            dve.scalar_tensor_tensor(oacc[:, t, :], psY[:, t, :], w4[:, t, e:e + 1], oacc[:, t, :],
                                                     ALU.mult, ALU.add).then_inc(y_sum, 1)
                dve.wait_ge(y_sum, GT * (E1 * i + E1))
                ln_stats(LNS * i + 7, lambda t: oacc[:, t, :])
                ln_apply(o32, lambda t: oacc[:, t, :])
                dve.wait_ge(xn_ready, XN + 4 * GT)
                dve.tensor_tensor(o32[:, :, :], o32[:, :, :], wide["on_g"][:, :].unsqueeze(1).broadcast_to([P, GT, D]),
                                  ALU.mult).then_inc(o_step, 1)
                dve.wait_ge(o_step, 3 * i + 1)
                dve.tensor_tensor(o32[:, :, :], o32[:, :, :], wide["on_b"][:, :].unsqueeze(1).broadcast_to([P, GT, D]),
                                  ALU.add).then_inc(o_step, 1)
                dve.wait_ge(o_step, 3 * i + 2)
                dve.wait_ge(out_done, 16 * i + 1)
                dve.scalar_tensor_tensor(out32[:, :, :], o32[:, :, :], tg[:, 3:4], x[:, bass.ds(i * GT, GT), :],
                                         ALU.mult, ALU.add).then_inc(o_step, 1)

        @block.tensor
        def _(pe):
            pe.wait_ge(w_lo, 5)
            pe.wait_ge(masks, 4 + 2 * (E1 - 1))
            with pe.Fori(0, GROUPS) as i:
                J = JB * i
                XN = 4 * GT * i

                def turn(job):
                    pe.wait_ge(ring_done, J + job - 1)

                def ln_jobs(job, src):
                    for c in range(KC):
                        turn(job + c)
                        for t in range(GT):
                            mm = pe.transpose(ring[c][:, t * P:t * P + P], src[:, t, c * P:c * P + P], ident[:, :])
                        mm.then_inc(job_done, 1)

                for c in range(KC):
                    product(pe, ring[c][:, :], lambda a, k: wt["ak"][a][:, k, c * P:c * P + P],
                            lambda b, k: ctxT[b][:, k, bass.ds(i * GW, GW)], KC).then_inc(job_done, 1)
                pe.wait_ge(staged, 2 * GT * (i + 1))
                for t in range(GT):
                    turn(V0 + t)
                    product(pe, ring[t % 2][:, 0:D], lambda a, k: stage[:, t, a, k, :],
                            lambda b, k: wt["av"][b][:, k, :], KC).then_inc(job_done, 1)
                pe.wait_ge(xn_ready, XN + GT)
                ln_jobs(N0, xn32)
                pe.wait_ge(ring_done, J + N0 + KC)
                for c in range(KC):
                    turn(Q0 + c)
                    product(pe, ring[c][:, :], lambda a, k: wt["aq"][a][:, k, c * P:c * P + P],
                            lambda b, k: hT[b][:, k, :], KC).then_inc(job_done, 1)
                pe.wait_ge(ring_done, J + Q0 + KC)
                for b in range(GT):
                    at = slice(b * P, b * P + P)
                    mm = product(pe, hid[0][:, at], lambda a, k: qT[a][:, k, at], lambda a, k: kT[a][:, k, at], KC)
                mm.then_inc(s_done, 1)
                pe.wait_ge(exp_done, i + 1)
                for b in range(GT):
                    mm = pe.transpose(hid[1][:, b * P:b * P + P], p32[:, b, :], ident[:, :])
                mm.then_inc(pt_done, 1)
                pe.wait_ge(ptlo_done, i + 1)
                for b in range(GT):
                    mm = product(pe, hid[2 + b // 2][:, (b % 2) * D:(b % 2) * D + D], lambda a, k: pT[a][:, b, :],
                                 lambda a, k: v[a][:, b, :], 1)
                mm.then_inc(pv_done, 1)
                pe.wait_ge(xn_ready, XN + 2 * GT)
                ln_jobs(M0, xn32)
                pe.wait_ge(xn_ready, XN + 3 * GT)
                ln_jobs(R0, oacc)
                pe.wait_ge(ring_done, J + JB)
                for t in range(GT):
                    mm = product(pe, hid[1][:, t * E1:t * E1 + E1], lambda a, k: rT[a][:, k, t * P:t * P + P],
                                 lambda b, k: wt["router"][b][:, k, :], KC)
                mm.then_inc(lg_done, 1)
                pe.wait_ge(l4_done, i + 1)

                def hidden(e):
                    for t in range(GT):
                        mm = product(pe, hid[t][:, :], lambda a, k: hT[a][:, k, t * P:t * P + P],
                                     lambda b, k: wt["w1"][b][:, e, k * H1:k * H1 + H1], KC)
                    mm.then_inc(hid_done, 1)

                def turned(e, c):
                    if e or c > 1:
                        pe.wait_ge(ahi_done, E1 * HC1 * i + e * HC1 + c - 1)
                    for t in range(GT):
                        mm = pe.transpose(ring[c % 2][:, t * P:t * P + P], z32[:, t, c * P:c * P + P], ident[:, :])
                    mm.then_inc(t_done, 1)

                def second(e, c):
                    pe.wait_ge(alo_done, E1 * HC1 * i + e * HC1 + c + 1)
                    if c == 0 and e:
                        pe.wait_ge(y_sum, GT * (E1 * i + e))
                    for t in range(GT):
                        for n, (p, q) in enumerate(PASSES):
                            mm = pe.matmul(psY[:, t, :], a[c % 2][p][:, t * P:t * P + P], wt["w2"][q][:, e, c * D:c * D + D],
                                           start=c == 0 and n == 0 and t % 2 == 0, stop=c == HC1 - 1 and n == 2,
                                           skip_group_check=True)
                    if c == HC1 - 1:
                        mm.then_inc(y_done, 1)

                hidden(0)
                for e in range(E1):
                    pe.wait_ge(z_done, E1 * i + e + 1)
                    if e < E1 - 1:
                        hidden(e + 1)
                    turned(e, 0)
                    turned(e, 1)
                    for c in range(HC1):
                        second(e, c)
                        if c + 2 < HC1:
                            turned(e, c + 2)


def program(nc, dram):
    with ExitStack() as stack:
        keep = Space(nc, stack, "all")
        x = keep.sb("x", [P, TILES, D])
        ctxT = keep.pair("ctxT", [P, KC, TOK])
        ident = keep.sb("ident", [P, P])
        tg = keep.sb("tg", [P, 4])
        with ExitStack() as first:
            xnT = Space(nc, first, "ab").pair("xnT", [P, KC, TOK])
            stage_a(nc, dram, (x, xnT, ctxT, ident, tg))
            stage_b(nc, dram, (x, xnT, ctxT, ident, tg))
        stage_cd(nc, dram, (x, None, ctxT, ident, tg))


def kernel(**inputs):
    import numpy as np
    import concourse.bacc as bacc
    from concourse.bass_utils import run_bass_kernel_spmd

    def rows(a):
        a = np.asarray(a)
        return a.reshape(-1, P, *a.shape[1:]).swapaxes(0, 1)

    x, ctx = (np.asarray(inputs[n]).reshape(TOK, D) for n in ("x", "ctx_1024"))
    laid = {
        "x": rows(x),
        "ctxT": rows(ctx.T),
        "g": np.concatenate([inputs["g_xattn"], inputs["g_ffn"]]),
        "wq": rows(inputs["L0_xattn_W_Q"]),
        "wk": rows(inputs["L0_xattn_W_K"]),
        "wv": rows(inputs["L0_xattn_W_V"]),
        "wo": rows(inputs["L0_xattn_W_O"]),
    }
    gu = inputs["L0_ffn_gate_up_w"].reshape(EGS, EG, 2 * XD, KC, P).transpose(0, 4, 1, 3, 2)
    dn = inputs["L0_ffn_down_w"].reshape(EGS, EG, D, XD).transpose(0, 3, 1, 2)
    laid["moe"] = np.concatenate([gu.reshape(EGS, P, -1), dn.reshape(EGS, P, -1)], axis=2)
    laid["gate"] = rows(inputs["L0_ffn_gate_w"].T)
    for short, name in (("aq", "Wq"), ("ak", "Wk"), ("av", "Wv")):
        laid[short] = rows(inputs["L1_xattn_" + name].T)
    laid["router"] = rows(inputs["L1_ffn_router_w"].T)
    laid["w1"] = inputs["L1_ffn_w1"].reshape(E1, KC, P, H1).transpose(2, 0, 1, 3).reshape(P, E1, KC * H1)
    laid["w2"] = inputs["L1_ffn_w2"].reshape(E1, HC1, P, D).transpose(2, 0, 1, 3).reshape(P, E1, HC1 * D)
    for short, name in (("bq", "xattn_bq"), ("bk", "xattn_bk"), ("rn_g", "ffn_rn_g"), ("rn_b", "ffn_rn_b")):
        laid[short] = rows(inputs["L1_" + name])
    for short in ("ln_g", "ln_b"):
        laid[short] = inputs["L1_ffn_" + short].reshape(E1, HC1, P).transpose(2, 0, 1).reshape(P, E1 * HC1)
    for short, name in (("bv", "xattn_bv"), ("on_g", "ffn_on_g"), ("on_b", "ffn_on_b")):
        laid[short] = inputs["L1_" + name]
    laid = {n: np.ascontiguousarray(a) for n, a in laid.items()}
    nc = bacc.Bacc("TRN2", target_bir_lowering=False, num_devices=1, dynamic_dma_scratch_size=1024)
    dram = {n: nc.dram_tensor(f"in_{n}", a.shape, F32, kind="ExternalInput").ap() for n, a in laid.items()}
    dram["shares"] = nc.dram_tensor("shares", (EXPERTS, TOK), F32, kind="Internal").ap()
    dram["out"] = nc.dram_tensor("out", (TILES, P, D), F32, kind="ExternalOutput").ap()
    program(nc, dram)
    r = run_bass_kernel_spmd(nc, [{f"in_{n}": a for n, a in laid.items()}], core_ids=[0])
    return r.results[0]["out"]
```

```python
from contextlib import ExitStack

import concourse.bass as bass
from concourse import mybir

F32 = mybir.dt.float32
F32R = mybir.dt.float32r
ALU = mybir.AluOpType
ACT = mybir.ActivationFunctionType
AX_X = mybir.AxisListType.X

P = 128
D = 256
KC = D // P
TOK = 2048
TILES = TOK // P
GT = 4
GW = GT * P
GROUPS = TILES // GT
HEADS, DH = 16, 64
HD = HEADS * DH
CH = HD // P
EXPERTS, TOPK, XD = 32, 8, 128
EG = 4
EGS = EXPERTS // EG
E1, H1 = 4, 512
HC1 = H1 // P
EPS_LN = 1e-5
EPS_GATE = 1e-8

PASSES = ((0, 0), (0, 1), (1, 0))


def product(pe, out, stationary, moving, chunks, start=True, stop=True, skip=False):
    last = None
    for k in range(chunks):
        for n, (a, b) in enumerate(PASSES):
            last = pe.matmul(out, stationary(a, k), moving(b, k), start=start and k == 0 and n == 0,
                             stop=stop and k == chunks - 1 and n == 2, skip_group_check=skip)
    return last


class Space:

    def __init__(self, nc, stack, prefix):
        self.nc, self.stack, self.prefix = nc, stack, prefix

    def sb(self, name, shape, dt=F32):
        return self.stack.enter_context(self.nc.sbuf_tensor(f"{self.prefix}_{name}", shape, dt))

    def pair(self, name, shape):
        return [self.sb(f"{name}_hi", shape, F32R), self.sb(f"{name}_lo", shape, F32R)]

    def ps(self, name, shape):
        return self.stack.enter_context(self.nc.psum_tensor(f"{self.prefix}_{name}", shape, F32))

    def sems(self, *names):
        return [self.stack.enter_context(self.nc.semaphore(f"{self.prefix}_{n}")) for n in names]


def carve(region, shapes):
    views, at = {}, 0
    for name, dims in shapes.items():
        size = 1
        for n in dims:
            size *= n
        view = region[:, at:at + size]
        if len(dims) > 1:
            letters = "abc"[:len(dims)]
            view = view.rearrange(f"p ({' '.join(letters)}) -> p {' '.join(letters)}", **dict(zip(letters, dims)))
        views[name], at = view, at + size
    return views


A_WEIGHTS = {"wq": (KC, HD), "wk": (KC, HD), "wv": (KC, HD), "wo": (CH, D)}
A_WORK = {"v32": (GT, HD), "p32": (GT, 2, P), "vs32": (GT, 2, DH), "neg": (2, GT), "sums": (GT, 2), "rinv": (GT, 2), "unused": (2536,), "xn32": (GT, D)}


def stage_a(nc, dram, keep, region):
    x, xnT, ctxT, ident, tg = keep
    with ExitStack() as stack:
        sp_ = Space(nc, stack, "a")
        w = {n: sp_.pair(n, [P, *s]) for n, s in A_WEIGHTS.items()}
        raw, work = carve(region, A_WEIGHTS), carve(region, A_WORK)
        with ExitStack() as early:
            ctx_raw = Space(nc, early, "a_raw").sb("ctx", [P, KC, TOK])
        qT = [sp_.pair(f"qT{b}", [P, GW]) for b in range(2)]
        kT = [sp_.pair(f"kT{b}", [P, GW]) for b in range(2)]
        probs = sp_.pair("probs", [P, GT, 2, P])
        v32, p32, vs32, xn32 = (work[n] for n in ("v32", "p32", "vs32", "xn32"))
        vs = sp_.pair("vs", [P, GT, 2, DH])
        oT = sp_.pair("oT", [P, GT, P])
        stage = sp_.sb("stage", [P, GT, 2, KC, P], F32R)
        graw = sp_.sb("graw", [P, 4])
        stats = sp_.sb("stats", [P, GT, 6])
        mv = sp_.sb("mv", [P, GT, 2])
        ve = sp_.sb("ve", [P, GT])
        rstd = sp_.sb("rstd", [P, GT])
        neghalf = sp_.sb("neghalf", [P, GT])
        pad = sp_.sb("pad", [P, 4])
        neg, sums, rinv = (work[n] for n in ("neg", "sums", "rinv"))

        ring = [sp_.ps(f"ring{b}", [P, GW]) for b in range(2)]
        psS = sp_.ps("scores", [P, 2, GT, P])
        psV = sp_.ps("values", [P, GT, 2 * P])
        psO = sp_.ps("outs", [P, GT, D])

        g_in, ctx_in, wq_in, wk_in, wv_in, wo_in = sp_.sems("g_in", "ctx_in", "wq_in", "wk_in", "wv_in", "wo_in")
        x_in = sp_.sems(*[f"x_in{g}" for g in range(GROUPS)])
        split_hi, split_lo, split_v, ident_done = sp_.sems("split_hi", "split_lo", "split_v", "ident_done")
        job_done, act_hi, ring_done = sp_.sems("job_done", "act_hi", "ring_done")
        s_done, neg_done, exp_done, rinv_done, vs32_done = sp_.sems("s_done", "neg_done", "exp_done", "rinv_done", "vs32_done")
        vhi_done, vlo_done, phi_done, plo_done, pv_done = sp_.sems("vhi_done", "vlo_done", "phi_done", "plo_done", "pv_done")
        ohi_done, ot_done, o_done, x_upd, staged = sp_.sems("ohi_done", "ot_done", "o_done", "x_upd", "staged")
        st_done, mv_done, ve_done, rstd_done, xn_ready, held = sp_.sems("st_done", "mv_done", "ve_done", "rstd_done", "xn_ready", "held")

        JOBS0, HIS0 = 10, 6
        jobs, his = {}, {}
        nj = nh = 0
        for s in range(CH):
            if s in (2, 4):
                jobs[s, "ln"], his[s, "ln"] = nj, nh
                nj, nh = nj + KC, nh + KC
            jobs[s, "v"] = nj
            jobs[s, "q"], his[s, "q"] = nj + 1, nh
            jobs[s, "k"], his[s, "k"] = nj + 2, nh + 1
            nj, nh = nj + 3, nh + 2
        JOBS, HIS = nj, nh
        assert JOBS % 2 == 0 and JOBS0 % 2 == 0
        SPLITS = ("wq", "ctx", "wk")

        block = stack.enter_context(nc.Block())

        @block.sync
        def _(sp):
            sp.dma_start(x[:, 0:GT, :], dram["x"][:, 0:GT, :]).then_inc(x_in[0], 16)
            sp.dma_start(ctx_raw[:, :, :], dram["ctxT"]).then_inc(ctx_in, 16)
            sp.dma_start(raw["wv"][:, :, :], dram["wv"]).then_inc(wv_in, 16)
            for g in range(1, GROUPS):
                sp.dma_start(x[:, GT * g:GT * g + GT, :], dram["x"][:, GT * g:GT * g + GT, :]).then_inc(x_in[g], 16)

        @block.gpsimd
        def _(pool):
            pool.memset(ident[:, :], 0.0).then_inc(ident_done, 1)
            pool.memset(neghalf[:, :], -0.5).then_inc(ident_done, 1)
            pool.wait_ge(ident_done, 2)
            pool.affine_select(out=ident[:, :], in_=ident[:, :], compare_op=ALU.not_equal, fill=1.0, base=0,
                               pattern=[[-1, P]], channel_multiplier=1).then_inc(ident_done, 1)

            def rsqrt(n):
                pool.wait_ge(ve_done, n + 1)
                pool.tensor_tensor(rstd[:, :], ve[:, :], neghalf[:, :], ALU.pow).then_inc(rstd_done, 1)

            def split_here(name, value):
                pool.tensor_copy(w[name][0][:, :, :], raw[name][:, :, :]).then_inc(split_v, 1)
                pool.wait_ge(split_v, value)
                pool.tensor_tensor(w[name][1][:, :, :], raw[name][:, :, :], w[name][0][:, :, :].bitcast(F32),
                                   ALU.subtract).then_inc(split_v, 1)

            def stage_tile(t, g):
                for part in range(2):
                    pool.tensor_copy(stage[:, t, part, :, :], ctxT[part][:, :, bass.ds(g * GW + t * P, P)].bitcast(F32)
                                     ).then_inc(staged, 1)

            def probs_lo(n):
                pool.wait_ge(phi_done, n + 1)
                pool.tensor_tensor(probs[1][:, :, :, :], p32[:, :, :, :], probs[0][:, :, :, :].bitcast(F32),
                                   ALU.subtract).then_inc(plo_done, 1)

            rsqrt(0)
            pool.wait_ge(wv_in, 16)
            split_here("wv", 1)
            pool.wait_ge(split_lo, 2)
            for t in range(GT):
                stage_tile(t, 0)
            pool.wait_ge(wo_in, 16)
            split_here("wo", 3)
            probs_lo(0)
            with pool.Fori(0, GROUPS) as i:
                for s in range(CH):
                    if s == 1:
                        rsqrt(2 * i + 1)
                    if s == 3:
                        rsqrt(2 * i + 2)
                    if s < GT:
                        pool.wait_ge(job_done, JOBS0 + JOBS * i + jobs[s, "v"] + 1)
                        stage_tile(s, (i + 1) % GROUPS)
                    probs_lo(CH * i + s + 1)
            rsqrt(2 * GROUPS + 1)

        @block.scalar
        def _(act):
            act.dma_start(raw["wq"], dram["wq"]).then_inc(wq_in, 16)
            act.dma_start(raw["wk"][:, :, :], dram["wk"]).then_inc(wk_in, 16)
            act.dma_start(raw["wo"][:, :, :], dram["wo"]).then_inc(wo_in, 16)
            act.dma_start(graw[:, :], dram["g"].partition_broadcast(P)).then_inc(g_in, 16)
            for name, sem in zip(SPLITS, (wq_in, ctx_in, wk_in)):
                act.wait_ge(sem, 16)
                hi, src = (ctxT[0], ctx_raw) if name == "ctx" else (w[name][0], raw[name])
                act.activation(hi[:, :, :], src[:, :, :], ACT.Copy).then_inc(split_hi, 1)
            act.wait_ge(g_in, 16)
            act.activation(tg[:, :], graw[:, :], ACT.Tanh).then_inc(g_in, 1)

            def ln_hi(job, kc, g):
                act.wait_ge(job_done, job + 1)
                act.activation(xnT[0][:, kc, bass.ds(g * GW, GW)], ring[kc][:, :], ACT.Copy).then_inc(act_hi, 1)

            def qk_hi(which, job, bank, buf, n):
                act.wait_ge(job_done, job + 1)
                if n is not None:
                    act.wait_ge(s_done, n)
                dst, scale = (qT, DH ** -0.5) if which == "q" else (kT, 1.0)
                act.activation(dst[buf][0][:, :], ring[bank][:, :], ACT.Copy, scale=scale).then_inc(act_hi, 1)

            def exps(n, part, first):
                if part == 0:
                    act.wait_ge(neg_done, n + 1)
                    if not first:
                        act.wait_ge(plo_done, n)
                        act.wait_ge(phi_done, n)
                for b in range(2 * part, 2 * part + 2):
                    for j in range(2):
                        ins = act.activation(p32[:, b, j, :], psS[:, j, b, :], ACT.Exp, bias=neg[:, j, b:b + 1],
                                             accum_out=sums[:, b, j:j + 1])
                if part == 1:
                    ins.then_inc(exp_done, 1)

            def out_hi(n):
                act.wait_ge(pv_done, n + 1)
                act.wait_ge(o_done, n + 1)
                for j in range(2):
                    lanes = slice(DH * j, DH * j + DH)
                    act.activation(oT[0][lanes, :, :], psV[lanes, :, P * j:P * j + P], ACT.Copy).then_inc(ohi_done, 1)

            for kc in range(KC):
                ln_hi(kc, kc, 0)
            for step in range(2):
                qk_hi("q", 6 + 2 * step, 0, step, None)
                qk_hi("k", 7 + 2 * step, 1, step, None)
            exps(0, 0, True)
            exps(0, 1, True)
            with act.Fori(0, GROUPS) as i:
                for s in range(CH):
                    n = CH * i + s + 1
                    J = JOBS0 + JOBS * i
                    if s in (2, 4):
                        for kc in range(KC):
                            ln_hi(J + jobs[s, "ln"] + kc, kc, (i + (3 if s == 2 else 1)) % GROUPS)
                    out_hi(n - 1)
                    exps(n, 0, False)
                    qk_hi("q", J + jobs[s, "q"], jobs[s, "q"] % 2, s % 2, n)
                    exps(n, 1, False)
                    qk_hi("k", J + jobs[s, "k"], jobs[s, "k"] % 2, s % 2, n)
            for kc in range(KC):
                ln_hi(JOBS0 + JOBS * GROUPS + kc, kc, GROUPS - 1)

        @block.vector
        def _(dve):
            dve.memset(pad[:, 1:2], 0.0).then_inc(x_upd, 1)
            dve.memset(pad[:, 2:3], 0.0).then_inc(ot_done, 1)
            dve.memset(pad[:, 3:4], 0.0).then_inc(o_done, 1)
            dve.memset(pad[:, 0:1], 0.0).then_inc(held, 1)

            def ln_stats(n, g, landed):
                if landed is not None:
                    dve.wait_ge(landed, 16)
                else:
                    dve.wait_ge(x_upd, g[1])
                gx = g[0]
                for t in range(GT):
                    dve.bn_stats(stats[:, t, :], x[:, gx * GT + t, :]).then_inc(st_done, 1)
                dve.wait_ge(held, n + 1)
                dve.wait_ge(st_done, GT * n + GT)
                dve.memset(pad[:, 0:1], 0.0).then_inc(held, 1)
                for t in range(GT):
                    dve.bn_aggr(mv[:, t, :], stats[:, t, :]).then_inc(mv_done, 1)
                dve.wait_ge(mv_done, GT * n + GT)
                dve.tensor_scalar(ve[:, :], mv[:, :, 1], EPS_LN, None, ALU.add).then_inc(ve_done, 1)

            def ln_apply(n, gx):
                dve.wait_ge(rstd_done, n + 1)
                for t in range(GT):
                    dve.tensor_scalar(xn32[:, t, :], x[:, gx * GT + t, :], mv[:, t, 0:1], rstd[:, t:t + 1],
                                      ALU.subtract, ALU.mult).then_inc(xn_ready, 1)

            def ln_lo(hi, kc, g):
                dve.wait_ge(act_hi, hi + 1)
                at = bass.ds(g * GW, GW)
                dve.tensor_tensor(xnT[1][:, kc, at], ring[kc][:, :], xnT[0][:, kc, at].bitcast(F32),
                                  ALU.subtract).then_inc(ring_done, 1)

            def v_out(job, bank, t, half):
                dve.wait_ge(job_done, job + 1)
                dve.tensor_copy(v32[:, t, half * 512:half * 512 + 512], ring[bank][:, :]).then_inc(ring_done, 1)

            def qk_lo(which, hi, bank, buf):
                dve.wait_ge(act_hi, hi + 1)
                if which == "q":
                    dve.scalar_tensor_tensor(qT[buf][1][:, :], ring[bank][:, :], DH ** -0.5,
                                             qT[buf][0][:, :].bitcast(F32), ALU.mult, ALU.subtract).then_inc(ring_done, 1)
                else:
                    dve.tensor_tensor(kT[buf][1][:, :], ring[bank][:, :], kT[buf][0][:, :].bitcast(F32),
                                      ALU.subtract).then_inc(ring_done, 1)

            def minus_max(n):
                dve.wait_ge(s_done, n + 1)
                dve.tensor_reduce(neg[:, :, :], psS[:, :, :, :], AX_X, ALU.max, negate=True).then_inc(neg_done, 1)

            def scale_values(n, c, rows, first):
                dve.wait_ge(exp_done, n + 1)
                dve.reciprocal(rinv[:, :, :], sums[:, :, :]).then_inc(rinv_done, 1)
                dve.wait_ge(rinv_done, n + 1)
                dve.wait_ge(ring_done, rows)
                dve.tensor_tensor(vs32[:, :, :, :], v32[:, :, c * P:c * P + P].rearrange("p t (j d) -> p t j d", j=2),
                                  rinv[:, :, :].unsqueeze(3).broadcast_to([P, GT, 2, DH]), ALU.mult).then_inc(vs32_done, 1)
                dve.wait_ge(vs32_done, n + 1)
                if not first:
                    dve.wait_ge(pv_done, n)
                dve.tensor_copy(vs[0][:, :, :, :], vs32[:, :, :, :]).then_inc(vhi_done, 1)
                dve.tensor_copy(probs[0][:, :, :, :], p32[:, :, :, :]).then_inc(phi_done, 1)
                dve.wait_ge(vhi_done, n + 1)
                dve.tensor_tensor(vs[1][:, :, :, :], vs32[:, :, :, :], vs[0][:, :, :, :].bitcast(F32),
                                  ALU.subtract).then_inc(vlo_done, 1)

            def out_lo(n):
                dve.wait_ge(ohi_done, 2 * n + 2)
                for j in range(2):
                    lanes = slice(DH * j, DH * j + DH)
                    ins = dve.tensor_tensor(oT[1][lanes, :, :], psV[lanes, :, P * j:P * j + P],
                                            oT[0][lanes, :, :].bitcast(F32), ALU.subtract)
                ins.then_inc(ot_done, 1)

            ln_stats(0, (0, None), x_in[0])
            dve.wait_ge(split_hi, 1)
            dve.tensor_tensor(w["wq"][1][:, :, :], raw["wq"][:, :, :], w["wq"][0][:, :, :].bitcast(F32),
                              ALU.subtract).then_inc(split_lo, 1)
            ln_apply(0, 0)
            dve.wait_ge(split_hi, 2)
            dve.tensor_tensor(ctxT[1][:, :, :], ctx_raw[:, :, :], ctxT[0][:, :, :].bitcast(F32),
                              ALU.subtract).then_inc(split_lo, 1)
            dve.wait_ge(split_hi, 3)
            dve.tensor_tensor(w["wk"][1][:, :, :], raw["wk"][:, :, :], w["wk"][0][:, :, :].bitcast(F32),
                              ALU.subtract).then_inc(split_lo, 1)
            dve.wait_ge(split_lo, 3)
            for kc in range(KC):
                ln_lo(kc, kc, 0)
            for t in range(GT):
                v_out(2 + t, t % 2, t, 0)
            for step in range(2):
                qk_lo("q", 2 + 2 * step, 0, step)
                qk_lo("k", 3 + 2 * step, 1, step)
            minus_max(0)
            dve.wait_ge(split_v, 4)
            scale_values(0, 0, 6, True)
            for g in range(1, GROUPS):
                dve.wait_ge(x_in[g], 16)
            dve.wait_ge(g_in, 17)
            with dve.Fori(0, GROUPS) as i:
                for s in range(CH):
                    n = CH * i + s + 1
                    J, H = JOBS0 + JOBS * i, HIS0 + HIS * i
                    minus_max(n)
                    if s in (2, 4):
                        for kc in range(KC):
                            ln_lo(H + his[s, "ln"] + kc, kc, (i + (3 if s == 2 else 1)) % GROUPS)
                    out_lo(n - 1)
                    v_out(J + jobs[s, "v"], jobs[s, "v"] % 2, s % GT, 1 - s // GT)
                    qk_lo("q", H + his[s, "q"], jobs[s, "q"] % 2, s % 2)
                    qk_lo("k", H + his[s, "k"], jobs[s, "k"] % 2, s % 2)
                    if s in (1, 3):
                        gx = (i + (3 if s == 1 else 1)) % GROUPS
                        ln_stats(2 * i + (1 if s == 1 else 2), (gx, i + 1), None)
                    scale_values(n, (s + 1) % CH, J + jobs[s, "v"] + 1, False)
                    if s in (1, 3):
                        ln_apply(2 * i + (1 if s == 1 else 2), gx)
                dve.wait_ge(o_done, CH * i + CH + 1)
                at = bass.ds(i * GT, GT)
                dve.scalar_tensor_tensor(x[:, at, :], psO[:, :, :], tg[:, 0:1], x[:, at, :],
                                         ALU.mult, ALU.add).then_inc(x_upd, 1)
            n = 2 * GROUPS + 1
            ln_stats(n, (GROUPS - 1, GROUPS + 1), None)
            ln_apply(n, GROUPS - 1)
            for kc in range(KC):
                ln_lo(HIS0 + HIS * GROUPS + kc, kc, GROUPS - 1)

        @block.tensor
        def _(pe):
            def ring_free(job, first=False):
                if not first:
                    pe.wait_ge(ring_done, job - 1)

            def ln_jobs(n, job, first=False):
                pe.wait_ge(xn_ready, GT * n + GT)
                for kc in range(KC):
                    ring_free(job + kc, first)
                    for t in range(GT):
                        mm = pe.transpose(ring[kc][:, t * P:t * P + P], xn32[:, t, kc * P:kc * P + P], ident[:, :])
                    mm.then_inc(job_done, 1)

            def v_job(job, bank, t, half):
                ring_free(job)
                product(pe, ring[bank][:, :], lambda a, k: stage[:, t, a, k, :],
                        lambda b, k: w["wv"][b][:, k, half * 512:half * 512 + 512], KC).then_inc(job_done, 1)

            def qk_job(which, job, bank, c, g):
                ring_free(job)
                src = xnT if which == "q" else ctxT
                wt = w["w" + which]
                product(pe, ring[bank][:, :], lambda a, k: wt[a][:, k, c * P:c * P + P],
                        lambda b, k: src[b][:, k, bass.ds(g * GW, GW)], KC).then_inc(job_done, 1)

            def scores(n, rows, buf, first):
                pe.wait_ge(ring_done, rows)
                if not first:
                    pe.wait_ge(exp_done, n)
                for b in range(GT):
                    for m, (ka, qb) in enumerate(PASSES):
                        for j in range(2):
                            lanes = slice(DH * j, DH * j + DH)
                            mm = pe.matmul(psS[:, j, b, :], kT[buf][ka][lanes, b * P:b * P + P],
                                           qT[buf][qb][lanes, b * P:b * P + P], start=m == 0, stop=m == 2)
                mm.then_inc(s_done, 1)

            def values(n):
                pe.wait_ge(vlo_done, n + 1)
                pe.wait_ge(plo_done, n + 1)
                pe.wait_ge(ot_done, n + 1)
                for b in range(GT):
                    for m, (a, q) in enumerate(PASSES):
                        mm = pe.matmul(psV[:, b, :], vs[a][:, b, :, :], probs[q][:, b, :, :], start=m == 0, stop=m == 2)
                mm.then_inc(pv_done, 1)

            def outs(n, c, free):
                pe.wait_ge(ot_done, n + 2)
                if c == 0:
                    pe.wait_ge(x_upd, free)
                for b in range(GT):
                    for m, (a, q) in enumerate(PASSES):
                        mm = pe.matmul(psO[:, b, :], oT[a][:, b, :], w["wo"][q][:, c, :],
                                       start=c == 0 and m == 0 and b % 2 == 0, stop=c == CH - 1 and m == 2,
                                       skip_group_check=True)
                mm.then_inc(o_done, 1)

            pe.wait_ge(ident_done, 3)
            ln_jobs(0, 0, True)
            pe.wait_ge(split_v, 2)
            pe.wait_ge(split_lo, 3)
            pe.wait_ge(staged, 2 * GT)
            for t in range(GT):
                v_job(2 + t, t % 2, t, 0)
            for step in range(2):
                qk_job("q", 6 + 2 * step, 0, step, 0)
                qk_job("k", 7 + 2 * step, 1, step, 0)
            scores(0, 8, 0, True)
            pe.wait_ge(split_v, 4)
            with pe.Fori(0, GROUPS) as i:
                for s in range(CH):
                    n = CH * i + s + 1
                    J = JOBS0 + JOBS * i
                    gq = i if s < CH - 2 else (i + 1) % GROUPS
                    scores(n, J + (jobs[s - 1, "k"] + 1 if s else 0), (s + 1) % 2, False)
                    if s in (2, 4):
                        ln_jobs(2 * i + (1 if s == 2 else 2), J + jobs[s, "ln"])
                    values(n - 1)
                    if s >= GT:
                        pe.wait_ge(staged, 2 * GT * (i + 1) + 2 * (s - GT + 1))
                    v_job(J + jobs[s, "v"], jobs[s, "v"] % 2, s % GT, 1 - s // GT)
                    qk_job("q", J + jobs[s, "q"], jobs[s, "q"] % 2, (s + 2) % CH, gq)
                    qk_job("k", J + jobs[s, "k"], jobs[s, "k"] % 2, (s + 2) % CH, gq)
                    outs(n - 1, s, i + 1)
            ln_jobs(2 * GROUPS + 1, JOBS0 + JOBS * GROUPS)


def stage_b(nc, dram, keep, region):
    x, xnT, ctxT, ident, tg = keep
    ITEMS = EG * GROUPS
    UP = KC * 2 * XD
    with ExitStack() as stack:
        sp_ = Space(nc, stack, "b")
        wraw = sp_.sb("wraw", [P, EG * (UP + D)])
        wsp = [sp_.pair(f"w{b}", [P, EG * (UP + D)]) for b in range(2)]
        graw = sp_.sb("graw", [P, KC, EXPERTS])
        gate = sp_.pair("gate", [P, KC, EXPERTS])
        neg = sp_.sb("neg", [P, TILES])
        lg = sp_.sb("lg", [P, TILES, EXPERTS])
        ex = sp_.sb("ex", [P, TILES, EXPERTS])
        top = sp_.sb("top", [P, TILES, TOPK])
        rest = lg
        total = sp_.sb("total", [P, TILES])
        inv = sp_.sb("inv", [P, TILES])
        comb = sp_.sb("comb", [P, TILES, EXPERTS])
        combT = sp_.sb("combT", [P, GROUPS, P])
        share = [sp_.sb(f"share{b}", [P, EG, GW]) for b in range(2)]
        silu = [sp_.sb(f"silu{b}", [P, GW]) for b in range(2)]
        weighted = sp_.sb("weighted", [P, GW])
        h32 = [sp_.sb(f"h32{b}", [P, GW]) for b in range(2)]
        h = [sp_.pair(f"h{b}", [P, GW]) for b in range(2)]
        later = carve(region, C_WEIGHTS)
        LATER = [n for n in C_WEIGHTS if n != "w1"]
        acc = region[:, 0:KC * TOK].rearrange("p (k t) -> p k t", k=KC)
        pad = sp_.sb("pad", [P, 4])
        psG = [sp_.ps(f"gate{b}", [P, GW]) for b in range(2)]
        psU = [sp_.ps(f"up{b}", [P, GW]) for b in range(2)]
        psY = [sp_.ps(f"down{b}", [P, KC, GW]) for b in range(2)]

        g_in, g_split, lg_done, r_done, ex_done, cT_ps, cT_done, cw_out, padded = sp_.sems(
            "g_in", "g_split", "lg_done", "r_done", "ex_done", "cT_ps", "cT_done", "cw_out", "padded")
        w_in, w_split, share_in0, share_in1, later_in = sp_.sems("w_in", "w_split", "share_in0", "share_in1", "later_in")
        share_in = [share_in0, share_in1]
        g_done, u_done, d_done, s_done, t_done, h_done, hhi_done, hlo_done, acc_done, yT_done, x_upd = sp_.sems(
            "g_done", "u_done", "d_done", "s_done", "t_done", "h_done", "hhi_done", "hlo_done", "acc_done", "yT_done", "x_upd")

        def up(buf, part, e, k, half):
            at = (e * KC + k) * 2 * XD + half * XD
            return wsp[buf][part][:, at:at + XD]

        def down(buf, part, e, c):
            at = EG * UP + e * D + c * P
            return wsp[buf][part][:, at:at + P]

        block = stack.enter_context(nc.Block())

        @block.sync
        def _(sp):
            def load_weights(eg):
                sp.dma_start(wraw[:, :], dram["moe"][eg, :, :]).then_inc(w_in, 16)

            def load_share(eg, tg_):
                rows = dram["shares"][bass.ds(eg * EG, EG), tg_ * GW:tg_ * GW + GW]
                sp.dma_start(share[tg_ % 2][:, :, :], rows.partition_broadcast(P)).then_inc(share_in[tg_ % 2], 16)

            load_weights(0)
            for n in LATER:
                sp.dma_start(later[n], dram[n]).then_inc(later_in, 16)
            sp.wait_ge(w_split, 2)
            load_weights(1)
            sp.wait_ge(cT_done, 1)
            for tt in range(GT):
                sp.dma_start(dram["shares"].rearrange("e (g t n) -> t e g n", t=GT, n=P)[tt, :, :, :],
                             combT[tt * EXPERTS:tt * EXPERTS + EXPERTS, :, :]).then_inc(cw_out, 16)
            sp.wait_ge(cw_out, 16 * GT)
            load_share(0, 0)
            load_share(0, 1)
            with sp.Fori(0, EGS) as eg:
                for t in range(GROUPS):
                    sp.wait_ge(t_done, ITEMS * eg + EG * (t + 1))
                    load_share((eg + (t + 2) // GROUPS) % EGS, (t + 2) % GROUPS)
                    if t == 1:
                        sp.wait_ge(w_split, 2 * eg + 4)
                        load_weights((eg + 2) % EGS)
            sp.wait_ge(later_in, 16 * len(LATER))
            sp.wait_ge(w_in, 16 * (EGS + 2))
            sp.wait_ge(share_in[0], 16 * (2 * EGS + 1))
            sp.wait_ge(share_in[1], 16 * (2 * EGS + 1))

        @block.gpsimd
        def _(pool):
            pool.memset(pad[:, 1:2], 0.0).then_inc(padded, 1)

            def split(n, buf):
                pool.tensor_copy(wsp[buf][0][:, :], wraw[:, :]).then_inc(w_split, 1)
                pool.wait_ge(w_split, 2 * n + 1)
                pool.tensor_tensor(wsp[buf][1][:, :], wraw[:, :], wsp[buf][0][:, :].bitcast(F32),
                                   ALU.subtract).then_inc(w_split, 1)

            for n in range(2):
                pool.wait_ge(w_in, 16 * (n + 1))
                split(n, n)
            with pool.Fori(0, EGS // 2 - 1) as p:
                for q in range(2):
                    n = 2 * p + q + 2
                    pool.wait_ge(d_done, ITEMS * (n - 1) + 1)
                    pool.wait_ge(w_in, 16 * n + 16)
                    pool.wait_ge(padded, n - 1)
                    pool.tensor_tensor(pad[:, 1:2], pad[:, 1:2], pad[:, 1:2], ALU.add).then_inc(padded, 1)
                    split(n, q)
            pool.wait_ge(w_split, 2 * EGS)
            pool.memset(pad[:, 2:3], 0.0).then_inc(w_split, 4)

        @block.scalar
        def _(act):
            act.dma_start(graw[:, :, :], dram["gate"]).then_inc(g_in, 16)
            act.wait_ge(ex_done, 1)
            act.activation(ex[:, :, :], lg[:, :, :], ACT.Exp).then_inc(ex_done, 1)

            def silus(n, buf):
                act.wait_ge(g_done, n + 1)
                act.activation(silu[buf][:, :], psG[buf][:, :], ACT.Silu).then_inc(s_done, 1)

            silus(0, 0)
            with act.Fori(0, EGS // 2) as p:
                for k in range(2 * ITEMS):
                    m = 2 * ITEMS * p + k
                    silus(m + 1, (k + 1) % 2)
                    act.wait_ge(h_done, m + 1)
                    act.activation(h[k % 2][0][:, :], h32[k % 2][:, :], ACT.Copy).then_inc(hhi_done, 1)

        @block.vector
        def _(dve):
            dve.memset(pad[:, 0:1], 0.0).then_inc(d_done, 1)
            dve.memset(psY[1][:, :, :], 0.0).then_inc(acc_done, 1)
            dve.memset(acc[:, :, :], 0.0).then_inc(acc_done, 1)
            dve.wait_ge(g_in, 16)
            dve.tensor_copy(gate[0][:, :, :], graw[:, :, :]).then_inc(g_split, 1)
            dve.wait_ge(g_split, 1)
            dve.tensor_tensor(gate[1][:, :, :], graw[:, :, :], gate[0][:, :, :].bitcast(F32),
                              ALU.subtract).then_inc(g_split, 1)
            logits = psG[0][:, :].rearrange("p (t e) -> p t e", e=EXPERTS)
            steps = [0]

            def chain(ins):
                steps[0] += 1
                ins.then_inc(r_done, 1)
                dve.wait_ge(r_done, steps[0])

            def wide(a, n=EXPERTS):
                return a.unsqueeze(2).broadcast_to([P, TILES, n])

            dve.wait_ge(lg_done, 1)
            chain(dve.tensor_reduce(neg[:, :], logits, AX_X, ALU.max, negate=True))
            dve.tensor_tensor(lg[:, :, :], logits, wide(neg[:, :]), ALU.add).then_inc(ex_done, 1)
            dve.wait_ge(ex_done, 2)
            for t in range(TILES):
                last = dve.max(top[:, t, :], ex[:, t, :])
            chain(last)
            for t in range(TILES):
                last = dve.match_replace(rest[:, t, :], top[:, t, :], ex[:, t, :], -1.0)
            chain(last)
            dve.tensor_reduce(total[:, :], top[:, :, :], AX_X, ALU.add)
            chain(dve.scalar_tensor_tensor(comb[:, :, :], rest[:, :, :], 0.0, ex[:, :, :], ALU.is_lt, ALU.mult))
            chain(dve.reciprocal(inv[:, :], total[:, :]))
            chain(dve.tensor_tensor(comb[:, :, :], comb[:, :, :], wide(inv[:, :]), ALU.mult))
            dve.wait_ge(cT_ps, 1)
            dve.tensor_copy(combT[:, :, :], psU[0][:, :].rearrange("p (g n) -> p g n", g=GROUPS)).then_inc(cT_done, 1)

            def add_up(t, buf):
                at = slice(t * GW, t * GW + GW)
                dve.tensor_tensor(acc[:, :, at], acc[:, :, at], psY[buf][:, :, :], ALU.add).then_inc(acc_done, 1)

            with dve.Fori(0, EGS // 2) as p:
                for k in range(2 * ITEMS):
                    m = 2 * ITEMS * p + k
                    e, t, b = k % EG, k // EG % GROUPS, k % 2
                    if e == 0:
                        dve.wait_ge(share_in[t % 2], 16 * (4 * p + k // (2 * EG) + 1))
                    dve.wait_ge(s_done, m + 1)
                    dve.tensor_tensor(weighted[:, :], silu[b][:, :], share[t % 2][:, e, :], ALU.mult).then_inc(t_done, 1)
                    dve.wait_ge(t_done, m + 1)
                    dve.wait_ge(u_done, m + 1)
                    dve.tensor_tensor(h32[b][:, :], weighted[:, :], psU[b][:, :], ALU.mult).then_inc(h_done, 1)
                    dve.wait_ge(hhi_done, m + 1)
                    dve.tensor_tensor(h[b][1][:, :], h32[b][:, :], h[b][0][:, :].bitcast(F32),
                                      ALU.subtract).then_inc(hlo_done, 1)
                    if e == 0:
                        dve.wait_ge(d_done, m + 1)
                        dve.wait_ge(acc_done, EGS * p + k // EG + 2)
                        add_up((t - 1) % GROUPS, (t - 1) % 2)
            n = ITEMS * EGS
            dve.wait_ge(d_done, n + 1)
            add_up(GROUPS - 1, 1)
            for g in range(GROUPS):
                dve.wait_ge(yT_done, g + 1)
                at = slice(g * GT, g * GT + GT)
                dve.scalar_tensor_tensor(x[:, at, :], psY[g % 2][:, :, :].rearrange("p k (t d) -> p (k t) d", d=D),
                                         tg[:, 2:3], x[:, at, :], ALU.mult, ALU.add).then_inc(x_upd, 1)

        @block.tensor
        def _(pe):
            pe.wait_ge(g_split, 2)
            for t in range(TILES):
                mm = product(pe, psG[0][:, t * EXPERTS:t * EXPERTS + EXPERTS],
                             lambda a, k: xnT[a][:, k, t * P:t * P + P], lambda b, k: gate[b][:, k, :], KC)
            mm.then_inc(lg_done, 1)
            pe.wait_ge(r_done, 6)
            for g in range(GROUPS):
                mm = pe.transpose(psU[0][:, g * P:g * P + P], comb[:, g * GT:g * GT + GT, :], ident[:, :])
            mm.then_inc(cT_ps, 1)
            pe.wait_ge(cT_done, 1)

            def gate_up(k, buf):
                e, t = k % EG, k // EG % GROUPS
                for half, out, sem in ((0, psG, g_done), (1, psU, u_done)):
                    product(pe, out[k % 2][:, :], lambda a, c: up(buf, a, e, c, half),
                            lambda b, c: xnT[b][:, c, t * GW:t * GW + GW], KC).then_inc(sem, 1)

            def down_products(k, m, tile):
                e, t, buf = k % EG, k // EG % GROUPS, k // ITEMS
                pe.wait_ge(hlo_done, m + 1)
                if e == 0:
                    pe.wait_ge(acc_done, tile + 2)
                for c in range(KC):
                    for n, (a, b) in enumerate(PASSES):
                        mm = pe.matmul(psY[t % 2][:, c, :], down(buf, a, e, c), h[k % 2][b][:, :],
                                       start=e == 0 and n == 0, stop=e == EG - 1 and n == 2)
                mm.then_inc(d_done, 1)

            pe.wait_ge(w_split, 2)
            gate_up(0, 0)
            with pe.Fori(0, EGS // 2) as p:
                for k in range(2 * ITEMS):
                    nxt = (k + 1) % (2 * ITEMS)
                    if nxt % ITEMS == 0:
                        pe.wait_ge(w_split, 4 * p + 2 * (k + 1) // ITEMS + 2)
                    gate_up(nxt, nxt // ITEMS)
                    down_products(k, 2 * ITEMS * p + k, 2 * EG * p + k // EG)
            for g in range(GROUPS):
                pe.wait_ge(acc_done, GROUPS * EGS + 3)
                if g >= 2:
                    pe.wait_ge(x_upd, g - 1)
                for t in range(GT):
                    for c in range(KC):
                        at = t * D + c * P
                        mm = pe.transpose(psY[g % 2][:, at // GW, at % GW:at % GW + P],
                                          acc[:, c, (g * GT + t) * P:(g * GT + t) * P + P], ident[:, :])
                mm.then_inc(yT_done, 1)


C_WEIGHTS = {"w1": (E1, KC * H1), "w2": (E1, HC1 * D), "aq": (KC, D), "ak": (KC, D), "av": (KC, D)}
C_WORK = {"z32": (GT, H1), "oacc": (GT, D), "out32": (GT, D), "xn32": (GT, D), "f32_0": (GW,), "f32_1": (GW,), "p32": (GT, P),
          "a32_0": (GW,), "a32_1": (GW,), "bv": (D,), "on_g": (D,), "on_b": (D,), "ln_g": (E1 * HC1,), "ln_b": (E1 * HC1,),
          "stats": (GT, 6), "mv": (GT, 2), "rstd": (GT,), "ve": (GT,), "neghalf": (GT,), "zs": (GT,), "mr": (GT,), "neg": (GT,), "sums": (GT,), "coef": (GT,),
          "g4": (GT, E1), "e4": (GT, E1), "rank": (GT, E1), "w4": (GT, E1), "z4": (GT,), "s4": (GT,),
          "below": (GT, E1, E1), "above": (GT, E1, E1), "ge": (GT, E1, E1), "gt": (GT, E1, E1)}

FIRST_JOBS = "K0 K1 V0 V1 N0 N1 Q0 Q1 S T0 T1 U0 U1 M0 M1".split()
LOOP_JOBS = ("K0 K1 R0 R1 t00 t01 L t02 t03  t10 t11 N0 N1 V0 Q0 t12 Q1 t13 V1  "
             "t20 t21 S T0 T1 t22 U0 t23 U1  t30 t31 t32 t33 M0 M1").split()
LAST_JOBS = [n for n in LOOP_JOBS if n[0] in "tRL"]


class Turns:

    COUNTED = {"job": "KVNQSTUMRLt", "out": "KVNQTMRL", "t": "t", "hi": "KVNQTMR", "lo": "KVQR", "S": "S", "U": "U"}

    def __init__(self, jobs, before):
        self.jobs, self.before = jobs, before

    def count(self, what, name):
        upto = self.jobs[:self.jobs.index(name) + 1]
        return self.before[what] + sum(n[0] in self.COUNTED[what] for n in upto)

    def parity(self, name):
        return (self.jobs.index(name) + (len(FIRST_JOBS) if self.jobs is not FIRST_JOBS else 0)) % 2

    def previous(self, name):
        k = self.jobs.index(name) - 2
        if k >= 0:
            kind = self.jobs[k][0]
            what = kind if kind in "tSU" else "out"
            return what, self.count(what, self.jobs[k]) * (2 if what == "U" else 1)
        return None if self.jobs is FIRST_JOBS else ("out", self.before["out"] + k + 1)


def turns(i):
    def number(what, jobs):
        return sum(n[0] in Turns.COUNTED[what] for n in jobs)

    if i is None:
        return Turns(FIRST_JOBS, {w: 0 for w in Turns.COUNTED})
    before = {w: number(w, LOOP_JOBS) * i + number(w, FIRST_JOBS) for w in Turns.COUNTED}
    return Turns(LAST_JOBS if isinstance(i, int) else LOOP_JOBS, before)


def stage_cd(nc, dram, keep, region):
    x, _, ctxT, ident, tg = keep
    LNS0, LNS = 4, 8
    with ExitStack() as stack:
        sp_ = Space(nc, stack, "c")
        raw, work = carve(region, C_WEIGHTS), carve(region, C_WORK)
        wt = {n: sp_.pair(n, [P, *s]) for n, s in C_WEIGHTS.items()}
        router = sp_.pair("router", [P, KC, E1])
        router_raw = sp_.sb("router_raw", [P, KC, E1])
        xn32, p32, z32, oacc, out32 = (work[n] for n in ("xn32", "p32", "z32", "oacc", "out32"))
        f32, a32 = ([work[f"{n}_{b}"] for b in range(2)] for n in ("f32", "a32"))
        nT = sp_.pair("nT", [P, KC, GW])
        rT = nT
        hT = sp_.pair("hT", [P, KC, GW])
        qT = sp_.pair("qT", [P, KC, GW])
        kT = sp_.pair("kT", [P, KC, GW])
        v = sp_.pair("v", [P, GT, D])
        stage = sp_.sb("stage", [P, GT, 2, KC, P], F32R)
        pT = sp_.pair("pT", [P, GT, P])
        a = [sp_.pair(f"a{b}", [P, GW]) for b in range(2)]
        vec = {n: sp_.sb(n, [P, KC]) for n in ("bq", "bk", "rn_g", "rn_b")}
        vec |= {n: work[n] for n in ("ln_g", "ln_b")}
        wide = {n: work[n] for n in ("bv", "on_g", "on_b")}
        pad = sp_.sb("pad", [P, 4])
        stats, mv, ve, neghalf, rstd, zs, mr, neg, sums, coef = (work[n] for n in ("stats", "mv", "ve", "neghalf", "rstd", "zs", "mr", "neg", "sums", "coef"))
        g4, e4, rank, w4, z4, s4 = (work[n] for n in ("g4", "e4", "rank", "w4", "z4", "s4"))
        below, above, ge, gt = (work[n] for n in ("below", "above", "ge", "gt"))

        ring = [sp_.ps(f"ring{b}", [P, GW]) for b in range(2)]
        hid = [sp_.ps(f"hid{t}", [P, H1]) for t in range(GT)]
        psY = sp_.ps("y", [P, GT, D])

        small = ("router", "bq", "bk", "rn_g", "rn_b")
        w1_in, small_in, wide_in, w1_hi, w1_lo = sp_.sems("w1_in", "small_in", "wide_in", "w1_hi", "w1_lo")
        EARLY = ("aq", "ak", "av", "w2")
        w_hi, w_lo, masks, staged, job_done, act_hi, ring_done, lo_done = sp_.sems(
            "w_hi", "w_lo", "masks", "staged", "job_done", "act_hi", "ring_done", "lo_done")
        held, st_done, mv_done, ve_done, rstd_done, xn_ready = sp_.sems("held", "st_done", "mv_done", "ve_done", "rstd_done", "xn_ready")
        neg_done, exp_done, coef_done, x_c = sp_.sems("neg_done", "exp_done", "coef_done", "x_c")
        e4_done, w4_done = sp_.sems("e4_done", "w4_done")
        hid_done, mr_done, z_done, ahi_done, alo_done, y_done, y_sum = sp_.sems(
            "hid_done", "mr_done", "z_done", "ahi_done", "alo_done", "y_done", "y_sum")
        o_step, out_done = sp_.sems("o_step", "out_done")
        out_of = {"out": ring_done, "t": ahi_done, "S": exp_done, "U": x_c}
        MASKS = 3 + 2 * (E1 - 1)

        def of_bank(r, name):
            return ring[r.parity(name)]

        block = stack.enter_context(nc.Block())

        @block.sync
        def _(sp):
            sp.dma_start(raw["w1"], dram["w1"]).then_inc(w1_in, 16)
            for n in small:
                dst = router_raw[:, :, :] if n == "router" else vec[n][:, :]
                sp.dma_start(dst, dram[n]).then_inc(small_in, 16)
            sp.wait_ge(w_lo, len(EARLY) + 1)
            for n in wide:
                sp.dma_start(wide[n], dram[n].partition_broadcast(P)).then_inc(wide_in, 16)
            for n in ("ln_g", "ln_b"):
                sp.dma_start(vec[n], dram[n]).then_inc(wide_in, 16)
            with sp.Fori(0, GROUPS) as i:
                sp.wait_ge(o_step, 7 * i + 7)
                sp.dma_start(dram["out"].rearrange("(g t) p d -> g p t d", t=GT)[i, :, :, :], out32).then_inc(out_done, 16)
            sp.wait_ge(out_done, 16 * GROUPS + 1)

        @block.gpsimd
        def _(pool):
            pool.memset(pad[:, 0:1], 0.0).then_inc(out_done, 1)
            pool.wait_ge(w_lo, len(EARLY) + 1)
            pool.memset(below[:, :, :, :], 0.0).then_inc(masks, 1)
            pool.memset(above[:, :, :, :], 0.0).then_inc(masks, 1)
            pool.memset(neghalf, -0.5).then_inc(masks, 1)
            pool.wait_ge(masks, 3)
            for e in range(E1):
                if e:
                    pool.memset(below[:, :, e, 0:e], 1.0).then_inc(masks, 1)
                if e < E1 - 1:
                    pool.memset(above[:, :, e, e + 1:E1], 1.0).then_inc(masks, 1)

            def stage_tiles(g, tiles=range(GT)):
                for t in tiles:
                    for part in range(2):
                        pool.tensor_copy(stage[:, t, part, :, :], ctxT[part][:, :, bass.ds(g * GW + t * P, P)].bitcast(F32)
                                         ).then_inc(staged, 1)

            def rsqrt(n, dst=rstd):
                pool.wait_ge(ve_done, n + 1)
                pool.tensor_tensor(dst, ve, neghalf, ALU.pow).then_inc(rstd_done, 1)

            stage_tiles(0)
            rsqrt(0)
            pool.wait_ge(job_done, turns(None).count("job", "V1"))
            stage_tiles(1)
            rsqrt(1)
            rsqrt(2)
            rsqrt(3, zs)
            with pool.Fori(0, GROUPS - 1) as i:
                n = LNS * i + LNS0
                rsqrt(n, zs)
                rsqrt(n + 1)
                rsqrt(n + 2, zs)
                pool.wait_ge(job_done, turns(i).count("job", "V1"))
                stage_tiles((i + 2) % GROUPS, (0, 1))
                rsqrt(n + 3, zs)
                stage_tiles((i + 2) % GROUPS, (2,))
                rsqrt(n + 4)
                stage_tiles((i + 2) % GROUPS, (3,))
                rsqrt(n + 5)
                rsqrt(n + 6, zs)
                rsqrt(n + 7)
            n = LNS * (GROUPS - 1) + LNS0
            for e in range(1, E1):
                rsqrt(n + e - 1, zs)
            rsqrt(n + E1 - 1)

        @block.scalar
        def _(act):
            for n in EARLY:
                act.activation(wt[n][0][:, :, :], raw[n], ACT.Copy).then_inc(w_hi, 1)
            act.wait_ge(small_in, 16 * len(small))
            act.activation(router[0][:, :, :], router_raw[:, :, :], ACT.Copy).then_inc(w_hi, 1)
            act.wait_ge(w_lo, len(EARLY) + 1)

            def hi(r, name, dst):
                if name[0] in "KVQR":
                    act.wait_ge(ring_done, r.count("out", name))
                    src = f32[int(name[1])]
                else:
                    act.wait_ge(job_done, r.count("job", name))
                    src = of_bank(r, name)[:, 0:(2 * P if name[0] == "T" else GW)]
                if name[0] in "VT":
                    src = src.rearrange("p (t n) -> p t n", t=2)
                act.activation(dst, src, ACT.Copy).then_inc(act_hi, 1)

            def pairs(r, *names):
                for name in names:
                    c = int(name[1])
                    two = slice(2 * c, 2 * c + 2)
                    hi(r, name, {"K": kT[0][:, c, :], "N": nT[0][:, c, :], "Q": qT[0][:, c, :], "M": hT[0][:, c, :],
                                 "R": rT[0][:, c, :], "V": v[0][:, two, :], "T": pT[0][:, two, :]}[name[0]])

            def exps(r, n):
                act.wait_ge(neg_done, n + 1)
                for b in range(GT):
                    ins = act.activation(p32[:, b, :], of_bank(r, "S")[:, b * P:b * P + P], ACT.Exp, bias=neg[:, b:b + 1],
                                         accum_out=sums[:, b:b + 1])
                ins.then_inc(exp_done, 1)

            def normalise(n, turned):
                act.wait_ge(mr_done, n + 1)
                if turned is not None:
                    act.wait_ge(job_done, turned)
                for t in range(GT):
                    ins = act.activation(z32[:, t, :], hid[t][:, :], ACT.Identity, scale=zs[:, t:t + 1], bias=mr[:, t:t + 1])
                ins.then_inc(z_done, 1)

            def relu(r, e, c):
                k = e * HC1 + c
                act.wait_ge(job_done, r.count("job", f"t{e}{c}"))
                src = of_bank(r, f"t{e}{c}")[:, :]
                act.activation(a32[c % 2], src, ACT.Relu, scale=vec["ln_g"][:, k:k + 1], bias=vec["ln_b"][:, k:k + 1])
                act.activation(a[c % 2][0][:, :], src, ACT.Relu, scale=vec["ln_g"][:, k:k + 1],
                               bias=vec["ln_b"][:, k:k + 1]).then_inc(ahi_done, 1)

            def round_(i, last):
                r = turns(i)
                go = () if last else (r,)
                for _ in go:
                    pairs(r, "K0", "K1")
                pairs(r, "R0", "R1")
                relu(r, 0, 0)
                relu(r, 0, 1)
                act.wait_ge(ring_done, r.count("out", "L"))
                act.activation(e4[:, :, :], g4[:, :, :], ACT.Exp).then_inc(e4_done, 1)
                relu(r, 0, 2)
                relu(r, 0, 3)
                normalise(E1 * i + 1, r.count("job", "t03"))
                relu(r, 1, 0)
                relu(r, 1, 1)
                for _ in go:
                    pairs(r, "N0", "N1", "V0", "Q0")
                relu(r, 1, 2)
                for _ in go:
                    pairs(r, "Q1")
                relu(r, 1, 3)
                normalise(E1 * i + 2, r.count("job", "t13"))
                for _ in go:
                    pairs(r, "V1")
                relu(r, 2, 0)
                relu(r, 2, 1)
                for _ in go:
                    exps(r, i + 1)
                    pairs(r, "T0", "T1")
                relu(r, 2, 2)
                relu(r, 2, 3)
                normalise(E1 * i + 3, r.count("job", "t23"))
                for c in range(HC1):
                    relu(r, 3, c)
                for _ in go:
                    pairs(r, "M0", "M1")
                    normalise(E1 * i + 4, r.count("job", "t33"))

            r = turns(None)
            pairs(r, "K0", "K1", "V0", "V1", "N0", "N1", "Q0", "Q1")
            act.wait_ge(w1_in, 16)
            act.activation(wt["w1"][0][:, :, :], raw["w1"], ACT.Copy).then_inc(w1_hi, 1)
            exps(r, 0)
            pairs(r, "T0", "T1", "M0", "M1")
            normalise(0, None)
            with act.Fori(0, GROUPS - 1) as i:
                round_(i, False)
            round_(GROUPS - 1, True)

        @block.vector
        def _(dve):
            dve.memset(pad[:, 1:2], 0.0).then_inc(held, 1)
            for k, n in enumerate(EARLY):
                dve.wait_ge(w_hi, k + 1)
                dve.tensor_tensor(wt[n][1][:, :, :], raw[n], wt[n][0][:, :, :].bitcast(F32), ALU.subtract).then_inc(w_lo, 1)
            dve.wait_ge(w_hi, len(EARLY) + 1)
            dve.tensor_tensor(router[1][:, :, :], router_raw[:, :, :], router[0][:, :, :].bitcast(F32),
                              ALU.subtract).then_inc(w_lo, 1)
            dve.wait_ge(w_lo, len(EARLY) + 1)
            dve.wait_ge(wide_in, 16 * (len(wide) + 2))
            dve.wait_ge(masks, MASKS)

            held_now = [0]

            def carry(base, sem, value):
                held_now[0] += 1
                dve.wait_ge(held, base + held_now[0])
                dve.wait_ge(sem, value)
                dve.memset(pad[:, 1:2], 0.0).then_inc(held, 1)

            def moments(n, base, src):
                for t in range(GT):
                    src_t, sem, value = src(t)
                    if sem is not None:
                        dve.wait_ge(sem, value)
                    dve.bn_stats(stats[:, t, :], src_t).then_inc(st_done, 1)
                carry(base, st_done, GT * n + GT)
                for t in range(GT):
                    dve.bn_aggr(mv[:, t, :], stats[:, t, :]).then_inc(mv_done, 1)
                dve.wait_ge(mv_done, GT * n + GT)

            def spread(n):
                dve.tensor_scalar(ve, mv[:, :, 1], EPS_LN, None, ALU.add).then_inc(ve_done, 1)
                dve.wait_ge(rstd_done, n + 1)

            def ln_apply(dst, src, sem):
                for t in range(GT):
                    dve.tensor_scalar(dst[:, t, :], src(t), mv[:, t, 0:1], rstd[:, t:t + 1],
                                      ALU.subtract, ALU.mult).then_inc(sem, 1)

            def norm_x(n, base, g):
                moments(n, base, lambda t: (x[:, g * GT + t, :], None, None))
                spread(n)
                ln_apply(xn32, lambda t: x[:, g * GT + t, :], xn_ready)

            def norm_h(n, base, ready):
                carry(base, xn_ready, ready)
                moments(n, base, lambda t: (xn32[:, t, :], None, None))
                spread(n)
                ln_apply(xn32, lambda t: xn32[:, t, :], xn_ready)

            def norm_hidden(n, base, expert):
                moments(n, base, lambda t: (hid[t][:, :], hid_done, GT * expert + t + 1))
                spread(n)
                dve.scalar_tensor_tensor(mr[:, :], mv[:, :, 0], -1.0, zs[:, :], ALU.mult, ALU.mult).then_inc(mr_done, 1)

            def full(r, *names):
                for k, name in enumerate(names):
                    c = int(name[1])
                    src, dst = of_bank(r, name)[:, :], f32[c]
                    if r.jobs is not FIRST_JOBS or name[0] != "K":
                        dve.wait_ge(lo_done, r.count("lo", name) - 1 - k)
                    dve.wait_ge(job_done, r.count("job", name))
                    if name[0] == "V":
                        ins = dve.tensor_tensor(dst.rearrange("p (t n) -> p t n", t=2), src.rearrange("p (t n) -> p t n", t=2),
                                                wide["bv"].unsqueeze(1).broadcast_to([P, 2, D]), ALU.add)
                    elif name[0] == "K":
                        ins = dve.tensor_scalar(dst, src, vec["bk"][:, c:c + 1], None, ALU.add)
                    elif name[0] == "Q":
                        ins = dve.tensor_scalar(dst, src, vec["bq"][:, c:c + 1], D ** -0.5, ALU.add, ALU.mult)
                    else:
                        ins = dve.tensor_scalar(dst, src, vec["rn_g"][:, c:c + 1], vec["rn_b"][:, c:c + 1],
                                                ALU.mult, ALU.add)
                    ins.then_inc(ring_done, 1)

            def lower(r, *names):
                for name in names:
                    c = int(name[1])
                    two = slice(2 * c, 2 * c + 2)
                    dst = {"K": kT, "N": nT, "Q": qT, "M": hT, "R": rT, "V": v, "T": pT}[name[0]]
                    up, low = (d[:, two, :] if name[0] in "VT" else d[:, c, :] for d in dst)
                    dve.wait_ge(act_hi, r.count("hi", name))
                    if name[0] in "KVQR":
                        src, sem = f32[c], lo_done
                    else:
                        src, sem = of_bank(r, name)[:, 0:(2 * P if name[0] == "T" else GW)], ring_done
                    if name[0] in "VT":
                        src = src.rearrange("p (t n) -> p t n", t=2)
                    dve.tensor_tensor(low, src, up.bitcast(F32), ALU.subtract).then_inc(sem, 1)

            def minus_max(r):
                dve.wait_ge(job_done, r.count("job", "S"))
                dve.tensor_reduce(neg[:, :], of_bank(r, "S")[:, :].rearrange("p (t n) -> p t n", t=GT), AX_X, ALU.max,
                                  negate=True).then_inc(neg_done, 1)

            def coefficients(n):
                dve.wait_ge(exp_done, n + 1)
                dve.reciprocal(coef[:, :], sums[:, :]).then_inc(coef_done, 1)
                dve.wait_ge(coef_done, 2 * n + 1)
                dve.tensor_scalar(coef[:, :], coef[:, :], tg[:, 1:2], None, ALU.mult).then_inc(coef_done, 1)
                dve.wait_ge(coef_done, 2 * n + 2)

            def add_attention(r, g, part):
                dve.wait_ge(job_done, r.count("job", f"U{part}"))
                for b in range(2):
                    at = g * GT + 2 * part + b
                    dve.scalar_tensor_tensor(x[:, at, :], of_bank(r, f"U{part}")[:, b * D:b * D + D],
                                             coef[:, 2 * part + b:2 * part + b + 1], x[:, at, :], ALU.mult, ALU.add).then_inc(x_c, 1)

            def gates(r, i):
                steps = [0]
                CHAIN = 15

                def chain(ins):
                    steps[0] += 1
                    ins.then_inc(w4_done, 1)
                    dve.wait_ge(w4_done, CHAIN * i + steps[0])

                def over(ap):
                    return ap[:, :].unsqueeze(2).broadcast_to([P, GT, E1])

                logits = of_bank(r, "L")[:, 0:GT * E1].rearrange("p (t e) -> p t e", e=E1)
                dve.wait_ge(job_done, r.count("job", "L"))
                chain(dve.tensor_reduce(s4[:, :], logits, AX_X, ALU.max, negate=True))
                dve.tensor_tensor(g4[:, :, :], logits, over(s4), ALU.add).then_inc(ring_done, 1)
                dve.wait_ge(e4_done, i + 1)
                chain(dve.tensor_reduce(z4[:, :], e4[:, :, :], AX_X, ALU.add))
                chain(dve.reciprocal(s4[:, :], z4[:, :]))
                chain(dve.tensor_tensor(e4[:, :, :], e4[:, :, :], over(s4), ALU.mult))
                mine = e4[:, :, :].unsqueeze(3).broadcast_to([P, GT, E1, E1])
                other = e4[:, :, :].unsqueeze(2).broadcast_to([P, GT, E1, E1])
                chain(dve.tensor_tensor(ge[:, :, :, :], other, mine, ALU.is_ge))
                chain(dve.tensor_tensor(ge[:, :, :, :], ge[:, :, :, :], below[:, :, :, :], ALU.mult))
                chain(dve.tensor_tensor(gt[:, :, :, :], other, mine, ALU.is_gt))
                chain(dve.tensor_tensor(gt[:, :, :, :], gt[:, :, :, :], above[:, :, :, :], ALU.mult))
                chain(dve.tensor_tensor(ge[:, :, :, :], ge[:, :, :, :], gt[:, :, :, :], ALU.add))
                chain(dve.tensor_reduce(rank[:, :, :], ge[:, :, :, :], AX_X, ALU.add))
                chain(dve.scalar_tensor_tensor(w4[:, :, :], rank[:, :, :], 1.5, e4[:, :, :], ALU.is_lt, ALU.mult))
                chain(dve.tensor_reduce(z4[:, :], w4[:, :, :], AX_X, ALU.add))
                chain(dve.tensor_scalar(z4[:, :], z4[:, :], EPS_GATE, None, ALU.add))
                chain(dve.reciprocal(s4[:, :], z4[:, :]))
                chain(dve.tensor_tensor(w4[:, :, :], w4[:, :, :], over(s4), ALU.mult))
                assert steps[0] == CHAIN

            def a_lo(i, e, c):
                dve.wait_ge(ahi_done, HC1 * (E1 * i + e) + c + 1)
                dve.tensor_tensor(a[c % 2][1][:, :], a32[c % 2], a[c % 2][0][:, :].bitcast(F32), ALU.subtract).then_inc(alo_done, 1)

            def add_expert(i, e):
                n = E1 * i + e
                dve.wait_ge(y_done, n + 1)
                if e:
                    dve.wait_ge(y_sum, GT * n)
                for t in range(GT):
                    if e == 0:
                        dve.tensor_scalar(oacc[:, t, :], psY[:, t, :], w4[:, t, e:e + 1], None, ALU.mult).then_inc(y_sum, 1)
                    else:
                        dve.scalar_tensor_tensor(oacc[:, t, :], psY[:, t, :], w4[:, t, e:e + 1], oacc[:, t, :],
                                                 ALU.mult, ALU.add).then_inc(y_sum, 1)

            def output(n, base, i):
                carry(base, y_sum, GT * E1 * (i + 1))
                moments(n, base, lambda t: (oacc[:, t, :], None, None))
                spread(n)
                dve.wait_ge(out_done, 16 * i + 1)
                ln_apply(out32, lambda t: oacc[:, t, :], o_step)
                dve.wait_ge(o_step, 7 * i + GT)
                dve.tensor_tensor(out32, out32, wide["on_g"].unsqueeze(1).broadcast_to([P, GT, D]), ALU.mult).then_inc(o_step, 1)
                dve.wait_ge(o_step, 7 * i + GT + 1)
                dve.tensor_tensor(out32, out32, wide["on_b"].unsqueeze(1).broadcast_to([P, GT, D]), ALU.add).then_inc(o_step, 1)
                dve.wait_ge(o_step, 7 * i + GT + 2)
                dve.scalar_tensor_tensor(out32, out32, tg[:, 3:4], x[:, bass.ds(i * GT, GT), :],
                                         ALU.mult, ALU.add).then_inc(o_step, 1)

            HELD0, HELD = 6, 11

            def round_(i, last):
                r = turns(i)
                n, base = LNS * i + LNS0, HELD * i + HELD0
                go = () if last else (r,)
                held_now[0] = 0
                for _ in go:
                    full(r, "K0", "K1")
                    lower(r, "K0", "K1")
                full(r, "R0", "R1")
                lower(r, "R0", "R1")
                a_lo(i, 0, 0)
                a_lo(i, 0, 1)
                gates(r, i)
                norm_hidden(n, base, E1 * i + 1)
                a_lo(i, 0, 2)
                a_lo(i, 0, 3)
                for _ in go:
                    norm_x(n + 1, base, i + 1)
                add_expert(i, 0)
                a_lo(i, 1, 0)
                a_lo(i, 1, 1)
                for _ in go:
                    lower(r, "N0", "N1")
                    full(r, "V0")
                    lower(r, "V0")
                norm_hidden(n + (1 if last else 2), base, E1 * i + 2)
                for _ in go:
                    full(r, "Q0")
                    lower(r, "Q0")
                a_lo(i, 1, 2)
                for _ in go:
                    full(r, "Q1")
                    lower(r, "Q1")
                a_lo(i, 1, 3)
                for _ in go:
                    full(r, "V1")
                    lower(r, "V1")
                add_expert(i, 1)
                a_lo(i, 2, 0)
                a_lo(i, 2, 1)
                for _ in go:
                    minus_max(r)
                norm_hidden(n + (2 if last else 3), base, E1 * i + 3)
                for _ in go:
                    lower(r, "T0", "T1")
                    coefficients(i + 1)
                a_lo(i, 2, 2)
                for _ in go:
                    add_attention(r, i + 1, 0)
                a_lo(i, 2, 3)
                for _ in go:
                    add_attention(r, i + 1, 1)
                add_expert(i, 2)
                for _ in go:
                    carry(base, x_c, GT * (i + 2))
                    norm_x(n + 4, base, i + 1)
                for c in range(HC1):
                    a_lo(i, 3, c)
                for _ in go:
                    lower(r, "M0", "M1")
                    norm_h(n + 5, base, 12 * i + 20)
                add_expert(i, 3)
                for _ in go:
                    norm_hidden(n + 6, base, E1 * i + 4)
                output(n + (3 if last else 7), base, i)
                assert last or held_now[0] == HELD

            r = turns(None)
            full(r, "K0", "K1")
            lower(r, "K0", "K1")
            full(r, "V0", "V1")
            lower(r, "V0", "V1")
            norm_x(0, 0, 0)
            lower(r, "N0", "N1")
            full(r, "Q0", "Q1")
            lower(r, "Q0", "Q1")
            minus_max(r)
            dve.wait_ge(w1_hi, 1)
            dve.tensor_tensor(wt["w1"][1][:, :, :], raw["w1"], wt["w1"][0][:, :, :].bitcast(F32), ALU.subtract).then_inc(w1_lo, 1)
            lower(r, "T0", "T1")
            coefficients(0)
            add_attention(r, 0, 0)
            add_attention(r, 0, 1)
            carry(0, x_c, GT)
            norm_x(1, 0, 0)
            lower(r, "M0", "M1")
            norm_h(2, 0, 2 * GT)
            norm_hidden(3, 0, 0)
            assert held_now[0] == HELD0
            with dve.Fori(0, GROUPS - 1) as i:
                round_(i, False)
            round_(GROUPS - 1, True)

        @block.tensor
        def _(pe):
            pe.wait_ge(w_lo, len(EARLY) + 1)
            pe.wait_ge(staged, 2 * GT)

            def turn(r, name):
                before = r.previous(name)
                if before is not None:
                    pe.wait_ge(out_of[before[0]], before[1])
                return of_bank(r, name)

            def transposed(r, name, src, c):
                bank = turn(r, name)
                for t in range(GT):
                    mm = pe.transpose(bank[:, t * P:t * P + P], src[:, t, c * P:c * P + P], ident[:, :])
                mm.then_inc(job_done, 1)

            def job(r, name, g=None, ready=None):
                kind = name[0]
                if kind in "NMR":
                    pe.wait_ge(xn_ready, ready)
                    transposed(r, name, xn32, int(name[1]))
                    return
                bank = turn(r, name)
                c = int(name[1]) if len(name) > 1 else None
                if kind == "K":
                    mm = product(pe, bank[:, :], lambda p, k: wt["ak"][p][:, k, c * P:c * P + P],
                                 lambda p, k: ctxT[p][:, k, bass.ds(g * GW, GW)], KC)
                elif kind == "Q":
                    pe.wait_ge(ring_done, r.count("out", "N1"))
                    mm = product(pe, bank[:, :], lambda p, k: wt["aq"][p][:, k, c * P:c * P + P],
                                 lambda p, k: nT[p][:, k, :], KC)
                elif kind == "V":
                    for b in range(2):
                        mm = product(pe, bank[:, b * D:b * D + D], lambda p, k: stage[:, 2 * c + b, p, k, :],
                                     lambda p, k: wt["av"][p][:, k, :], KC)
                elif kind == "S":
                    pe.wait_ge(lo_done, r.count("lo", "Q1"))
                    for b in range(GT):
                        at = slice(b * P, b * P + P)
                        mm = product(pe, bank[:, at], lambda p, k: qT[p][:, k, at], lambda p, k: kT[p][:, k, at], KC)
                elif kind == "T":
                    pe.wait_ge(exp_done, r.count("S", "S"))
                    for b in range(2):
                        mm = pe.transpose(bank[:, b * P:b * P + P], p32[:, 2 * c + b, :], ident[:, :])
                elif kind == "U":
                    pe.wait_ge(ring_done, r.count("out", f"T{c}"))
                    if c == 1:
                        pe.wait_ge(lo_done, r.count("lo", "V1"))
                    for b in range(2):
                        mm = product(pe, bank[:, b * D:b * D + D], lambda p, k: pT[p][:, 2 * c + b, :],
                                     lambda p, k: v[p][:, 2 * c + b, :], 1)
                elif kind == "L":
                    pe.wait_ge(lo_done, r.count("lo", "R1"))
                    for t in range(GT):
                        mm = product(pe, bank[:, t * E1:t * E1 + E1], lambda p, k: rT[p][:, k, t * P:t * P + P],
                                     lambda p, k: router[p][:, k, :], KC)
                mm.then_inc(job_done, 1)

            def hidden(e, tiles):
                for t in tiles:
                    product(pe, hid[t][:, :], lambda p, k: hT[p][:, k, t * P:t * P + P],
                            lambda p, k: wt["w1"][p][:, e, k * H1:k * H1 + H1], KC).then_inc(hid_done, 1)

            def second(i, e, c):
                pe.wait_ge(alo_done, HC1 * (E1 * i + e) + c + 1)
                if c == 0 and e:
                    pe.wait_ge(y_sum, GT * (E1 * i + e))
                for t in range(GT):
                    for n, (p, q) in enumerate(PASSES):
                        mm = pe.matmul(psY[:, t, :], a[c % 2][p][:, t * P:t * P + P], wt["w2"][q][:, e, c * D:c * D + D],
                                       start=c == 0 and n == 0 and t % 2 == 0, stop=c == HC1 - 1 and n == 2,
                                       skip_group_check=True)
                if c == HC1 - 1:
                    mm.then_inc(y_done, 1)

            def round_(i, last):
                r = turns(i)

                def jobs(*names, **more):
                    if not last:
                        for name in names:
                            job(r, name, **more)

                def turned(e, c):
                    transposed(r, f"t{e}{c}", z32, c)

                def z_ready(e):
                    pe.wait_ge(z_done, E1 * i + e + 1)

                jobs("K0", "K1", g=i + 1)
                for name in ("R0", "R1"):
                    job(r, name, ready=12 * i + 12)
                z_ready(0)
                turned(0, 0)
                turned(0, 1)
                hidden(1, (0, 1))
                job(r, "L")
                hidden(1, (2, 3))
                second(i, 0, 0)
                turned(0, 2)
                second(i, 0, 1)
                turned(0, 3)
                second(i, 0, 2)
                second(i, 0, 3)
                z_ready(1)
                turned(1, 0)
                turned(1, 1)
                jobs("N0", "N1", ready=12 * i + 16)
                hidden(2, (0, 1))
                if not last:
                    pe.wait_ge(staged, 2 * GT * (i + 2))
                jobs("V0")
                hidden(2, (2, 3))
                jobs("Q0")
                second(i, 1, 0)
                turned(1, 2)
                jobs("Q1")
                second(i, 1, 1)
                turned(1, 3)
                second(i, 1, 2)
                second(i, 1, 3)
                jobs("V1")
                z_ready(2)
                turned(2, 0)
                turned(2, 1)
                jobs("S")
                hidden(3, range(GT))
                jobs("T0", "T1")
                second(i, 2, 0)
                turned(2, 2)
                jobs("U0")
                second(i, 2, 1)
                turned(2, 3)
                jobs("U1")
                second(i, 2, 2)
                second(i, 2, 3)
                z_ready(3)
                turned(3, 0)
                turned(3, 1)
                second(i, 3, 0)
                turned(3, 2)
                second(i, 3, 1)
                turned(3, 3)
                second(i, 3, 2)
                jobs("M0", "M1", ready=12 * i + 20)
                second(i, 3, 3)
                if not last:
                    pe.wait_ge(ring_done, r.count("out", "M1"))
                    hidden(0, range(GT))

            r = turns(None)
            for name in ("K0", "K1"):
                job(r, name, g=0)
            job(r, "V0")
            job(r, "V1")
            for name in ("N0", "N1"):
                job(r, name, ready=GT)
            for name in ("Q0", "Q1", "S", "T0", "T1", "U0", "U1"):
                job(r, name)
            for name in ("M0", "M1"):
                job(r, name, ready=2 * GT)
            pe.wait_ge(ring_done, r.count("out", "M1"))
            pe.wait_ge(w1_lo, 1)
            hidden(0, range(GT))
            with pe.Fori(0, GROUPS - 1) as i:
                round_(i, False)
            round_(GROUPS - 1, True)


def program(nc, dram):
    with ExitStack() as stack:
        keep = Space(nc, stack, "all")
        x = keep.sb("x", [P, TILES, D])
        ctxT = keep.pair("ctxT", [P, KC, TOK])
        ident = keep.sb("ident", [P, P])
        tg = keep.sb("tg", [P, 4])
        region = keep.sb("region", [P, sum(a * b for a, b in C_WEIGHTS.values())])
        with ExitStack() as first:
            xnT = Space(nc, first, "ab").pair("xnT", [P, KC, TOK])
            stage_a(nc, dram, (x, xnT, ctxT, ident, tg), region)
            stage_b(nc, dram, (x, xnT, ctxT, ident, tg), region)
        stage_cd(nc, dram, (x, None, ctxT, ident, tg), region)


def kernel(**inputs):
    import numpy as np
    import concourse.bacc as bacc
    from concourse.bass_utils import run_bass_kernel_spmd

    def rows(a):
        a = np.asarray(a)
        return a.reshape(-1, P, *a.shape[1:]).swapaxes(0, 1)

    x, ctx = (np.asarray(inputs[n]).reshape(TOK, D) for n in ("x", "ctx_1024"))
    laid = {
        "x": rows(x),
        "ctxT": rows(ctx.T),
        "g": np.concatenate([inputs["g_xattn"], inputs["g_ffn"]]),
        "wq": rows(inputs["L0_xattn_W_Q"]),
        "wk": rows(inputs["L0_xattn_W_K"]),
        "wv": rows(inputs["L0_xattn_W_V"]),
        "wo": rows(inputs["L0_xattn_W_O"]),
    }
    gu = inputs["L0_ffn_gate_up_w"].reshape(EGS, EG, 2 * XD, KC, P).transpose(0, 4, 1, 3, 2)
    dn = inputs["L0_ffn_down_w"].reshape(EGS, EG, D, XD).transpose(0, 3, 1, 2)
    laid["moe"] = np.concatenate([gu.reshape(EGS, P, -1), dn.reshape(EGS, P, -1)], axis=2)
    laid["gate"] = rows(inputs["L0_ffn_gate_w"].T)
    for short, name in (("aq", "Wq"), ("ak", "Wk"), ("av", "Wv")):
        laid[short] = rows(inputs["L1_xattn_" + name].T)
    laid["router"] = rows(inputs["L1_ffn_router_w"].T)
    laid["w1"] = inputs["L1_ffn_w1"].reshape(E1, KC, P, H1).transpose(2, 0, 1, 3).reshape(P, E1, KC * H1)
    laid["w2"] = inputs["L1_ffn_w2"].reshape(E1, HC1, P, D).transpose(2, 0, 1, 3).reshape(P, E1, HC1 * D)
    for short, name in (("bq", "xattn_bq"), ("bk", "xattn_bk"), ("rn_g", "ffn_rn_g"), ("rn_b", "ffn_rn_b")):
        laid[short] = rows(inputs["L1_" + name])
    for short in ("ln_g", "ln_b"):
        laid[short] = inputs["L1_ffn_" + short].reshape(E1, HC1, P).transpose(2, 0, 1).reshape(P, E1 * HC1)
    for short, name in (("bv", "xattn_bv"), ("on_g", "ffn_on_g"), ("on_b", "ffn_on_b")):
        laid[short] = inputs["L1_" + name]
    laid = {n: np.ascontiguousarray(a) for n, a in laid.items()}
    nc = bacc.Bacc("TRN2", target_bir_lowering=False, num_devices=1, dynamic_dma_scratch_size=1024)
    dram = {n: nc.dram_tensor(f"in_{n}", a.shape, F32, kind="ExternalInput").ap() for n, a in laid.items()}
    dram["shares"] = nc.dram_tensor("shares", (EXPERTS, TOK), F32, kind="Internal").ap()
    dram["out"] = nc.dram_tensor("out", (TILES, P, D), F32, kind="ExternalOutput").ap()
    program(nc, dram)
    r = run_bass_kernel_spmd(nc, [{f"in_{n}": a for n, a in laid.items()}], core_ids=[0])
    return r.results[0]["out"]
```

```python
from contextlib import ExitStack

import concourse.bass as bass
from concourse import mybir

F32 = mybir.dt.float32
F32R = mybir.dt.float32r
ALU = mybir.AluOpType
ACT = mybir.ActivationFunctionType
AX_X = mybir.AxisListType.X

P = 128
D = 256
KC = D // P
TOK = 2048
TILES = TOK // P
GT = 4
GW = GT * P
GROUPS = TILES // GT
HEADS, DH = 16, 64
HD = HEADS * DH
CH = HD // P
EXPERTS, TOPK, XD = 32, 8, 128
EG = 4
EGS = EXPERTS // EG
E1, H1 = 4, 512
HC1 = H1 // P
EPS_LN = 1e-5
EPS_GATE = 1e-8

PASSES = ((0, 0), (0, 1), (1, 0))


def product(pe, out, stationary, moving, chunks, start=True, stop=True, skip=False):
    last = None
    for k in range(chunks):
        for n, (a, b) in enumerate(PASSES):
            last = pe.matmul(out, stationary(a, k), moving(b, k), start=start and k == 0 and n == 0,
                             stop=stop and k == chunks - 1 and n == 2, skip_group_check=skip)
    return last


class Space:

    def __init__(self, nc, stack, prefix):
        self.nc, self.stack, self.prefix = nc, stack, prefix

    def sb(self, name, shape, dt=F32):
        return self.stack.enter_context(self.nc.sbuf_tensor(f"{self.prefix}_{name}", shape, dt))

    def pair(self, name, shape):
        return [self.sb(f"{name}_hi", shape, F32R), self.sb(f"{name}_lo", shape, F32R)]

    def ps(self, name, shape):
        return self.stack.enter_context(self.nc.psum_tensor(f"{self.prefix}_{name}", shape, F32))

    def sems(self, *names):
        return [self.stack.enter_context(self.nc.semaphore(f"{self.prefix}_{n}")) for n in names]


def carve(region, shapes):
    views, at = {}, 0
    for name, dims in shapes.items():
        size = 1
        for n in dims:
            size *= n
        view = region[:, at:at + size]
        if len(dims) > 1:
            letters = "abc"[:len(dims)]
            view = view.rearrange(f"p ({' '.join(letters)}) -> p {' '.join(letters)}", **dict(zip(letters, dims)))
        views[name], at = view, at + size
    return views


A_WEIGHTS = {"wq": (KC, HD), "wk": (KC, HD), "wv": (KC, HD), "wo": (CH, D)}
A_RAW = {"wv": (KC, HD), "ctx0": (KC, GW), "ctx1": (KC, GW)}
A_WORK = {"v32": (GT, HD), "p32": (GT, 2, P), "vs32": (GT, 2, DH), "neg": (GT, 2), "sums": (GT, 2), "rinv": (GT, 2),
          "xn32": (GT, D), "ctx2": (KC, 2 * GW)}


def stage_a(nc, dram, keep, region):
    x, xnT, ctxT, ident, tg = keep
    with ExitStack() as stack:
        sp_ = Space(nc, stack, "a")
        w = {n: sp_.pair(n, [P, *s]) for n, s in A_WEIGHTS.items()}
        raw, work = carve(region, A_RAW), carve(region, A_WORK)
        raw["ctx2"] = work["ctx2"]
        raw["wo"] = work["ctx2"].rearrange("p k t -> p (k t)").rearrange("p (c d) -> p c d", d=D)
        with ExitStack() as early:
            raw |= {n: Space(nc, early, "a_raw").sb(n, [P, KC, HD]) for n in ("wq", "wk")}
        qT = sp_.pair("qT", [P, GT, 2, P])
        kT = [sp_.pair(f"kT{b}", [P, GW]) for b in range(2)]
        probs = sp_.pair("probs", [P, GT, 2, P])
        v32, p32, vs32, xn32 = (work[n] for n in ("v32", "p32", "vs32", "xn32"))
        vs = sp_.pair("vs", [P, GT, 2, DH])
        oT = sp_.pair("oT", [P, GT, P])
        stage = sp_.sb("stage", [P, GT, 2, KC, P], F32R)
        graw = sp_.sb("graw", [P, 4])
        stats = sp_.sb("stats", [P, GT, 6])
        mv = sp_.sb("mv", [P, GT, 2])
        ve = sp_.sb("ve", [P, GT])
        rstd = sp_.sb("rstd", [P, GT])
        neghalf = sp_.sb("neghalf", [P, GT])
        pad = sp_.sb("pad", [P, 4])
        neg, sums, rinv = (work[n] for n in ("neg", "sums", "rinv"))

        ring = [sp_.ps(f"ring{b}", [P, GW]) for b in range(2)]
        psS = sp_.ps("scores", [P, GT, 2, P])
        psV = sp_.ps("values", [P, GT, 2 * P])
        psO = sp_.ps("outs", [P, GT, D])

        SPLITS = ("wq", "ctx0", "wk", "wv", "ctx1", "ctx2", "wo")
        in_sems = dict(zip(SPLITS, sp_.sems(*[f"{n}_in" for n in SPLITS])))
        g_in, next_in, zeros = sp_.sems("g_in", "next_in", "zeros")
        x_in = sp_.sems(*[f"x_in{g}" for g in range(GROUPS)])
        split_hi, split_lo, ident_done = sp_.sems("split_hi", "split_lo", "ident_done")
        job_done, act_hi, ring_done = sp_.sems("job_done", "act_hi", "ring_done")
        s_done, neg_done, exp_done, rinv_done, vs32_done = sp_.sems("s_done", "neg_done", "exp_done", "rinv_done", "vs32_done")
        vhi_done, vlo_done, phi_done, plo_done, pv_done = sp_.sems("vhi_done", "vlo_done", "phi_done", "plo_done", "pv_done")
        ohi_done, ot_done, o_done, x_upd, staged = sp_.sems("ohi_done", "ot_done", "o_done", "x_upd", "staged")
        st_done, mv_done, ve_done, rstd_done, xn_ready, held = sp_.sems("st_done", "mv_done", "ve_done", "rstd_done", "xn_ready", "held")

        JOBS0, HIS0 = 14, 8

        def table(last):
            jobs, his = {}, {}
            nj = nh = 0
            for s in range(CH):
                if s < CH - 3 or not last:
                    jobs[s, "q"], his[s, "q"] = nj, nh
                    jobs[s, "k"], his[s, "k"] = nj + 1, nh + 1
                    nj, nh = nj + 2, nh + 2
                if s == 2 or (s == 4 and not last):
                    jobs[s, "ln"], his[s, "ln"] = nj, nh
                    nj, nh = nj + KC, nh + KC
                if s < 2 or not last:
                    jobs[s, "v"] = nj
                    nj += 1
            return jobs, his, nj, nh

        JOBS, HIS = table(False)[2:]
        JOBS_ALL, HIS_ALL = (f + n * (GROUPS - 1) + l for f, n, l in zip((JOBS0, HIS0), (JOBS, HIS), table(True)[2:]))
        assert JOBS % 2 == 0 and JOBS0 % 2 == 0 and JOBS_ALL % 2 == 0

        def v_part(s):
            u = (s + 2) % CH
            return u % GT, 1 - u // GT

        def part(name):
            if name[:3] == "ctx":
                at = {"ctx0": slice(0, GW), "ctx1": slice(GW, 2 * GW), "ctx2": slice(2 * GW, TOK)}[name]
                return raw[name], ctxT[0][:, :, at], ctxT[1][:, :, at]
            return raw[name] if name in ("wv", "wo") else raw[name][:, :, :], w[name][0][:, :, :], w[name][1][:, :, :]

        block = stack.enter_context(nc.Block())

        @block.sync
        def _(sp):
            sp.dma_start(x[:, 0:GT, :], dram["x"][:, 0:GT, :]).then_inc(x_in[0], 16)
            sp.dma_start(raw["ctx0"], dram["ctxT"][:, :, 0:GW]).then_inc(in_sems["ctx0"], 16)
            sp.dma_start(raw["wk"][:, :, :], dram["wk"]).then_inc(in_sems["wk"], 16)
            sp.dma_start(raw["ctx1"], dram["ctxT"][:, :, GW:2 * GW]).then_inc(in_sems["ctx1"], 16)
            sp.dma_start(raw["ctx2"], dram["ctxT"][:, :, 2 * GW:TOK]).then_inc(in_sems["ctx2"], 16)
            for g in range(1, GROUPS):
                sp.dma_start(x[:, GT * g:GT * g + GT, :], dram["x"][:, GT * g:GT * g + GT, :]).then_inc(x_in[g], 16)
            sp.wait_ge(split_lo, SPLITS.index("ctx2") + 1)
            sp.dma_start(raw["wo"], dram["wo"]).then_inc(in_sems["wo"], 16)
            sp.wait_ge(vs32_done, CH * GROUPS)
            first = carve(region, B_FIRST)
            sp.dma_start(first["weights"], dram["moe"][0, :, :]).then_inc(next_in, 16)
            sp.dma_start(first["gate"], dram["gate"]).then_inc(next_in, 16)
            sp.wait_ge(next_in, 32)

        @block.gpsimd
        def _(pool):
            pool.memset(ident[:, :], 0.0).then_inc(ident_done, 1)
            pool.memset(neghalf[:, :], -0.5).then_inc(ident_done, 1)
            pool.wait_ge(ident_done, 2)
            pool.affine_select(out=ident[:, :], in_=ident[:, :], compare_op=ALU.not_equal, fill=1.0, base=0,
                               pattern=[[-1, P]], channel_multiplier=1).then_inc(ident_done, 1)

            def rsqrt(n):
                pool.wait_ge(ve_done, n + 1)
                pool.tensor_tensor(rstd[:, :], ve[:, :], neghalf[:, :], ALU.pow).then_inc(rstd_done, 1)

            def stage_tile(t, g):
                for part in range(2):
                    pool.tensor_copy(stage[:, t, part, :, :], ctxT[part][:, :, bass.ds(g * GW + t * P, P)].bitcast(F32)
                                     ).then_inc(staged, 1)

            def probs_lo(n):
                pool.wait_ge(phi_done, n + 1)
                pool.tensor_tensor(probs[1][:, :, :, :], p32[:, :, :, :], probs[0][:, :, :, :].bitcast(F32),
                                   ALU.subtract).then_inc(plo_done, 1)
                pool.wait_ge(vhi_done, n + 1)
                pool.tensor_tensor(vs[1][:, :, :, :], vs32, vs[0][:, :, :, :].bitcast(F32), ALU.subtract).then_inc(vlo_done, 1)

            def slots(i, last):
                jobs = table(last)[0]
                for s in range(CH):
                    J = JOBS0 + JOBS * i
                    if s == 1 or (s == 3 and not last):
                        rsqrt(2 * i + (1 if s == 1 else 2))
                    if s < GT and not last:
                        pool.wait_ge(job_done, J + (jobs[s - 2, "v"] + 1 if s >= 2 else 0))
                        stage_tile(s, (i + 1) % GROUPS)
                    if s < CH - 2 or not last:
                        probs_lo(CH * i + s + 2)

            rsqrt(0)
            pool.wait_ge(split_lo, 3)
            for a in qT:
                for j in range(2):
                    pool.memset(a[DH * j:DH * j + DH, :, 1 - j, :].bitcast(F32), 0.0).then_inc(zeros, 1)
            probs_lo(0)
            probs_lo(1)
            pool.wait_ge(split_lo, len(SPLITS))
            with pool.Fori(0, GROUPS - 1) as i:
                slots(i, False)
            slots(GROUPS - 1, True)
            rsqrt(2 * GROUPS)

        @block.scalar
        def _(act):
            act.dma_start(raw["wq"][:, :, :], dram["wq"]).then_inc(in_sems["wq"], 16)
            act.dma_start(raw["wv"], dram["wv"]).then_inc(in_sems["wv"], 16)
            act.dma_start(graw[:, :], dram["g"].partition_broadcast(P)).then_inc(g_in, 16)

            def split(name):
                src, hi, _ = part(name)
                act.wait_ge(in_sems[name], 16)
                act.activation(hi, src, ACT.Copy).then_inc(split_hi, 1)

            def ln_hi(job, kc, g):
                act.wait_ge(job_done, job + 1)
                act.activation(xnT[0][:, kc, bass.ds(g * GW, GW)], ring[kc][:, :], ACT.Copy).then_inc(act_hi, 1)

            def qk_hi(which, job, bank, buf, n):
                act.wait_ge(job_done, job + 1)
                if which == "k":
                    if n is not None and not (isinstance(n, int) and n == 0):
                        act.wait_ge(s_done, n)
                    act.activation(kT[buf][0][:, :], ring[bank][:, :], ACT.Copy).then_inc(act_hi, 1)
                    return
                if n is not None:
                    act.wait_ge(s_done, n + 1)
                for j in range(2):
                    lanes = slice(DH * j, DH * j + DH)
                    ins = act.activation(qT[0][lanes, :, j, :], ring[bank][lanes, :].rearrange("p (b n) -> p b n", b=GT),
                                         ACT.Copy, scale=DH ** -0.5)
                ins.then_inc(act_hi, 1)

            def exps(n, part, first):
                if part == 0:
                    act.wait_ge(neg_done, n + 1)
                    if not first:
                        act.wait_ge(plo_done, n)
                        act.wait_ge(phi_done, n)
                for b in range(2 * part, 2 * part + 2):
                    for j in range(2):
                        ins = act.activation(p32[:, b, j, :], psS[:, b, j, :], ACT.Exp, bias=neg[:, b, j:j + 1],
                                             accum_out=sums[:, b, j:j + 1])
                if part == 1:
                    ins.then_inc(exp_done, 1)

            def probs_hi(n):
                act.wait_ge(exp_done, n + 1)
                if not (isinstance(n, int) and n == 0):
                    act.wait_ge(pv_done, n)
                act.activation(probs[0][:, :, :, :], p32[:, :, :, :], ACT.Copy).then_inc(phi_done, 1)

            def out_hi(n):
                act.wait_ge(pv_done, n + 1)
                act.wait_ge(o_done, n + 1)
                for j in range(2):
                    lanes = slice(DH * j, DH * j + DH)
                    act.activation(oT[0][lanes, :, :], psV[lanes, :, P * j:P * j + P], ACT.Copy).then_inc(ohi_done, 1)

            for name in ("wq", "ctx0"):
                split(name)
            for kc in range(KC):
                ln_hi(kc, kc, 0)
            split("wk")
            split("wv")
            act.wait_ge(split_lo, 2)
            for t in range(GT):
                for k in range(2):
                    act.activation(stage[:, t, k, :, :], ctxT[k][:, :, t * P:t * P + P].bitcast(F32),
                                   ACT.Copy).then_inc(staged, 1)
            act.wait_ge(split_lo, 3)
            qk_hi("q", 2, 0, 0, None)
            qk_hi("k", 3, 1, 0, None)
            split("ctx1")
            split("ctx2")
            act.wait_ge(g_in, 16)
            act.activation(tg[:, :], graw[:, :], ACT.Tanh).then_inc(g_in, 1)
            for n in range(2):
                if n:
                    qk_hi("q", 10 + 2 * n, 0, (n + 1) % 2, n)
                exps(n, 0, n == 0)
                exps(n, 1, n == 0)
                if n == 0:
                    qk_hi("q", 10 + 2 * n, 0, (n + 1) % 2, n)
                qk_hi("k", 11 + 2 * n, 1, (n + 1) % 2, n)
                probs_hi(n)
                if n == 0:
                    split("wo")
                else:
                    out_hi(n - 1)

            def slots(i, last):
                jobs = table(last)[0]
                for s in range(CH):
                    n = CH * i + s + 2
                    J = JOBS0 + JOBS * i
                    mine = s < CH - 2 or not last
                    if (s, "q") in jobs:
                        qk_hi("q", J + jobs[s, "q"], jobs[s, "q"] % 2, (s + 1) % 2, n)
                    if mine:
                        exps(n, 0, False)
                    if (s, "k") in jobs:
                        qk_hi("k", J + jobs[s, "k"], jobs[s, "k"] % 2, (s + 1) % 2, n)
                    if (s, "ln") in jobs:
                        for kc in range(KC):
                            ln_hi(J + jobs[s, "ln"] + kc, kc, (i + (3 if s == 2 else 1)) % GROUPS)
                    if mine:
                        exps(n, 1, False)
                        probs_hi(n)
                    if s < CH - 1 or not last:
                        out_hi(n - 1)

            with act.Fori(0, GROUPS - 1) as i:
                slots(i, False)
            slots(GROUPS - 1, True)
            for kc in range(KC):
                ln_hi(JOBS_ALL + kc, kc, GROUPS - 1)

        @block.vector
        def _(dve):
            dve.memset(pad[:, 1:2], 0.0).then_inc(x_upd, 1)
            dve.memset(pad[:, 2:3], 0.0).then_inc(ot_done, 1)
            dve.memset(pad[:, 3:4], 0.0).then_inc(o_done, 1)
            dve.memset(pad[:, 0:1], 0.0).then_inc(held, 1)

            def ln_stats(n, g, landed):
                if landed is not None:
                    dve.wait_ge(landed, 16)
                else:
                    dve.wait_ge(x_upd, g[1])
                gx = g[0]
                for t in range(GT):
                    dve.bn_stats(stats[:, t, :], x[:, gx * GT + t, :]).then_inc(st_done, 1)
                dve.wait_ge(held, n + 1)
                dve.wait_ge(st_done, GT * n + GT)
                dve.memset(pad[:, 0:1], 0.0).then_inc(held, 1)
                for t in range(GT):
                    dve.bn_aggr(mv[:, t, :], stats[:, t, :]).then_inc(mv_done, 1)
                dve.wait_ge(mv_done, GT * n + GT)
                dve.tensor_scalar(ve[:, :], mv[:, :, 1], EPS_LN, None, ALU.add).then_inc(ve_done, 1)

            def ln_apply(n, gx):
                dve.wait_ge(rstd_done, n + 1)
                for t in range(GT):
                    dve.tensor_scalar(xn32[:, t, :], x[:, gx * GT + t, :], mv[:, t, 0:1], rstd[:, t:t + 1],
                                      ALU.subtract, ALU.mult).then_inc(xn_ready, 1)

            def ln_lo(hi, kc, g):
                dve.wait_ge(act_hi, hi + 1)
                at = bass.ds(g * GW, GW)
                dve.tensor_tensor(xnT[1][:, kc, at], ring[kc][:, :], xnT[0][:, kc, at].bitcast(F32),
                                  ALU.subtract).then_inc(ring_done, 1)

            def v_out(job, bank, t, half):
                dve.wait_ge(job_done, job + 1)
                dve.tensor_copy(v32[:, t, half * 512:half * 512 + 512], ring[bank][:, :]).then_inc(ring_done, 1)

            def qk_lo(which, hi, bank, buf):
                dve.wait_ge(act_hi, hi + 1)
                if which == "q":
                    for j in range(2):
                        lanes = slice(DH * j, DH * j + DH)
                        ins = dve.scalar_tensor_tensor(qT[1][lanes, :, j, :], ring[bank][lanes, :].rearrange("p (b n) -> p b n", b=GT),
                                                       DH ** -0.5, qT[0][lanes, :, j, :].bitcast(F32), ALU.mult, ALU.subtract)
                    ins.then_inc(ring_done, 1)
                else:
                    dve.tensor_tensor(kT[buf][1][:, :], ring[bank][:, :], kT[buf][0][:, :].bitcast(F32),
                                      ALU.subtract).then_inc(ring_done, 1)

            def minus_max(n):
                dve.wait_ge(s_done, n + 1)
                dve.tensor_reduce(neg[:, :, :], psS[:, :, :, :], AX_X, ALU.max, negate=True).then_inc(neg_done, 1)

            def scale_values(n, c, rows, first):
                dve.wait_ge(exp_done, n + 1)
                dve.reciprocal(rinv[:, :, :], sums[:, :, :]).then_inc(rinv_done, 1)
                dve.wait_ge(rinv_done, n + 1)
                if not first:
                    dve.wait_ge(vlo_done, n)
                dve.wait_ge(ring_done, rows)
                dve.tensor_tensor(vs32[:, :, :, :], v32[:, :, c * P:c * P + P].rearrange("p t (j d) -> p t j d", j=2),
                                  rinv[:, :, :].unsqueeze(3).broadcast_to([P, GT, 2, DH]), ALU.mult).then_inc(vs32_done, 1)
                dve.wait_ge(vs32_done, n + 1)
                if not first:
                    dve.wait_ge(pv_done, n)
                dve.tensor_copy(vs[0][:, :, :, :], vs32[:, :, :, :]).then_inc(vhi_done, 1)

            def out_lo(n):
                dve.wait_ge(ohi_done, 2 * n + 2)
                for j in range(2):
                    lanes = slice(DH * j, DH * j + DH)
                    ins = dve.tensor_tensor(oT[1][lanes, :, :], psV[lanes, :, P * j:P * j + P],
                                            oT[0][lanes, :, :].bitcast(F32), ALU.subtract)
                ins.then_inc(ot_done, 1)

            def split(name):
                k = SPLITS.index(name)
                src, hi, lo = part(name)
                dve.wait_ge(split_hi, k + 1)
                dve.tensor_tensor(lo, src, hi.bitcast(F32), ALU.subtract).then_inc(split_lo, 1)

            ln_stats(0, (0, None), x_in[0])
            split("wq")
            ln_apply(0, 0)
            split("ctx0")
            for kc in range(KC):
                ln_lo(kc, kc, 0)
            split("wk")
            split("wv")
            qk_lo("q", 2, 0, 0)
            qk_lo("k", 3, 1, 0)
            split("ctx1")
            split("ctx2")
            minus_max(0)
            dve.wait_ge(split_lo, 6)
            for t in range(GT):
                v_out(4 + t, t % 2, t, 0)
            v_out(8, 0, 0, 1)
            v_out(9, 1, 1, 1)
            for n in range(2):
                if n:
                    minus_max(n)
                qk_lo("q", 4 + 2 * n, 0, (n + 1) % 2)
                qk_lo("k", 5 + 2 * n, 1, (n + 1) % 2)
                scale_values(n, n, 8, n == 0)
                if n == 0:
                    split("wo")
                else:
                    out_lo(n - 1)
            for g in range(1, GROUPS):
                dve.wait_ge(x_in[g], 16)
            dve.wait_ge(g_in, 17)

            def slots(i, last):
                jobs, his = table(last)[:2]
                for s in range(CH):
                    n = CH * i + s + 2
                    J, H = JOBS0 + JOBS * i, HIS0 + HIS * i
                    mine = s < CH - 2 or not last
                    if mine:
                        minus_max(n)
                    lns = s == 1 or (s == 3 and not last)
                    if lns:
                        gx = (i + (3 if s == 1 else 1)) % GROUPS
                        ln_stats(2 * i + (1 if s == 1 else 2), (gx, i + 1), None)
                    if (s, "q") in jobs:
                        qk_lo("q", H + his[s, "q"], jobs[s, "q"] % 2, (s + 1) % 2)
                        qk_lo("k", H + his[s, "k"], jobs[s, "k"] % 2, (s + 1) % 2)
                    if (s, "ln") in jobs:
                        for kc in range(KC):
                            ln_lo(H + his[s, "ln"] + kc, kc, (i + (3 if s == 2 else 1)) % GROUPS)
                    if mine:
                        before = max((t for t in range(s) if (t, "v") in jobs), default=None)
                        scale_values(n, (s + 2) % CH, J + (jobs[before, "v"] + 1 if s else 0), False)
                    if (s, "v") in jobs:
                        t, half = v_part(s)
                        v_out(J + jobs[s, "v"], jobs[s, "v"] % 2, t, half)
                    if lns:
                        ln_apply(2 * i + (1 if s == 1 else 2), gx)
                    if s < CH - 1 or not last:
                        out_lo(n - 1)
                dve.wait_ge(o_done, CH * i + CH + 1)
                at = bass.ds(i * GT, GT)
                dve.scalar_tensor_tensor(x[:, at, :], psO[:, :, :], tg[:, 0:1], x[:, at, :],
                                         ALU.mult, ALU.add).then_inc(x_upd, 1)

            with dve.Fori(0, GROUPS - 1) as i:
                slots(i, False)
            slots(GROUPS - 1, True)
            ln_stats(2 * GROUPS, (GROUPS - 1, GROUPS + 1), None)
            ln_apply(2 * GROUPS, GROUPS - 1)
            for kc in range(KC):
                ln_lo(HIS_ALL + kc, kc, GROUPS - 1)

        @block.tensor
        def _(pe):
            def ring_free(job, first=False):
                if not first:
                    pe.wait_ge(ring_done, job - 1)

            def ln_jobs(n, job, first=False, chunks=range(KC)):
                pe.wait_ge(xn_ready, GT * n + GT)
                for kc in chunks:
                    ring_free(job + kc, first)
                    for t in range(GT):
                        mm = pe.transpose(ring[kc][:, t * P:t * P + P], xn32[:, t, kc * P:kc * P + P], ident[:, :])
                    mm.then_inc(job_done, 1)

            def v_job(job, bank, t, half):
                ring_free(job)
                product(pe, ring[bank][:, :], lambda a, k: stage[:, t, a, k, :],
                        lambda b, k: w["wv"][b][:, k, half * 512:half * 512 + 512], KC).then_inc(job_done, 1)

            def qk_job(which, job, bank, c, g):
                ring_free(job)
                src = xnT if which == "q" else ctxT
                wt = w["w" + which]
                product(pe, ring[bank][:, :], lambda a, k: wt[a][:, k, c * P:c * P + P],
                        lambda b, k: src[b][:, k, bass.ds(g * GW, GW)], KC).then_inc(job_done, 1)

            def scores(n, rows, buf, first):
                pe.wait_ge(ring_done, rows)
                if not first:
                    pe.wait_ge(exp_done, n)
                for b in range(GT):
                    for m, (ka, qb) in enumerate(PASSES):
                        mm = pe.matmul(psS[:, b, :, :], kT[buf][ka][:, b * P:b * P + P], qT[qb][:, b, :, :],
                                       start=m == 0, stop=m == 2)
                mm.then_inc(s_done, 1)

            def values(n):
                pe.wait_ge(vlo_done, n + 1)
                pe.wait_ge(plo_done, n + 1)
                pe.wait_ge(ot_done, n + 1)
                for b in range(GT):
                    for m, (a, q) in enumerate(PASSES):
                        mm = pe.matmul(psV[:, b, :], vs[a][:, b, :, :], probs[q][:, b, :, :], start=m == 0, stop=m == 2)
                mm.then_inc(pv_done, 1)

            def outs(n, c, free):
                pe.wait_ge(ot_done, n + 2)
                if c == 0:
                    pe.wait_ge(x_upd, free)
                for b in range(GT):
                    for m, (a, q) in enumerate(PASSES):
                        mm = pe.matmul(psO[:, b, :], oT[a][:, b, :], w["wo"][q][:, c, :],
                                       start=c == 0 and m == 0 and b % 2 == 0, stop=c == CH - 1 and m == 2,
                                       skip_group_check=True)
                mm.then_inc(o_done, 1)

            pe.wait_ge(ident_done, 3)
            ln_jobs(0, 0, True)
            pe.wait_ge(split_lo, 1)
            pe.wait_ge(ring_done, 2)
            qk_job("q", 2, 0, 0, 0)
            pe.wait_ge(split_lo, 3)
            qk_job("k", 3, 1, 0, 0)
            pe.wait_ge(zeros, 4)
            scores(0, 4, 0, True)
            pe.wait_ge(split_lo, 4)
            pe.wait_ge(staged, 2 * GT)
            for t in range(GT):
                v_job(4 + t, t % 2, t, 0)
            v_job(8, 0, 0, 1)
            v_job(9, 1, 1, 1)
            for n in range(2):
                if n:
                    scores(n, 10 + 2 * n, n, False)
                qk_job("q", 10 + 2 * n, 0, n + 1, 0)
                qk_job("k", 11 + 2 * n, 1, n + 1, 0)
                if n:
                    values(n - 1)
            pe.wait_ge(split_lo, len(SPLITS))

            def slots(i, last):
                jobs = table(last)[0]
                for s in range(CH):
                    n = CH * i + s + 2
                    J = JOBS0 + JOBS * i
                    gq = i if s < CH - 3 else (i + 1) % GROUPS
                    if s < CH - 2 or not last:
                        scores(n, J + (jobs[s - 1, "k"] + 1 if s else 0), s % 2, False)
                    if (s, "q") in jobs:
                        qk_job("q", J + jobs[s, "q"], jobs[s, "q"] % 2, (s + 3) % CH, gq)
                        qk_job("k", J + jobs[s, "k"], jobs[s, "k"] % 2, (s + 3) % CH, gq)
                    outs(n - 2, s, i + 1)
                    if (s, "ln") in jobs:
                        ln_jobs(2 * i + (1 if s == 2 else 2), J + jobs[s, "ln"], chunks=(0,))
                    if s < CH - 1 or not last:
                        values(n - 1)
                    if (s, "ln") in jobs:
                        ln_jobs(2 * i + (1 if s == 2 else 2), J + jobs[s, "ln"], chunks=(1,))
                    if (s, "v") in jobs:
                        t, half = v_part(s)
                        if half == 0:
                            pe.wait_ge(staged, 2 * GT * (i + 1) + 2 * (t + 1))
                        v_job(J + jobs[s, "v"], jobs[s, "v"] % 2, t, half)

            with pe.Fori(0, GROUPS - 1) as i:
                slots(i, False)
            slots(GROUPS - 1, True)
            ln_jobs(2 * GROUPS, JOBS_ALL)


B_FIRST = {"weights": (EG * (KC * 2 * XD + D),), "gate": (KC, EXPERTS)}


def stage_b(nc, dram, keep, region):
    x, xnT, ctxT, ident, tg = keep
    ITEMS = EG * GROUPS
    UP = KC * 2 * XD
    with ExitStack() as stack:
        sp_ = Space(nc, stack, "b")
        wraw = sp_.sb("wraw", [P, EG * (UP + D)])
        wsp = [sp_.pair(f"w{b}", [P, EG * (UP + D)]) for b in range(2)]
        first = carve(region, B_FIRST)
        neg = sp_.sb("neg", [P, TILES])
        lg = sp_.sb("lg", [P, TILES, EXPERTS])
        ex = sp_.sb("ex", [P, TILES, EXPERTS])
        top = sp_.sb("top", [P, TILES, TOPK])
        rest = lg
        total = sp_.sb("total", [P, TILES])
        inv = sp_.sb("inv", [P, TILES])
        comb = sp_.sb("comb", [P, TILES, EXPERTS])
        combT = sp_.sb("combT", [P, GROUPS, P])
        share = [sp_.sb(f"share{b}", [P, EG, GW]) for b in range(2)]
        silu = [sp_.sb(f"silu{b}", [P, GW]) for b in range(2)]
        weighted = sp_.sb("weighted", [P, GW])
        h32 = [sp_.sb(f"h32{b}", [P, GW]) for b in range(2)]
        h = [sp_.pair(f"h{b}", [P, GW]) for b in range(2)]
        later, _ = c_region(region)
        LATER = ("w2", "ak", "av", "aq")
        acc = region[:, 0:KC * TOK].rearrange("p (k t) -> p k t", k=KC)
        gate = [a[:, 0:KC * P].rearrange("p (k c) -> p k c", k=KC) for a in h[0]]
        lgT = [*silu, *h32]
        pad = sp_.sb("pad", [P, 4])
        psG = [sp_.ps(f"gate{b}", [P, GW]) for b in range(2)]
        psU = [sp_.ps(f"up{b}", [P, GW]) for b in range(2)]
        psY = [sp_.ps(f"down{b}", [P, KC, GW]) for b in range(2)]
        banks = [*psG, *psU]

        g_split, lgT_ps, lgT_done, lg_done, r_done, ex_done, cT_ps, cT_done, cw_out, padded = sp_.sems(
            "g_split", "lgT_ps", "lgT_done", "lg_done", "r_done", "ex_done", "cT_ps", "cT_done", "cw_out", "padded")
        w_in, w_split, share_in0, share_in1, later_in = sp_.sems("w_in", "w_split", "share_in0", "share_in1", "later_in")
        share_in = [share_in0, share_in1]
        g_done, u_done, d_done, s_done, t_done, h_done, hhi_done, hlo_done, acc_done, yT_done, x_upd = sp_.sems(
            "g_done", "u_done", "d_done", "s_done", "t_done", "h_done", "hhi_done", "hlo_done", "acc_done", "yT_done", "x_upd")

        def up(buf, part, e, k, half):
            at = (e * KC + k) * 2 * XD + half * XD
            return wsp[buf][part][:, at:at + XD]

        def down(buf, part, e, c):
            at = EG * UP + e * D + c * P
            return wsp[buf][part][:, at:at + P]

        def write_share(queue, tt):
            queue.dma_start(dram["shares"].rearrange("e (g t n) -> t e g n", t=GT, n=P)[tt, :, :, :],
                            combT[tt * EXPERTS:tt * EXPERTS + EXPERTS, :, :]).then_inc(cw_out, 16)

        block = stack.enter_context(nc.Block())

        @block.sync
        def _(sp):
            def load_weights(eg):
                sp.dma_start(wraw[:, :], dram["moe"][eg, :, :]).then_inc(w_in, 16)

            def load_share(eg, tg_):
                rows = dram["shares"][bass.ds(eg * EG, EG), tg_ * GW:tg_ * GW + GW]
                sp.dma_start(share[tg_ % 2][:, :, :], rows.partition_broadcast(P)).then_inc(share_in[tg_ % 2], 16)

            load_weights(1)
            for n in LATER:
                sp.dma_start(later[n], dram[n]).then_inc(later_in, 16)
            sp.wait_ge(cT_done, 1)
            for tt in range(GT // 2):
                write_share(sp, tt)
            sp.wait_ge(cw_out, 16 * GT)
            load_share(0, 0)
            load_share(0, 1)

            def loads(eg):
                for t in range(GROUPS):
                    last = isinstance(eg, int) and eg == EGS - 1
                    if last and t + 2 >= GROUPS:
                        break
                    sp.wait_ge(t_done, ITEMS * eg + EG * (t + 1))
                    load_share(eg + (t + 2) // GROUPS, (t + 2) % GROUPS)
                    if t == 1 and not isinstance(eg, int):
                        sp.wait_ge(w_split, 2 * eg + 4)
                        load_weights(eg + 2)

            with sp.Fori(0, EGS - 2) as eg:
                loads(eg)
            loads(EGS - 2)
            loads(EGS - 1)
            sp.wait_ge(later_in, 16 * len(LATER))
            sp.wait_ge(w_in, 16 * (EGS - 1))
            sp.wait_ge(share_in[0], 32 * EGS)
            sp.wait_ge(share_in[1], 32 * EGS)

        @block.gpsimd
        def _(pool):
            pool.memset(pad[:, 1:2], 0.0).then_inc(padded, 1)

            def split(n, buf):
                pool.tensor_copy(wsp[buf][0][:, :], wraw[:, :]).then_inc(w_split, 1)
                pool.wait_ge(w_split, 2 * n + 1)
                pool.tensor_tensor(wsp[buf][1][:, :], wraw[:, :], wsp[buf][0][:, :].bitcast(F32),
                                   ALU.subtract).then_inc(w_split, 1)

            pool.wait_ge(w_split, 2)
            pool.wait_ge(w_in, 16)
            split(1, 1)
            with pool.Fori(0, EGS // 2 - 1) as p:
                for q in range(2):
                    n = 2 * p + q + 2
                    pool.wait_ge(d_done, ITEMS * (n - 1) + 1)
                    pool.wait_ge(w_in, 16 * n)
                    pool.wait_ge(padded, n - 1)
                    pool.tensor_tensor(pad[:, 1:2], pad[:, 1:2], pad[:, 1:2], ALU.add).then_inc(padded, 1)
                    split(n, q)

        @block.scalar
        def _(act):
            act.activation(wsp[0][0][:, :], first["weights"], ACT.Copy).then_inc(w_split, 1)
            for g in range(2):
                act.wait_ge(lgT_ps, g + 1)
                act.activation(lgT[g][0:EXPERTS, :], banks[g][0:EXPERTS, :], ACT.Copy).then_inc(lgT_done, 1)
            act.wait_ge(ex_done, 1)
            act.activation(ex[:, :, :], lg[:, :, :], ACT.Exp).then_inc(ex_done, 1)

            def silus(n, buf):
                act.wait_ge(g_done, n + 1)
                act.activation(silu[buf][:, :], psG[buf][:, :], ACT.Silu).then_inc(s_done, 1)

            act.wait_ge(lg_done, 1)
            silus(0, 0)
            act.wait_ge(cT_done, 1)
            for tt in range(GT // 2, GT):
                write_share(act, tt)
            def items(p, last):
                for k in range(2 * ITEMS):
                    m = 2 * ITEMS * p + k
                    act.wait_ge(h_done, m + 1)
                    act.activation(h[k % 2][0][:, :], h32[k % 2][:, :], ACT.Copy).then_inc(hhi_done, 1)
                    if not last or k < 2 * ITEMS - 1:
                        silus(m + 1, (k + 1) % 2)

            with act.Fori(0, EGS // 2 - 1) as p:
                items(p, False)
            items(EGS // 2 - 1, True)

        @block.vector
        def _(dve):
            four = [a.rearrange("p k (r e) -> p k r e", e=EXPERTS) for a in gate]
            beside = first["gate"].unsqueeze(2).broadcast_to([P, KC, P // EXPERTS, EXPERTS])
            dve.tensor_copy(four[0], beside).then_inc(g_split, 1)
            dve.wait_ge(g_split, 1)
            dve.tensor_tensor(four[1], beside, four[0].bitcast(F32), ALU.subtract).then_inc(g_split, 1)
            dve.memset(pad[:, 0:1], 0.0).then_inc(d_done, 1)
            dve.memset(psY[1][:, :, :], 0.0).then_inc(acc_done, 1)
            dve.wait_ge(w_split, 1)
            dve.tensor_tensor(wsp[0][1][:, :], first["weights"], wsp[0][0][:, :].bitcast(F32), ALU.subtract).then_inc(w_split, 1)
            for g in range(2, GROUPS):
                dve.wait_ge(lgT_ps, g + 1)
                dve.tensor_copy(lgT[g][0:EXPERTS, :], banks[g][0:EXPERTS, :]).then_inc(lgT_done, 1)
            logits = psY[0][:, 0, :].rearrange("p (t e) -> p t e", e=EXPERTS)
            steps = [0]

            def chain(ins):
                steps[0] += 1
                ins.then_inc(r_done, 1)
                dve.wait_ge(r_done, steps[0])

            def wide(a, n=EXPERTS):
                return a.unsqueeze(2).broadcast_to([P, TILES, n])

            dve.wait_ge(lg_done, 1)
            chain(dve.tensor_reduce(neg[:, :], logits, AX_X, ALU.max, negate=True))
            dve.tensor_tensor(lg[:, :, :], logits, wide(neg[:, :]), ALU.add).then_inc(ex_done, 1)
            dve.wait_ge(ex_done, 2)
            for t in range(TILES):
                last = dve.max(top[:, t, :], ex[:, t, :])
            chain(last)
            for t in range(TILES):
                last = dve.match_replace(rest[:, t, :], top[:, t, :], ex[:, t, :], -1.0)
            chain(last)
            dve.tensor_reduce(total[:, :], top[:, :, :], AX_X, ALU.add)
            chain(dve.scalar_tensor_tensor(comb[:, :, :], rest[:, :, :], 0.0, ex[:, :, :], ALU.is_lt, ALU.mult))
            chain(dve.reciprocal(inv[:, :], total[:, :]))
            chain(dve.tensor_tensor(comb[:, :, :], comb[:, :, :], wide(inv[:, :]), ALU.mult))
            dve.wait_ge(cT_ps, 1)
            dve.tensor_copy(combT[:, :, :], psY[0][:, 1, :].rearrange("p (g n) -> p g n", g=GROUPS)).then_inc(cT_done, 1)

            dve.memset(acc[:, :, :], 0.0).then_inc(acc_done, 1)

            def add_up(t, buf):
                at = slice(t * GW, t * GW + GW)
                dve.tensor_tensor(acc[:, :, at], acc[:, :, at], psY[buf][:, :, :], ALU.add).then_inc(acc_done, 1)

            with dve.Fori(0, EGS // 2) as p:
                for k in range(2 * ITEMS):
                    m = 2 * ITEMS * p + k
                    e, t, b = k % EG, k // EG % GROUPS, k % 2
                    if e == 0:
                        dve.wait_ge(share_in[t % 2], 16 * (4 * p + k // (2 * EG) + 1))
                    dve.wait_ge(s_done, m + 1)
                    dve.tensor_tensor(weighted[:, :], silu[b][:, :], share[t % 2][:, e, :], ALU.mult).then_inc(t_done, 1)
                    dve.wait_ge(t_done, m + 1)
                    dve.wait_ge(u_done, m + 1)
                    dve.tensor_tensor(h32[b][:, :], weighted[:, :], psU[b][:, :], ALU.mult).then_inc(h_done, 1)
                    dve.wait_ge(hhi_done, m + 1)
                    dve.tensor_tensor(h[b][1][:, :], h32[b][:, :], h[b][0][:, :].bitcast(F32),
                                      ALU.subtract).then_inc(hlo_done, 1)
                    if e == 0:
                        dve.wait_ge(d_done, m + 1)
                        dve.wait_ge(acc_done, EGS * p + k // EG + 2)
                        add_up((t - 1) % GROUPS, (t - 1) % 2)
            n = ITEMS * EGS
            dve.wait_ge(d_done, n + 1)
            add_up(GROUPS - 1, 1)
            for g in range(GROUPS):
                dve.wait_ge(yT_done, g + 1)
                at = slice(g * GT, g * GT + GT)
                dve.scalar_tensor_tensor(x[:, at, :], psY[g % 2][:, :, :].rearrange("p k (t d) -> p (k t) d", d=D),
                                         tg[:, 2:3], x[:, at, :], ALU.mult, ALU.add).then_inc(x_upd, 1)

        @block.tensor
        def _(pe):
            def gate_up(k, buf):
                e, t = k % EG, k // EG % GROUPS
                for half, out, sem in ((0, psG, g_done), (1, psU, u_done)):
                    product(pe, out[k % 2][:, :], lambda a, c: up(buf, a, e, c, half),
                            lambda b, c: xnT[b][:, c, t * GW:t * GW + GW], KC).then_inc(sem, 1)

            def down_products(k, m, tile):
                e, t, buf = k % EG, k // EG % GROUPS, k // ITEMS
                pe.wait_ge(hlo_done, m + 1)
                if e == 0:
                    pe.wait_ge(acc_done, tile + 2)
                for c in range(KC):
                    for n, (a, b) in enumerate(PASSES):
                        mm = pe.matmul(psY[t % 2][:, c, :], down(buf, a, e, c), h[k % 2][b][:, :],
                                       start=e == 0 and n == 0, stop=e == EG - 1 and n == 2)
                mm.then_inc(d_done, 1)

            pe.wait_ge(g_split, 2)
            for g in range(GROUPS):
                product(pe, banks[g][:, :], lambda a, k: gate[a][:, k, :],
                        lambda b, k: xnT[b][:, k, g * GW:g * GW + GW], KC).then_inc(lgT_ps, 1)
            pe.wait_ge(lgT_done, GROUPS)
            for t in range(TILES):
                at = t % GT * P
                mm = pe.transpose(psY[0][:, 0, t * EXPERTS:t * EXPERTS + EXPERTS], lgT[t // GT][0:EXPERTS, at:at + P],
                                  ident[0:EXPERTS, 0:EXPERTS])
            mm.then_inc(lg_done, 1)
            pe.wait_ge(w_split, 2)
            gate_up(0, 0)
            pe.wait_ge(r_done, 6)
            for g in range(GROUPS):
                mm = pe.transpose(psY[0][:, 1, g * P:g * P + P], comb[:, g * GT:g * GT + GT, :], ident[:, :])
            mm.then_inc(cT_ps, 1)
            pe.wait_ge(cT_done, 1)
            def items(p, last):
                for k in range(2 * ITEMS):
                    if not last or k < 2 * ITEMS - 1:
                        nxt = (k + 1) % (2 * ITEMS)
                        if nxt % ITEMS == 0:
                            pe.wait_ge(w_split, 4 * p + 2 * (k + 1) // ITEMS + 2)
                        gate_up(nxt, nxt // ITEMS)
                    down_products(k, 2 * ITEMS * p + k, 2 * EG * p + k // EG)

            with pe.Fori(0, EGS // 2 - 1) as p:
                items(p, False)
            items(EGS // 2 - 1, True)
            for g in range(GROUPS):
                pe.wait_ge(acc_done, GROUPS * EGS + 3)
                if g >= 2:
                    pe.wait_ge(x_upd, g - 1)
                for t in range(GT):
                    for c in range(KC):
                        at = t * D + c * P
                        mm = pe.transpose(psY[g % 2][:, at // GW, at % GW:at % GW + P],
                                          acc[:, c, (g * GT + t) * P:(g * GT + t) * P + P], ident[:, :])
                mm.then_inc(yT_done, 1)


C_WEIGHTS = {"w1": (E1, KC * H1), "w2": (E1, HC1 * D), "aq": (KC, D), "ak": (KC, D), "av": (KC, D)}
C_FIRST = {"xn32": (GT, D), "f32_0": (GW,), "f32_1": (GW,), "p32": (GT, P), "a32_0": (GW,), "a32_1": (GW,),
           "ln_g": (E1 * HC1,), "ln_b": (E1 * HC1,), "stats": (GT, 6), "mv": (GT, 2), "ve": (GT,), "rstd": (GT,),
           "neghalf": (GT,), "zs": (GT,), "mr": (GT,), "mvo": (GT, 2), "veo": (GT,), "os": (GT,), "om": (GT,),
           "neg": (GT,), "sums": (GT,), "coef": (GT,), "g4": (GT, E1), "e4": (GT, E1), "rank": (GT, E1), "w4": (GT, E1),
           "z4": (GT,), "s4": (GT,), "below": (GT, E1, E1), "above": (GT, E1, E1), "ge": (GT, E1, E1), "gt": (GT, E1, E1)}
C_SECOND = {"z32": (GT, H1), "oacc": (GT, D), "out32": (GT, D), "bv": (D,), "on_g": (D,), "on_b": (D,), "f32_2": (GW,)}


def c_region(region):
    half = KC * TOK
    raw = carve(region[:, half:], {n: C_WEIGHTS[n] for n in ("w2", "aq", "ak", "av")})
    raw |= carve(region[:, half:], {"w1": C_WEIGHTS["w1"]})
    return raw, carve(region[:, 0:half], C_FIRST) | carve(region[:, half:], C_SECOND)


FIRST_JOBS = "K0 K1 V0 V1 N0 N1 Q0 Q1 S T0 T1 U0 U1 M0 M1".split()
LOOP_JOBS = ("K0 K1 t00 t01 R0 R1 L t02 t03  t10 t11 N0 N1 V0 t12 t13 V1 Q0 Q1  "
             "t20 t21 S T0 T1 t22 t23 U0 U1  t30 t31 t32 t33 M0 M1").split()
LAST_JOBS = [n for n in LOOP_JOBS if n[0] in "tRL"]


class Turns:

    COUNTED = {"job": "KVNQSTUMRLt", "out": "KVNQTMRL", "t": "t", "hi": "KVNQTMR", "lo": "KVQR", "S": "S", "U": "U"}

    def __init__(self, jobs, before):
        self.jobs, self.before = jobs, before

    def count(self, what, name):
        upto = self.jobs[:self.jobs.index(name) + 1]
        return self.before[what] + sum(n[0] in self.COUNTED[what] for n in upto)

    def parity(self, name):
        return (self.jobs.index(name) + (len(FIRST_JOBS) if self.jobs is not FIRST_JOBS else 0)) % 2

    def previous(self, name):
        k = self.jobs.index(name) - 2
        if k >= 0:
            kind = self.jobs[k][0]
            what = kind if kind in "tSU" else "out"
            return what, self.count(what, self.jobs[k]) * (2 if what == "U" else 1)
        return None if self.jobs is FIRST_JOBS else ("out", self.before["out"] + k + 1)


def turns(i):
    def number(what, jobs):
        return sum(n[0] in Turns.COUNTED[what] for n in jobs)

    if i is None:
        return Turns(FIRST_JOBS, {w: 0 for w in Turns.COUNTED})
    before = {w: number(w, LOOP_JOBS) * i + number(w, FIRST_JOBS) for w in Turns.COUNTED}
    return Turns(LAST_JOBS if isinstance(i, int) else LOOP_JOBS, before)


def stage_cd(nc, dram, keep, region):
    x, _, ctxT, ident, tg = keep
    LNS0, LNS = 3, 8
    with ExitStack() as stack:
        sp_ = Space(nc, stack, "c")
        raw, work = c_region(region)
        wt = {n: sp_.pair(n, [P, *s]) for n, s in C_WEIGHTS.items()}
        router = sp_.pair("router", [P, KC, E1])
        router_raw = sp_.sb("router_raw", [P, KC, E1])
        xn32, p32, z32, oacc, out32 = (work[n] for n in ("xn32", "p32", "z32", "oacc", "out32"))
        f32, a32 = ([work[f"{n}_{b}"] for b in range(k)] for n, k in (("f32", 3), ("a32", 2)))
        nT = sp_.pair("nT", [P, KC, GW])
        rT = nT
        hT = sp_.pair("hT", [P, KC, GW])
        qT = sp_.pair("qT", [P, KC, GW])
        kT = sp_.pair("kT", [P, KC, GW])
        v = sp_.pair("v", [P, GT, D])
        stage = sp_.sb("stage", [P, GT, 2, KC, P], F32R)
        pT = sp_.pair("pT", [P, GT, P])
        a = [sp_.pair(f"a{b}", [P, GW]) for b in range(2)]
        vec = {n: sp_.sb(n, [P, KC]) for n in ("bq", "bk", "rn_g", "rn_b")}
        vec |= {n: work[n] for n in ("ln_g", "ln_b")}
        wide = {n: work[n] for n in ("bv", "on_g", "on_b")}
        pad = sp_.sb("pad", [P, 4])
        stats, mv, ve, neghalf, rstd, zs, mr, neg, sums, coef = (work[n] for n in ("stats", "mv", "ve", "neghalf", "rstd", "zs", "mr", "neg", "sums", "coef"))
        mvo, veo, os_, om = (work[n] for n in ("mvo", "veo", "os", "om"))
        g4, e4, rank, w4, z4, s4 = (work[n] for n in ("g4", "e4", "rank", "w4", "z4", "s4"))
        below, above, ge, gt = (work[n] for n in ("below", "above", "ge", "gt"))

        ring = [sp_.ps(f"ring{b}", [P, GW]) for b in range(2)]
        hid = [sp_.ps(f"hid{t}", [P, H1]) for t in range(GT)]
        psY = sp_.ps("y", [P, GT, D])

        small = ("router", "bq", "bk", "rn_g", "rn_b")
        w1_in, small_in, wide_in, w1_hi, w1_lo, w2_hi, w2_lo = sp_.sems(
            "w1_in", "small_in", "wide_in", "w1_hi", "w1_lo", "w2_hi", "w2_lo")
        EARLY = ("ak", "av", "aq")
        w_hi, w_lo, masks, staged, job_done, act_hi, ring_done, lo_done = sp_.sems(
            "w_hi", "w_lo", "masks", "staged", "job_done", "act_hi", "ring_done", "lo_done")
        held, st_done, mv_done, ve_done, rstd_done, xn_ready = sp_.sems("held", "st_done", "mv_done", "ve_done", "rstd_done", "xn_ready")
        neg_done, exp_done, coef_done, x_c = sp_.sems("neg_done", "exp_done", "coef_done", "x_c")
        e4_done, w4_done = sp_.sems("e4_done", "w4_done")
        hid_done, mr_done, z_done, ahi_done, alo_done, second_done, y_sum = sp_.sems(
            "hid_done", "mr_done", "z_done", "ahi_done", "alo_done", "second_done", "y_sum")
        o_step, out_done, om_done, normed = sp_.sems("o_step", "out_done", "om_done", "normed")
        out_of = {"out": ring_done, "t": ahi_done, "S": exp_done, "U": x_c}
        MASKS = 3 + 2 * (E1 - 1)

        def full32(name):
            return f32[2 if name[0] == "V" else int(name[1])]

        def of_bank(r, name):
            return ring[r.parity(name)]

        block = stack.enter_context(nc.Block())

        @block.sync
        def _(sp):
            for n in small:
                dst = router_raw[:, :, :] if n == "router" else vec[n][:, :]
                sp.dma_start(dst, dram[n]).then_inc(small_in, 16)
            for n in ("ln_g", "ln_b"):
                sp.dma_start(vec[n], dram[n]).then_inc(small_in, 16)
            sp.wait_ge(w_lo, len(EARLY))
            for n in wide:
                sp.dma_start(wide[n], dram[n].partition_broadcast(P)).then_inc(wide_in, 16)
            sp.wait_ge(w2_lo, 1)
            sp.dma_start(raw["w1"], dram["w1"]).then_inc(w1_in, 16)
            with sp.Fori(0, GROUPS) as i:
                sp.wait_ge(o_step, 3 * i + 5)
                sp.dma_start(dram["out"].rearrange("(g t) p d -> g p t d", t=GT)[i, :, :, :], out32).then_inc(out_done, 16)
            sp.wait_ge(out_done, 16 * GROUPS + 1)

        @block.gpsimd
        def _(pool):
            pool.memset(pad[:, 0:1], 0.0).then_inc(out_done, 1)
            pool.memset(below[:, :, :, :], 0.0).then_inc(masks, 1)
            pool.memset(above[:, :, :, :], 0.0).then_inc(masks, 1)
            pool.memset(neghalf, -0.5).then_inc(masks, 1)
            pool.wait_ge(masks, 3)
            for e in range(E1):
                if e:
                    pool.memset(below[:, :, e, 0:e], 1.0).then_inc(masks, 1)
                if e < E1 - 1:
                    pool.memset(above[:, :, e, e + 1:E1], 1.0).then_inc(masks, 1)

            def stage_tiles(g, tiles=range(GT)):
                for t in tiles:
                    for part in range(2):
                        pool.tensor_copy(stage[:, t, part, :, :], ctxT[part][:, :, bass.ds(g * GW + t * P, P)].bitcast(F32)
                                         ).then_inc(staged, 1)

            def rsqrt(n, dst=rstd, ve=ve):
                pool.wait_ge(ve_done, n + 1)
                pool.tensor_tensor(dst, ve, neghalf, ALU.pow).then_inc(rstd_done, 1)

            def output(i):
                pool.wait_ge(normed, i + 1)
                pool.tensor_tensor(out32, out32, wide["on_g"].unsqueeze(1).broadcast_to([P, GT, D]), ALU.mult).then_inc(o_step, 1)
                pool.wait_ge(o_step, 3 * i + 3)
                pool.tensor_tensor(out32, out32, wide["on_b"].unsqueeze(1).broadcast_to([P, GT, D]), ALU.add).then_inc(o_step, 1)
                pool.wait_ge(o_step, 3 * i + 4)
                pool.tensor_tensor(out32, out32, x[:, bass.ds(i * GT, GT), :], ALU.add).then_inc(o_step, 1)

            rsqrt(0)
            pool.wait_ge(w2_hi, 1)
            pool.tensor_tensor(wt["w2"][1][:, :, :], raw["w2"], wt["w2"][0][:, :, :].bitcast(F32), ALU.subtract).then_inc(w2_lo, 1)
            pool.wait_ge(job_done, turns(None).count("job", "V1"))
            stage_tiles(1)
            rsqrt(1)
            rsqrt(2, zs)
            pool.wait_ge(o_step, 2)
            rsqrt(LNS0)
            with pool.Fori(0, GROUPS - 1) as i:
                n = LNS * i + LNS0
                rsqrt(n + 1, zs)
                rsqrt(n + 2)
                rsqrt(n + 3, zs)
                pool.wait_ge(job_done, turns(i).count("job", "V1"))
                stage_tiles((i + 2) % GROUPS, (0, 1))
                rsqrt(n + 4, zs)
                stage_tiles((i + 2) % GROUPS, (2,))
                rsqrt(n + 5)
                stage_tiles((i + 2) % GROUPS, (3,))
                rsqrt(n + 6, os_, veo)
                rsqrt(n + 7, zs)
                rsqrt(n + 8)
                output(i)
            n = LNS * (GROUPS - 1) + LNS0
            last_x = x[:, (GROUPS - 1) * GT:, :]
            pool.wait_ge(xn_ready, 3 * GT * (GROUPS - 1) + 2 * GT)
            pool.tensor_tensor(last_x, last_x, wide["on_b"].unsqueeze(1).broadcast_to([P, GT, D]), ALU.add).then_inc(o_step, 1)
            for e in range(1, E1):
                rsqrt(n + e, zs)
            rsqrt(n + E1, os_, veo)

        @block.scalar
        def _(act):
            for n in EARLY:
                act.activation(wt[n][0][:, :, :], raw[n], ACT.Copy).then_inc(w_hi, 1)
            for t in range(GT):
                for part in range(2):
                    act.activation(stage[:, t, part, :, :], ctxT[part][:, :, t * P:t * P + P].bitcast(F32),
                                   ACT.Copy).then_inc(staged, 1)
            act.activation(wt["w2"][0][:, :, :], raw["w2"], ACT.Copy).then_inc(w2_hi, 1)
            act.wait_ge(small_in, 16 * (len(small) + 2))
            act.activation(router[0][:, :, :], router_raw[:, :, :], ACT.Copy).then_inc(w_hi, 1)

            def hi(r, name, dst):
                if name[0] in "KVQR":
                    act.wait_ge(ring_done, r.count("out", name))
                    src = full32(name)
                else:
                    act.wait_ge(job_done, r.count("job", name))
                    src = of_bank(r, name)[:, 0:(2 * P if name[0] == "T" else GW)]
                if name[0] in "VT":
                    src = src.rearrange("p (t n) -> p t n", t=2)
                act.activation(dst, src, ACT.Copy).then_inc(act_hi, 1)

            def pairs(r, *names):
                for name in names:
                    c = int(name[1])
                    two = slice(2 * c, 2 * c + 2)
                    hi(r, name, {"K": kT[0][:, c, :], "N": nT[0][:, c, :], "Q": qT[0][:, c, :], "M": hT[0][:, c, :],
                                 "R": rT[0][:, c, :], "V": v[0][:, two, :], "T": pT[0][:, two, :]}[name[0]])

            def exps(r, n):
                act.wait_ge(neg_done, n + 1)
                for b in range(GT):
                    ins = act.activation(p32[:, b, :], of_bank(r, "S")[:, b * P:b * P + P], ACT.Exp, bias=neg[:, b:b + 1],
                                         accum_out=sums[:, b:b + 1])
                ins.then_inc(exp_done, 1)

            def normalise(n, turned):
                act.wait_ge(mr_done, n + 1)
                if turned is not None:
                    act.wait_ge(job_done, turned)
                for t in range(GT):
                    act.activation(z32[:, t, :], hid[t][:, :], ACT.Identity, scale=zs[:, t:t + 1],
                                   bias=mr[:, t:t + 1]).then_inc(z_done, 1)

            def normalise_output(i):
                act.wait_ge(om_done, i + 1)
                act.wait_ge(out_done, 16 * i + 1)
                for t in range(GT):
                    ins = act.activation(out32[:, t, :], oacc[:, t, :], ACT.Identity, scale=os_[:, t:t + 1], bias=om[:, t:t + 1])
                ins.then_inc(normed, 1)

            def relu(r, i, e, c):
                k = e * HC1 + c
                act.wait_ge(job_done, r.count("job", f"t{e}{c}"))
                if c >= 2:
                    act.wait_ge(second_done, HC1 * (E1 * i + e) + c - 1)
                src = of_bank(r, f"t{e}{c}")[:, :]
                act.activation(a32[c % 2], src, ACT.Relu, scale=vec["ln_g"][:, k:k + 1], bias=vec["ln_b"][:, k:k + 1])
                act.activation(a[c % 2][0][:, :], src, ACT.Relu, scale=vec["ln_g"][:, k:k + 1],
                               bias=vec["ln_b"][:, k:k + 1]).then_inc(ahi_done, 1)

            def round_(i, last):
                r = turns(i)
                if not last:
                    pairs(r, "K0", "K1")
                relu(r, i, 0, 0)
                relu(r, i, 0, 1)
                pairs(r, "R0", "R1")
                act.wait_ge(ring_done, r.count("out", "L"))
                act.activation(e4[:, :, :], g4[:, :, :], ACT.Exp).then_inc(e4_done, 1)
                relu(r, i, 0, 2)
                relu(r, i, 0, 3)
                normalise(E1 * i + 1, r.count("job", "t03"))
                relu(r, i, 1, 0)
                relu(r, i, 1, 1)
                if not last:
                    pairs(r, "N0", "N1", "V0")
                relu(r, i, 1, 2)
                relu(r, i, 1, 3)
                normalise(E1 * i + 2, r.count("job", "t13"))
                if not last:
                    pairs(r, "V1", "Q0", "Q1")
                relu(r, i, 2, 0)
                relu(r, i, 2, 1)
                if not last:
                    exps(r, i + 1)
                    pairs(r, "T0", "T1")
                relu(r, i, 2, 2)
                relu(r, i, 2, 3)
                normalise(E1 * i + 3, r.count("job", "t23"))
                for c in range(HC1):
                    relu(r, i, 3, c)
                if not last:
                    pairs(r, "M0", "M1")
                    normalise(E1 * i + 4, r.count("job", "t33"))
                normalise_output(i)

            r = turns(None)
            pairs(r, "K0", "K1", "V0", "V1", "N0", "N1", "Q0", "Q1")
            exps(r, 0)
            pairs(r, "T0", "T1")
            act.wait_ge(w1_in, 16)
            act.activation(wt["w1"][0][:, :, :], raw["w1"], ACT.Copy).then_inc(w1_hi, 1)
            pairs(r, "M0", "M1")
            act.wait_ge(w1_lo, 2)
            normalise(0, None)
            with act.Fori(0, GROUPS - 1) as i:
                round_(i, False)
            round_(GROUPS - 1, True)

        @block.vector
        def _(dve):
            dve.memset(pad[:, 1:2], 0.0).then_inc(held, 1)

            def weight_lo(k):
                n = (*EARLY, "router")[k]
                hi, lo = (a[:, :, :] for a in (router if n == "router" else wt[n]))
                src = router_raw[:, :, :] if n == "router" else raw[n]
                dve.wait_ge(w_hi, k + 1)
                dve.tensor_tensor(lo, src, hi.bitcast(F32), ALU.subtract).then_inc(w_lo, 1)

            held_now = [0]

            def carry(base, sem, value):
                held_now[0] += 1
                dve.wait_ge(held, base + held_now[0])
                dve.wait_ge(sem, value)
                dve.memset(pad[:, 1:2], 0.0).then_inc(held, 1)

            def moments(n, base, src, mv=mv):
                for t in range(GT):
                    src_t, sem, value = src(t)
                    if sem is not None:
                        dve.wait_ge(sem, value)
                    dve.bn_stats(stats[:, t, :], src_t).then_inc(st_done, 1)
                carry(base, st_done, GT * n + GT)
                for t in range(GT):
                    dve.bn_aggr(mv[:, t, :], stats[:, t, :]).then_inc(mv_done, 1)
                dve.wait_ge(mv_done, GT * n + GT)

            def spread(n, mv=mv, ve=ve):
                dve.tensor_scalar(ve, mv[:, :, 1], EPS_LN, None, ALU.add).then_inc(ve_done, 1)

            def ln_apply(dst, src, sem):
                for t in range(GT):
                    dve.tensor_scalar(dst[:, t, :], src(t), mv[:, t, 0:1], rstd[:, t:t + 1],
                                      ALU.subtract, ALU.mult).then_inc(sem, 1)

            def x_moments(n, base, g):
                moments(n, base, lambda t: (x[:, g * GT + t, :], None, None))
                spread(n)

            def x_apply(n, g):
                dve.wait_ge(rstd_done, n + 1)
                ln_apply(xn32, lambda t: x[:, g * GT + t, :], xn_ready)

            def norm_h(n, base, ready):
                carry(base, xn_ready, ready)
                moments(n, base, lambda t: (xn32[:, t, :], None, None))
                spread(n)
                dve.wait_ge(rstd_done, n + 1)
                ln_apply(xn32, lambda t: xn32[:, t, :], xn_ready)

            def hidden_moments(n, base, expert):
                moments(n, base, lambda t: (hid[t][:, :], hid_done, GT * expert + t + 1))
                spread(n)

            def hidden_shift(n):
                dve.wait_ge(rstd_done, n + 1)
                dve.scalar_tensor_tensor(mr[:, :], mv[:, :, 0], -1.0, zs[:, :], ALU.mult, ALU.mult).then_inc(mr_done, 1)

            def full(r, *names):
                for k, name in enumerate(names):
                    c = int(name[1])
                    src, dst = of_bank(r, name)[:, :], full32(name)
                    if r.jobs is not FIRST_JOBS or name[0] != "K":
                        dve.wait_ge(lo_done, r.count("lo", name) - 1 - k)
                    dve.wait_ge(job_done, r.count("job", name))
                    if name[0] == "V":
                        ins = dve.tensor_tensor(dst.rearrange("p (t n) -> p t n", t=2), src.rearrange("p (t n) -> p t n", t=2),
                                                wide["bv"].unsqueeze(1).broadcast_to([P, 2, D]), ALU.add)
                    elif name[0] == "K":
                        ins = dve.tensor_scalar(dst, src, vec["bk"][:, c:c + 1], None, ALU.add)
                    elif name[0] == "Q":
                        ins = dve.tensor_scalar(dst, src, vec["bq"][:, c:c + 1], D ** -0.5, ALU.add, ALU.mult)
                    else:
                        ins = dve.tensor_scalar(dst, src, vec["rn_g"][:, c:c + 1], vec["rn_b"][:, c:c + 1],
                                                ALU.mult, ALU.add)
                    ins.then_inc(ring_done, 1)

            def lower(r, *names):
                for name in names:
                    c = int(name[1])
                    two = slice(2 * c, 2 * c + 2)
                    dst = {"K": kT, "N": nT, "Q": qT, "M": hT, "R": rT, "V": v, "T": pT}[name[0]]
                    up, low = (d[:, two, :] if name[0] in "VT" else d[:, c, :] for d in dst)
                    dve.wait_ge(act_hi, r.count("hi", name))
                    if name[0] in "KVQR":
                        src, sem = full32(name), lo_done
                    else:
                        src, sem = of_bank(r, name)[:, 0:(2 * P if name[0] == "T" else GW)], ring_done
                    if name[0] in "VT":
                        src = src.rearrange("p (t n) -> p t n", t=2)
                    dve.tensor_tensor(low, src, up.bitcast(F32), ALU.subtract).then_inc(sem, 1)

            def minus_max(r):
                dve.wait_ge(job_done, r.count("job", "S"))
                dve.tensor_reduce(neg[:, :], of_bank(r, "S")[:, :].rearrange("p (t n) -> p t n", t=GT), AX_X, ALU.max,
                                  negate=True).then_inc(neg_done, 1)

            def coefficients(n):
                dve.wait_ge(exp_done, n + 1)
                dve.reciprocal(coef[:, :], sums[:, :]).then_inc(coef_done, 1)
                dve.wait_ge(coef_done, 2 * n + 1)
                dve.tensor_scalar(coef[:, :], coef[:, :], tg[:, 1:2], None, ALU.mult).then_inc(coef_done, 1)
                dve.wait_ge(coef_done, 2 * n + 2)

            def add_attention(r, g, part):
                dve.wait_ge(job_done, r.count("job", f"U{part}"))
                for b in range(2):
                    at = g * GT + 2 * part + b
                    dve.scalar_tensor_tensor(x[:, at, :], of_bank(r, f"U{part}")[:, b * D:b * D + D],
                                             coef[:, 2 * part + b:2 * part + b + 1], x[:, at, :], ALU.mult, ALU.add).then_inc(x_c, 1)

            def gates(r, i, first):
                steps = [0 if first else 1]
                CHAIN = 15

                def chain(ins):
                    steps[0] += 1
                    ins.then_inc(w4_done, 1)
                    dve.wait_ge(w4_done, CHAIN * i + steps[0])

                def over(ap):
                    return ap[:, :].unsqueeze(2).broadcast_to([P, GT, E1])

                logits = of_bank(r, "L")[:, 0:GT * E1].rearrange("p (t e) -> p t e", e=E1)
                if first:
                    dve.wait_ge(job_done, r.count("job", "L"))
                    chain(dve.tensor_reduce(s4[:, :], logits, AX_X, ALU.max, negate=True))
                    dve.tensor_tensor(g4[:, :, :], logits, over(s4), ALU.add).then_inc(ring_done, 1)
                    return
                dve.wait_ge(e4_done, i + 1)
                chain(dve.tensor_reduce(z4[:, :], e4[:, :, :], AX_X, ALU.add))
                chain(dve.reciprocal(s4[:, :], z4[:, :]))
                chain(dve.tensor_tensor(e4[:, :, :], e4[:, :, :], over(s4), ALU.mult))
                mine = e4[:, :, :].unsqueeze(3).broadcast_to([P, GT, E1, E1])
                other = e4[:, :, :].unsqueeze(2).broadcast_to([P, GT, E1, E1])
                chain(dve.tensor_tensor(ge[:, :, :, :], other, mine, ALU.is_ge))
                chain(dve.tensor_tensor(ge[:, :, :, :], ge[:, :, :, :], below[:, :, :, :], ALU.mult))
                chain(dve.tensor_tensor(gt[:, :, :, :], other, mine, ALU.is_gt))
                chain(dve.tensor_tensor(gt[:, :, :, :], gt[:, :, :, :], above[:, :, :, :], ALU.mult))
                chain(dve.tensor_tensor(ge[:, :, :, :], ge[:, :, :, :], gt[:, :, :, :], ALU.add))
                chain(dve.tensor_reduce(rank[:, :, :], ge[:, :, :, :], AX_X, ALU.add))
                chain(dve.scalar_tensor_tensor(w4[:, :, :], rank[:, :, :], 1.5, e4[:, :, :], ALU.is_lt, ALU.mult))
                chain(dve.tensor_reduce(z4[:, :], w4[:, :, :], AX_X, ALU.add))
                chain(dve.tensor_scalar(z4[:, :], z4[:, :], EPS_GATE, None, ALU.add))
                chain(dve.reciprocal(s4[:, :], z4[:, :]))
                chain(dve.tensor_tensor(w4[:, :, :], w4[:, :, :], over(s4), ALU.mult))
                assert steps[0] == CHAIN

            def a_lo(i, e, c):
                dve.wait_ge(ahi_done, HC1 * (E1 * i + e) + c + 1)
                dve.tensor_tensor(a[c % 2][1][:, :], a32[c % 2], a[c % 2][0][:, :].bitcast(F32), ALU.subtract).then_inc(alo_done, 1)

            def add_expert(i, e):
                n = E1 * i + e
                dve.wait_ge(second_done, HC1 * (n + 1))
                if e:
                    dve.wait_ge(y_sum, GT * n)
                for t in range(GT):
                    if e == 0:
                        dve.tensor_scalar(oacc[:, t, :], psY[:, t, :], w4[:, t, e:e + 1], None, ALU.mult).then_inc(y_sum, 1)
                    else:
                        dve.scalar_tensor_tensor(oacc[:, t, :], psY[:, t, :], w4[:, t, e:e + 1], oacc[:, t, :],
                                                 ALU.mult, ALU.add).then_inc(y_sum, 1)

            def output_moments(n, base, i):
                carry(base, y_sum, GT * E1 * (i + 1))
                moments(n, base, lambda t: (oacc[:, t, :], None, None), mvo)
                spread(n, mvo, veo)

            def output_shift(n, i):
                dve.wait_ge(rstd_done, n + 1)
                dve.scalar_tensor_tensor(om, mvo[:, :, 0], -1.0, os_, ALU.mult, ALU.mult).then_inc(om_done, 1)

            HELD0, HELD = 4, 11

            def round_(i, last):
                r = turns(i)
                n, base = LNS * i + LNS0, HELD * i + HELD0
                held_now[0] = 0
                if not last:
                    full(r, "K0", "K1")
                norm_h(n, base, 3 * GT * i + 2 * GT)
                if not last:
                    lower(r, "K0", "K1")
                a_lo(i, 0, 0)
                a_lo(i, 0, 1)
                full(r, "R0", "R1")
                lower(r, "R0", "R1")
                hidden_moments(n + 1, base, E1 * i + 1)
                gates(r, i, True)
                hidden_shift(n + 1)
                a_lo(i, 0, 2)
                a_lo(i, 0, 3)
                if not last:
                    x_moments(n + 2, base, i + 1)
                gates(r, i, False)
                if not last:
                    x_apply(n + 2, i + 1)
                add_expert(i, 0)
                a_lo(i, 1, 0)
                a_lo(i, 1, 1)
                if not last:
                    lower(r, "N0", "N1")
                hidden_moments(n + (2 if last else 3), base, E1 * i + 2)
                if not last:
                    full(r, "V0")
                hidden_shift(n + (2 if last else 3))
                if not last:
                    lower(r, "V0")
                a_lo(i, 1, 2)
                a_lo(i, 1, 3)
                if not last:
                    full(r, "V1", "Q0", "Q1")
                add_expert(i, 1)
                if not last:
                    lower(r, "V1", "Q0", "Q1")
                a_lo(i, 2, 0)
                a_lo(i, 2, 1)
                if not last:
                    minus_max(r)
                hidden_moments(n + (3 if last else 4), base, E1 * i + 3)
                if not last:
                    lower(r, "T0", "T1")
                hidden_shift(n + (3 if last else 4))
                if not last:
                    coefficients(i + 1)
                a_lo(i, 2, 2)
                a_lo(i, 2, 3)
                if not last:
                    add_attention(r, i + 1, 0)
                    add_attention(r, i + 1, 1)
                add_expert(i, 2)
                a_lo(i, 3, 0)
                if not last:
                    carry(base, x_c, GT * (i + 2))
                    x_moments(n + 5, base, i + 1)
                a_lo(i, 3, 1)
                if not last:
                    x_apply(n + 5, i + 1)
                a_lo(i, 3, 2)
                a_lo(i, 3, 3)
                if not last:
                    lower(r, "M0", "M1")
                add_expert(i, 3)
                output_moments(n + (4 if last else 6), base, i)
                if not last:
                    hidden_moments(n + 7, base, E1 * i + 4)
                    hidden_shift(n + 7)
                output_shift(n + (4 if last else 6), i)
                if last:
                    dve.wait_ge(normed, GROUPS)
                    dve.wait_ge(o_step, 3 * i + 3)
                    dve.tensor_tensor(out32, out32, wide["on_g"].unsqueeze(1).broadcast_to([P, GT, D]), ALU.mult).then_inc(o_step, 1)
                    dve.wait_ge(o_step, 3 * i + 4)
                    dve.tensor_tensor(out32, out32, x[:, i * GT:, :], ALU.add).then_inc(o_step, 1)
                assert last or held_now[0] == HELD

            r = turns(None)
            weight_lo(0)
            x_moments(0, 0, 0)
            weight_lo(1)
            weight_lo(2)
            dve.wait_ge(small_in, 16 * (len(small) + 2))
            full(r, "K0", "K1")
            x_apply(0, 0)
            lower(r, "K0", "K1")
            dve.wait_ge(wide_in, 16 * len(wide))
            for name in ("V0", "V1"):
                full(r, name)
                lower(r, name)
            lower(r, "N0", "N1")
            full(r, "Q0", "Q1")
            lower(r, "Q0", "Q1")
            weight_lo(3)
            for n in ("on_g", "on_b"):
                dve.tensor_scalar(wide[n], wide[n], tg[:, 3:4], None, ALU.mult).then_inc(o_step, 1)
            minus_max(r)
            lower(r, "T0", "T1")
            coefficients(0)
            add_attention(r, 0, 0)
            add_attention(r, 0, 1)
            carry(0, x_c, GT)
            x_moments(1, 0, 0)
            x_apply(1, 0)
            dve.wait_ge(w1_hi, 1)
            for part in (slice(0, 1), slice(1, E1)):
                dve.tensor_tensor(wt["w1"][1][:, part, :], raw["w1"][:, part, :], wt["w1"][0][:, part, :].bitcast(F32),
                                  ALU.subtract).then_inc(w1_lo, 1)
                if part.start == 0:
                    lower(r, "M0", "M1")
            dve.wait_ge(masks, MASKS)
            hidden_moments(2, 0, 0)
            hidden_shift(2)
            assert held_now[0] == HELD0
            with dve.Fori(0, GROUPS - 1) as i:
                round_(i, False)
            round_(GROUPS - 1, True)

        @block.tensor
        def _(pe):

            def turn(r, name):
                before = r.previous(name)
                if before is not None:
                    pe.wait_ge(out_of[before[0]], before[1])
                return of_bank(r, name)

            def transposed(r, name, src, c, tiles_before=None):
                bank = turn(r, name)
                for t in range(GT):
                    if tiles_before is not None:
                        pe.wait_ge(z_done, tiles_before + t + 1)
                    mm = pe.transpose(bank[:, t * P:t * P + P], src[:, t, c * P:c * P + P], ident[:, :])
                mm.then_inc(job_done, 1)

            def job(r, name, g=None, ready=None):
                kind = name[0]
                if kind in "NMR":
                    pe.wait_ge(xn_ready, ready)
                    transposed(r, name, xn32, int(name[1]))
                    return
                bank = turn(r, name)
                c = int(name[1]) if len(name) > 1 else None
                if kind == "K":
                    mm = product(pe, bank[:, :], lambda p, k: wt["ak"][p][:, k, c * P:c * P + P],
                                 lambda p, k: ctxT[p][:, k, bass.ds(g * GW, GW)], KC)
                elif kind == "Q":
                    pe.wait_ge(ring_done, r.count("out", "N1"))
                    mm = product(pe, bank[:, :], lambda p, k: wt["aq"][p][:, k, c * P:c * P + P],
                                 lambda p, k: nT[p][:, k, :], KC)
                elif kind == "V":
                    for b in range(2):
                        mm = product(pe, bank[:, b * D:b * D + D], lambda p, k: stage[:, 2 * c + b, p, k, :],
                                     lambda p, k: wt["av"][p][:, k, :], KC)
                elif kind == "S":
                    pe.wait_ge(lo_done, r.count("lo", "Q1"))
                    for b in range(GT):
                        at = slice(b * P, b * P + P)
                        mm = product(pe, bank[:, at], lambda p, k: qT[p][:, k, at], lambda p, k: kT[p][:, k, at], KC)
                elif kind == "T":
                    pe.wait_ge(exp_done, r.count("S", "S"))
                    for b in range(2):
                        mm = pe.transpose(bank[:, b * P:b * P + P], p32[:, 2 * c + b, :], ident[:, :])
                elif kind == "U":
                    pe.wait_ge(ring_done, r.count("out", f"T{c}"))
                    if c == 1:
                        pe.wait_ge(lo_done, r.count("lo", "V1"))
                    for b in range(2):
                        mm = product(pe, bank[:, b * D:b * D + D], lambda p, k: pT[p][:, 2 * c + b, :],
                                     lambda p, k: v[p][:, 2 * c + b, :], 1)
                elif kind == "L":
                    pe.wait_ge(lo_done, r.count("lo", "R1"))
                    for t in range(GT):
                        mm = product(pe, bank[:, t * E1:t * E1 + E1], lambda p, k: rT[p][:, k, t * P:t * P + P],
                                     lambda p, k: router[p][:, k, :], KC)
                mm.then_inc(job_done, 1)

            def hidden(e, tiles):
                for t in tiles:
                    product(pe, hid[t][:, :], lambda p, k: hT[p][:, k, t * P:t * P + P],
                            lambda p, k: wt["w1"][p][:, e, k * H1:k * H1 + H1], KC).then_inc(hid_done, 1)

            def second(i, e, c):
                pe.wait_ge(alo_done, HC1 * (E1 * i + e) + c + 1)
                if c == 0 and e:
                    pe.wait_ge(y_sum, GT * (E1 * i + e))
                for t in range(GT):
                    for n, (p, q) in enumerate(PASSES):
                        mm = pe.matmul(psY[:, t, :], a[c % 2][p][:, t * P:t * P + P], wt["w2"][q][:, e, c * D:c * D + D],
                                       start=c == 0 and n == 0 and t % 2 == 0, stop=c == HC1 - 1 and n == 2,
                                       skip_group_check=True)
                mm.then_inc(second_done, 1)

            def round_(i, last):
                r = turns(i)

                def jobs(*names, **more):
                    if not last:
                        for name in names:
                            job(r, name, **more)

                def turned(e, c):
                    transposed(r, f"t{e}{c}", z32, c, GT * (E1 * i + e) if c == 0 else None)

                jobs("K0", "K1", g=i + 1)
                turned(0, 0)
                turned(0, 1)
                hidden(1, (0, 1))
                for name in ("R0", "R1"):
                    job(r, name, ready=3 * GT * i + 3 * GT)
                hidden(1, (2, 3))
                job(r, "L")
                turned(0, 2)
                second(i, 0, 0)
                turned(0, 3)
                second(i, 0, 1)
                second(i, 0, 2)
                second(i, 0, 3)
                turned(1, 0)
                turned(1, 1)
                hidden(2, (0, 1, 2))
                jobs("N0", "N1", ready=3 * GT * i + 4 * GT)
                hidden(2, (3,))
                if not last:
                    pe.wait_ge(staged, 2 * GT * (i + 2))
                jobs("V0")
                turned(1, 2)
                second(i, 1, 0)
                turned(1, 3)
                second(i, 1, 1)
                jobs("V1")
                second(i, 1, 2)
                jobs("Q0")
                second(i, 1, 3)
                jobs("Q1")
                turned(2, 0)
                turned(2, 1)
                hidden(3, (0, 1))
                jobs("S")
                hidden(3, (2, 3))
                jobs("T0", "T1")
                second(i, 2, 0)
                turned(2, 2)
                turned(2, 3)
                second(i, 2, 1)
                jobs("U0")
                second(i, 2, 2)
                jobs("U1")
                second(i, 2, 3)
                turned(3, 0)
                turned(3, 1)
                turned(3, 2)
                second(i, 3, 0)
                turned(3, 3)
                second(i, 3, 1)
                second(i, 3, 2)
                jobs("M0", "M1", ready=3 * GT * i + 5 * GT)
                second(i, 3, 3)
                if not last:
                    pe.wait_ge(ring_done, r.count("out", "M1"))
                    hidden(0, range(GT))

            r = turns(None)
            pe.wait_ge(w_lo, 1)
            for name in ("K0", "K1"):
                job(r, name, g=0)
            pe.wait_ge(w_lo, 2)
            pe.wait_ge(staged, 2 * GT)
            job(r, "V0")
            job(r, "V1")
            for name in ("N0", "N1"):
                job(r, name, ready=GT)
            pe.wait_ge(w_lo, 3)
            for name in ("Q0", "Q1", "S", "T0", "T1", "U0", "U1"):
                job(r, name)
            for name in ("M0", "M1"):
                job(r, name, ready=2 * GT)
            pe.wait_ge(ring_done, r.count("out", "M1"))
            pe.wait_ge(w1_lo, 1)
            hidden(0, range(GT))
            pe.wait_ge(w1_lo, 2)
            pe.wait_ge(w2_lo, 1)
            pe.wait_ge(w_lo, len(EARLY) + 1)
            with pe.Fori(0, GROUPS - 1) as i:
                round_(i, False)
            round_(GROUPS - 1, True)


def program(nc, dram):
    with ExitStack() as stack:
        keep = Space(nc, stack, "all")
        x = keep.sb("x", [P, TILES, D])
        ctxT = keep.pair("ctxT", [P, KC, TOK])
        ident = keep.sb("ident", [P, P])
        tg = keep.sb("tg", [P, 4])
        region = keep.sb("region", [P, sum(a * b for a, b in C_WEIGHTS.values())])
        with ExitStack() as first:
            xnT = Space(nc, first, "ab").pair("xnT", [P, KC, TOK])
            stage_a(nc, dram, (x, xnT, ctxT, ident, tg), region)
            stage_b(nc, dram, (x, xnT, ctxT, ident, tg), region)
        stage_cd(nc, dram, (x, None, ctxT, ident, tg), region)


def kernel(**inputs):
    import numpy as np
    import concourse.bacc as bacc
    from concourse.bass_utils import run_bass_kernel_spmd

    def rows(a):
        a = np.asarray(a)
        return a.reshape(-1, P, *a.shape[1:]).swapaxes(0, 1)

    x, ctx = (np.asarray(inputs[n]).reshape(TOK, D) for n in ("x", "ctx_1024"))
    laid = {
        "x": rows(x),
        "ctxT": rows(ctx.T),
        "g": np.concatenate([inputs["g_xattn"], inputs["g_ffn"]]),
        "wq": rows(inputs["L0_xattn_W_Q"]),
        "wk": rows(inputs["L0_xattn_W_K"]),
        "wv": rows(inputs["L0_xattn_W_V"]),
        "wo": rows(inputs["L0_xattn_W_O"]),
    }
    gu = inputs["L0_ffn_gate_up_w"].reshape(EGS, EG, 2 * XD, KC, P).transpose(0, 4, 1, 3, 2)
    dn = inputs["L0_ffn_down_w"].reshape(EGS, EG, D, XD).transpose(0, 3, 1, 2)
    laid["moe"] = np.concatenate([gu.reshape(EGS, P, -1), dn.reshape(EGS, P, -1)], axis=2)
    laid["gate"] = rows(inputs["L0_ffn_gate_w"].T)
    for short, name in (("aq", "Wq"), ("ak", "Wk"), ("av", "Wv")):
        laid[short] = rows(inputs["L1_xattn_" + name].T)
    laid["router"] = rows(inputs["L1_ffn_router_w"].T)
    laid["w1"] = inputs["L1_ffn_w1"].reshape(E1, KC, P, H1).transpose(2, 0, 1, 3).reshape(P, E1, KC * H1)
    laid["w2"] = inputs["L1_ffn_w2"].reshape(E1, HC1, P, D).transpose(2, 0, 1, 3).reshape(P, E1, HC1 * D)
    for short, name in (("bq", "xattn_bq"), ("bk", "xattn_bk"), ("rn_g", "ffn_rn_g"), ("rn_b", "ffn_rn_b")):
        laid[short] = rows(inputs["L1_" + name])
    for short in ("ln_g", "ln_b"):
        laid[short] = inputs["L1_ffn_" + short].reshape(E1, HC1, P).transpose(2, 0, 1).reshape(P, E1 * HC1)
    for short, name in (("bv", "xattn_bv"), ("on_g", "ffn_on_g"), ("on_b", "ffn_on_b")):
        laid[short] = inputs["L1_" + name]
    laid = {n: np.ascontiguousarray(a) for n, a in laid.items()}
    nc = bacc.Bacc("TRN2", target_bir_lowering=False, num_devices=1, dynamic_dma_scratch_size=1024)
    dram = {n: nc.dram_tensor(f"in_{n}", a.shape, F32, kind="ExternalInput").ap() for n, a in laid.items()}
    dram["shares"] = nc.dram_tensor("shares", (EXPERTS, TOK), F32, kind="Internal").ap()
    dram["out"] = nc.dram_tensor("out", (TILES, P, D), F32, kind="ExternalOutput").ap()
    program(nc, dram)
    r = run_bass_kernel_spmd(nc, [{f"in_{n}": a for n, a in laid.items()}], core_ids=[0])
    return r.results[0]["out"]
```
